# Optimizing a Trainium2 kernel written in Bass

```python
import numpy as np
import jax
import jax.numpy as jnp

def _softmax(x, axis=-1):
    return jax.nn.softmax(x, axis=axis)

def _gelu(x):
    return jax.nn.gelu(x, approximate=True)

def _silu(x):
    return jax.nn.silu(x)

def _sigmoid(x):
    return jax.nn.sigmoid(x)

def _layernorm(x, axis=-1, eps=1e-05):
    m = jnp.mean(x, axis=axis, keepdims=True)
    v = jnp.var(x, axis=axis, keepdims=True)
    return (x - m) / jnp.sqrt(v + eps)

def _scatter_add(tgt, idx, src, axis=0):
    return tgt.at[idx].add(src)

def _segment_sum(src, seg, n):
    return jax.ops.segment_sum(src, seg, n)
kernel_name = 'mk_gps_d1_gnn_r8_843729'

def setup_inputs(seed: int=0):
    np.random.seed(seed)
    _w = jnp.asarray

    def _rec_inputs():
        import jax
        import jax.numpy as jnp
        _gk = jax.random.key(seed)
        x = -0.0003713 + 1 * jax.random.normal(jax.random.fold_in(_gk, 1), (6250, 256), jnp.float32)
        src = jax.random.randint(jax.random.fold_in(_gk, 2), (100000,), 0, 6250, jnp.int32)
        dst = jnp.minimum((6250 * jax.random.uniform(jax.random.fold_in(_gk, 3), (100000,)) ** 2.0).astype(jnp.int32), 49999)
        _o = jnp.argsort(dst, stable=True)
        src = src[_o]
        dst = dst[_o]
        edge_attr_128 = -5.16925e-05 + 1.00005 * jax.random.normal(jax.random.fold_in(_gk, 11), (100000, 128), jnp.float32)
        return (x, src, dst, edge_attr_128)
    x, src, dst, edge_attr_128 = _rec_inputs()

    def _L0_gnn_setup():
        import jax, jax.numpy as jnp
        import numpy as np
        N_NODES = 6250
        N_EDGES = 100000
        IN_DIM = 256
        OUT_DIM = 256
        EDGE_DIM = 128
        BN_EPS = 1e-05
        key = jax.random.key(seed)
        ks = jax.random.split(key, 10)
        s = lambda d: 1.0 / np.sqrt(d)
        return {'x': jax.random.normal(ks[0], (N_NODES, IN_DIM), dtype=jnp.float32), 'edge_index': jax.random.randint(ks[1], (2, N_EDGES), 0, N_NODES, dtype=jnp.int64), 'edge_attr': jax.random.normal(ks[2], (N_EDGES, EDGE_DIM), dtype=jnp.float32), 'W_edge': jax.random.uniform(ks[3], (EDGE_DIM, IN_DIM), jnp.float32, -s(EDGE_DIM), s(EDGE_DIM)), 'b_edge': jnp.zeros((IN_DIM,), jnp.float32), 'W1': jax.random.uniform(ks[4], (IN_DIM, OUT_DIM), jnp.float32, -s(IN_DIM), s(IN_DIM)), 'b1': jnp.zeros((OUT_DIM,), jnp.float32), 'W2': jax.random.uniform(ks[5], (OUT_DIM, OUT_DIM), jnp.float32, -s(OUT_DIM), s(OUT_DIM)), 'b2': jnp.zeros((OUT_DIM,), jnp.float32), 'eps': jnp.float32(0.0), 'gamma': jnp.ones((OUT_DIM,), jnp.float32), 'beta': jnp.zeros((OUT_DIM,), jnp.float32)}
    _L0_gnn_all = _L0_gnn_setup()
    _L0_gnn_in = {k: v for k, v in _L0_gnn_all.items() if k in ('W_edge', 'b_edge', 'W1', 'b1', 'W2', 'b2', 'eps', 'gamma', 'beta')}
    del _L0_gnn_all

    def _L0_mix_setup():
        import jax, jax.numpy as jnp
        import numpy as np
        N, F, C, H = (32, 512, 256, 8)
        D = C // H
        EPS_ATTN = 1e-06
        EPS_LN = 1e-05

        def layer_norm(x, g, b):
            mu = jnp.mean(x, axis=-1, keepdims=True)
            var = jnp.var(x, axis=-1, keepdims=True)
            return (x - mu) * jax.lax.rsqrt(var + EPS_LN) * g + b
        key = jax.random.key(seed)
        ks = jax.random.split(key, 8)
        s = 1.0 / np.sqrt(C)
        return {'x': jax.random.normal(ks[0], (N, F, C), jnp.float32), 'Wqkv': jax.random.uniform(ks[1], (3 * C, C), jnp.float32, -s, s), 'ln1_g': jnp.ones((C,), jnp.float32), 'ln1_b': jnp.zeros((C,), jnp.float32), 'W1': jax.random.uniform(ks[2], (C, C), jnp.float32, -s, s), 'b1': jax.random.uniform(ks[3], (C,), jnp.float32, -s, s), 'W2': jax.random.uniform(ks[4], (C, C), jnp.float32, -s, s), 'b2': jax.random.uniform(ks[5], (C,), jnp.float32, -s, s), 'ln2_g': jnp.ones((C,), jnp.float32), 'ln2_b': jnp.zeros((C,), jnp.float32)}
    _L0_mix_all = _L0_mix_setup()
    _L0_mix_in = {k: v for k, v in _L0_mix_all.items() if k in ('Wqkv', 'ln1_g', 'ln1_b', 'W1', 'b1', 'W2', 'b2', 'ln2_g', 'ln2_b')}
    del _L0_mix_all

    def _L0_ffn_setup():
        import jax, jax.numpy as jnp
        import numpy as np
        B, N, D = (16, 512, 256)
        NUM_EXPERTS, TOP_K, HEADS = (4, 2, 4)
        N_EDGES = 131072
        LN_EPS = 1e-05

        def _layernorm(x, g, b):
            mu = x.mean(-1, keepdims=True)
            var = ((x - mu) ** 2).mean(-1, keepdims=True)
            return (x - mu) * jax.lax.rsqrt(var + LN_EPS) * g + b

        def _forward(x, edge_index, W_gat, att_src, att_dst, b_gat, ln_gamma, ln_beta, W1, b1, W2, b2):
            Bc, Nc, Dc = x.shape
            M = Bc * Nc
            x_flat = x.reshape(M, Dc)
            h = (x_flat @ W_gat).reshape(M, HEADS, NUM_EXPERTS)
            loops = jnp.arange(M, dtype=edge_index.dtype)
            src = jnp.concatenate([edge_index[0], loops])
            dst = jnp.concatenate([edge_index[1], loops])
            a_src = (h * att_src).sum(-1)
            a_dst = (h * att_dst).sum(-1)
            e = jax.nn.leaky_relu(a_src[src] + a_dst[dst], negative_slope=0.2)
            e_max = jax.ops.segment_max(e, dst, num_segments=M)
            ee = jnp.exp(e - e_max[dst])
            denom = jax.ops.segment_sum(ee, dst, num_segments=M)
            alpha = ee / (denom[dst] + 1e-16)
            msg = h[src] * alpha[:, :, None]
            agg = jax.ops.segment_sum(msg, dst, num_segments=M).reshape(M, HEADS * NUM_EXPERTS) + b_gat
            scores = _layernorm(agg, ln_gamma, ln_beta).reshape(M, HEADS, NUM_EXPERTS).mean(1)
            scores = scores.reshape(Bc, Nc, NUM_EXPERTS)
            topk_s, topk_i = jax.lax.top_k(scores, TOP_K)
            w = jax.nn.softmax(topk_s, axis=-1)
            out = jnp.zeros_like(x)
            for ei in range(NUM_EXPERTS):
                g = jnp.where(topk_i == ei, w, 0.0).sum(-1)
                hh = jax.nn.gelu(x @ W1[ei] + b1[ei], approximate=False)
                out = out + g[..., None] * (hh @ W2[ei] + b2[ei])
            return out
        key = jax.random.key(seed)
        ks = jax.random.split(key, 8)
        s = 0.05
        return {'x': jax.random.normal(ks[0], (B, N, D), jnp.float32), 'W_gat': jax.random.normal(ks[1], (D, HEADS * NUM_EXPERTS), jnp.float32) * s, 'att_src': jax.random.normal(ks[2], (HEADS, NUM_EXPERTS), jnp.float32) * s, 'att_dst': jax.random.normal(ks[3], (HEADS, NUM_EXPERTS), jnp.float32) * s, 'b_gat': jnp.zeros((HEADS * NUM_EXPERTS,), jnp.float32), 'ln_gamma': jnp.ones((HEADS * NUM_EXPERTS,), jnp.float32), 'ln_beta': jnp.zeros((HEADS * NUM_EXPERTS,), jnp.float32), 'W1': jax.random.normal(ks[4], (NUM_EXPERTS, D, 2 * D), jnp.float32) * s, 'b1': jnp.zeros((NUM_EXPERTS, 2 * D), jnp.float32), 'W2': jax.random.normal(ks[5], (NUM_EXPERTS, 2 * D, D), jnp.float32) * s, 'b2': jnp.zeros((NUM_EXPERTS, D), jnp.float32), 'edge_index': jax.random.randint(ks[6], (2, N_EDGES), 0, B * N, jnp.int32)}
    _L0_ffn_all = _L0_ffn_setup()
    _L0_ffn_in = {k: v for k, v in _L0_ffn_all.items() if k in ('W_gat', 'att_src', 'att_dst', 'b_gat', 'ln_gamma', 'ln_beta', 'W1', 'b1', 'W2', 'b2', 'edge_index')}
    del _L0_ffn_all
    return {'x': x, 'src': src, 'dst': dst, 'edge_attr_128': edge_attr_128, 'L0_gnn_W_edge': _L0_gnn_in['W_edge'], 'L0_gnn_b_edge': _L0_gnn_in['b_edge'], 'L0_gnn_W1': _L0_gnn_in['W1'], 'L0_gnn_b1': _L0_gnn_in['b1'], 'L0_gnn_W2': _L0_gnn_in['W2'], 'L0_gnn_b2': _L0_gnn_in['b2'], 'L0_gnn_eps': _L0_gnn_in['eps'], 'L0_gnn_gamma': _L0_gnn_in['gamma'], 'L0_gnn_beta': _L0_gnn_in['beta'], 'L0_mix_Wqkv': _L0_mix_in['Wqkv'], 'L0_mix_ln1_g': _L0_mix_in['ln1_g'], 'L0_mix_ln1_b': _L0_mix_in['ln1_b'], 'L0_mix_W1': _L0_mix_in['W1'], 'L0_mix_b1': _L0_mix_in['b1'], 'L0_mix_W2': _L0_mix_in['W2'], 'L0_mix_b2': _L0_mix_in['b2'], 'L0_mix_ln2_g': _L0_mix_in['ln2_g'], 'L0_mix_ln2_b': _L0_mix_in['ln2_b'], 'L0_ffn_W_gat': _L0_ffn_in['W_gat'], 'L0_ffn_att_src': _L0_ffn_in['att_src'], 'L0_ffn_att_dst': _L0_ffn_in['att_dst'], 'L0_ffn_b_gat': _L0_ffn_in['b_gat'], 'L0_ffn_ln_gamma': _L0_ffn_in['ln_gamma'], 'L0_ffn_ln_beta': _L0_ffn_in['ln_beta'], 'L0_ffn_W1': _L0_ffn_in['W1'], 'L0_ffn_b1': _L0_ffn_in['b1'], 'L0_ffn_W2': _L0_ffn_in['W2'], 'L0_ffn_b2': _L0_ffn_in['b2'], 'L0_ffn_edge_index': _L0_ffn_in['edge_index']}

def reference(x, src, dst, edge_attr_128, L0_gnn_W_edge, L0_gnn_b_edge, L0_gnn_W1, L0_gnn_b1, L0_gnn_W2, L0_gnn_b2, L0_gnn_eps, L0_gnn_gamma, L0_gnn_beta, L0_mix_Wqkv, L0_mix_ln1_g, L0_mix_ln1_b, L0_mix_W1, L0_mix_b1, L0_mix_W2, L0_mix_b2, L0_mix_ln2_g, L0_mix_ln2_b, L0_ffn_W_gat, L0_ffn_att_src, L0_ffn_att_dst, L0_ffn_b_gat, L0_ffn_ln_gamma, L0_ffn_ln_beta, L0_ffn_W1, L0_ffn_b1, L0_ffn_W2, L0_ffn_b2, L0_ffn_edge_index):
    import jax
    import jax.numpy as jnp

    def _L0_gnn_ref(x, edge_index, edge_attr, W_edge, b_edge, W1, b1, W2, b2, eps, gamma, beta):
        import jax, jax.numpy as jnp
        import numpy as np
        N_NODES = 6250
        N_EDGES = 100000
        IN_DIM = 256
        OUT_DIM = 256
        EDGE_DIM = 128
        BN_EPS = 1e-05
        src, dst = (edge_index[0], edge_index[1])
        e = edge_attr @ W_edge + b_edge
        msg = jax.nn.relu(x[src] + e)
        agg = jax.ops.segment_sum(msg, dst, num_segments=x.shape[0])
        h = (1.0 + eps) * x + agg
        h = jax.nn.relu(h @ W1 + b1) @ W2 + b2
        mean = jnp.mean(h, axis=0)
        var = jnp.var(h, axis=0)
        h = (h - mean) * jax.lax.rsqrt(var + BN_EPS) * gamma + beta
        return jax.nn.relu(h)

    def _L0_mix_ref(x, Wqkv, ln1_g, ln1_b, W1, b1, W2, b2, ln2_g, ln2_b):
        import jax, jax.numpy as jnp
        import numpy as np
        N, F, C, H = (32, 512, 256, 8)
        D = C // H
        EPS_ATTN = 1e-06
        EPS_LN = 1e-05

        def layer_norm(x, g, b):
            mu = jnp.mean(x, axis=-1, keepdims=True)
            var = jnp.var(x, axis=-1, keepdims=True)
            return (x - mu) * jax.lax.rsqrt(var + EPS_LN) * g + b
        n, f, c = x.shape
        qkv = jnp.einsum('nfc,oc->nfo', x, Wqkv)
        q, k, v = jnp.split(qkv, 3, axis=-1)
        q = q.reshape(n, f, H, D)
        k = k.reshape(n, f, H, D)
        v = v.reshape(n, f, H, D)
        q = jax.nn.elu(q) + 1.0
        k = jax.nn.elu(k) + 1.0
        kv = jnp.einsum('nshd,nshm->nhmd', k, v)
        ksum = jnp.sum(k, axis=1)
        z = 1.0 / (jnp.einsum('nlhd,nhd->nlh', q, ksum) + EPS_ATTN)
        t = jnp.einsum('nlhd,nhmd,nlh->nlhm', q, kv, z)
        t = t.reshape(n, f, c)
        x1 = layer_norm(t + x, ln1_g, ln1_b)
        h = jax.nn.gelu(jnp.einsum('nfc,oc->nfo', x1, W1) + b1, approximate=False)
        y = jnp.einsum('nfc,oc->nfo', h, W2) + b2
        return layer_norm(y + x1, ln2_g, ln2_b)

    def _L0_ffn_ref(x, W_gat, att_src, att_dst, b_gat, ln_gamma, ln_beta, W1, b1, W2, b2, edge_index):
        import jax, jax.numpy as jnp
        import numpy as np
        B, N, D = (16, 512, 256)
        NUM_EXPERTS, TOP_K, HEADS = (4, 2, 4)
        N_EDGES = 131072
        LN_EPS = 1e-05

        def _layernorm(x, g, b):
            mu = x.mean(-1, keepdims=True)
            var = ((x - mu) ** 2).mean(-1, keepdims=True)
            return (x - mu) * jax.lax.rsqrt(var + LN_EPS) * g + b

        def _forward(x, edge_index, W_gat, att_src, att_dst, b_gat, ln_gamma, ln_beta, W1, b1, W2, b2):
            Bc, Nc, Dc = x.shape
            M = Bc * Nc
            x_flat = x.reshape(M, Dc)
            h = (x_flat @ W_gat).reshape(M, HEADS, NUM_EXPERTS)
            loops = jnp.arange(M, dtype=edge_index.dtype)
            src = jnp.concatenate([edge_index[0], loops])
            dst = jnp.concatenate([edge_index[1], loops])
            a_src = (h * att_src).sum(-1)
            a_dst = (h * att_dst).sum(-1)
            e = jax.nn.leaky_relu(a_src[src] + a_dst[dst], negative_slope=0.2)
            e_max = jax.ops.segment_max(e, dst, num_segments=M)
            ee = jnp.exp(e - e_max[dst])
            denom = jax.ops.segment_sum(ee, dst, num_segments=M)
            alpha = ee / (denom[dst] + 1e-16)
            msg = h[src] * alpha[:, :, None]
            agg = jax.ops.segment_sum(msg, dst, num_segments=M).reshape(M, HEADS * NUM_EXPERTS) + b_gat
            scores = _layernorm(agg, ln_gamma, ln_beta).reshape(M, HEADS, NUM_EXPERTS).mean(1)
            scores = scores.reshape(Bc, Nc, NUM_EXPERTS)
            topk_s, topk_i = jax.lax.top_k(scores, TOP_K)
            w = jax.nn.softmax(topk_s, axis=-1)
            out = jnp.zeros_like(x)
            for ei in range(NUM_EXPERTS):
                g = jnp.where(topk_i == ei, w, 0.0).sum(-1)
                hh = jax.nn.gelu(x @ W1[ei] + b1[ei], approximate=False)
                out = out + g[..., None] * (hh @ W2[ei] + b2[ei])
            return out
        return _forward(x, edge_index, W_gat, att_src, att_dst, b_gat, ln_gamma, ln_beta, W1, b1, W2, b2)
    edge_index = jnp.stack([src, dst])
    xn = _layernorm(x, axis=-1)
    x = x + _L0_gnn_ref(xn, edge_index, edge_attr_128, L0_gnn_W_edge, L0_gnn_b_edge, L0_gnn_W1, L0_gnn_b1, L0_gnn_W2, L0_gnn_b2, L0_gnn_eps, L0_gnn_gamma, L0_gnn_beta) + _L0_mix_ref(xn[None], L0_mix_Wqkv, L0_mix_ln1_g, L0_mix_ln1_b, L0_mix_W1, L0_mix_b1, L0_mix_W2, L0_mix_b2, L0_mix_ln2_g, L0_mix_ln2_b)[0]
    x = x + _L0_ffn_ref(_layernorm(x, axis=-1)[None], L0_ffn_W_gat, L0_ffn_att_src, L0_ffn_att_dst, L0_ffn_b_gat, L0_ffn_ln_gamma, L0_ffn_ln_beta, L0_ffn_W1, L0_ffn_b1, L0_ffn_W2, L0_ffn_b2, L0_ffn_edge_index)[0]
    return x

_drawn_inputs = setup_inputs


def setup_inputs(seed=0):
    import zlib

    import numpy as np

    out = dict(_drawn_inputs(seed))
    spreads = {'L0_gnn_b_edge': (0.0, 0.1),
     'L0_gnn_b1': (0.0, 0.731),
     'L0_gnn_b2': (0.0, 0.8),
     'L0_gnn_gamma': (1.0, 0.2),
     'L0_gnn_beta': (0.0, 0.1),
     'L0_mix_ln1_g': (1.0, 0.2),
     'L0_mix_ln1_b': (0.0, 0.1),
     'L0_mix_ln2_g': (1.0, 0.2),
     'L0_mix_ln2_b': (0.0, 0.1),
     'L0_ffn_b_gat': (0.0, 0.1),
     'L0_ffn_ln_gamma': (1.0, 0.2),
     'L0_ffn_ln_beta': (0.0, 0.268),
     'L0_ffn_b1': (0.0, 0.313),
     'L0_ffn_b2': (0.0, 0.1)}
    factors = {'L0_mix_Wqkv': 5.626, 'L0_mix_b1': 7.367, 'L0_ffn_att_src': 2.858, 'L0_ffn_att_dst': 5.797}
    for name, (base, spread) in spreads.items():
        noise = np.random.default_rng([zlib.crc32(name.encode()), seed]).standard_normal(out[name].shape)
        drawn = base * np.exp(spread * noise) if base else spread * noise
        out[name] = jnp.asarray(drawn.astype(out[name].dtype))
    for name, factor in factors.items():
        out[name] = (out[name] * factor).astype(out[name].dtype)
    return out
```

```python
import numpy as np
import concourse.bass as bass
from concourse import mybir
from contextlib import ExitStack

F32 = mybir.dt.float32
BF16 = mybir.dt.bfloat16
I32 = mybir.dt.int32
ALU = mybir.AluOpType
ACT = mybir.ActivationFunctionType
AX = mybir.AxisListType.X

P = 128
N_NODES = 6250
C = 256
KC = C // P
N_EDGES = 100000
E_DIM = 128
G_EDGES = 131072
NT = -(-N_NODES // P)
NPAD = NT * P
ST = 7
STEPS = NT // ST
SN = ST * P
HN = SN // 2
LN_EPS = 1e-5
HD = 32
HH = P // HD
EXPERTS = 4
HEADS = 4
GF = HEADS * EXPERTS
FF = 512
FC = FF // P
ROW = GF + HEADS
BIG = 1.0e30


class Chain:

    def __init__(self, eng, sem, base=0):
        self.eng, self.sem, self.base, self.n = eng, sem, base, 0

    def add(self, ins):
        self.n += 1
        ins.then_inc(self.sem, 1)

    def wait(self):
        self.eng.wait_ge(self.sem, self.base + self.n)

    def __call__(self, ins):
        self.add(ins)
        self.wait()


class Program:

    def __init__(self, nc, args, stack):
        self.nc, self.a, self.stack = nc, args, stack
        self.turns = stack.enter_context(nc.semaphore("turns"))
        self.sems = []

    def sem(self, name):
        self.sems.append(self.nc.alloc_semaphore(name=name))
        return self.sems[-1]

    def end_stage(self):
        self.nc.clear_and_free_semaphores(self.sems)
        self.nc.all_engine_barrier()
        self.sems = []

    def dram(self, name, shape, dtype=F32):
        return self.nc.dram_tensor(name, shape, dtype)

    def keep(self, name, shape, dtype=F32):
        return self.stack.enter_context(self.nc.sbuf_tensor(name, shape, dtype))


def node_rows(ap, i):
    return ap[bass.ds(i * SN, SN), :].rearrange("(j p) c -> p j c", p=P)


def feat_cols(ap, i):
    return ap[:, :, bass.ds(i * SN, SN)].rearrange("h p n -> p h n")


def setup(pg):
    nc, a = pg.nc, pg.a
    pg.ident = pg.keep("ident", [P, P])
    pg.ones_row = pg.keep("ones_row", [1, P])
    pg.zeros = pg.keep("zeros", [P, 512])
    pg.headmask = pg.keep("headmask", [P, HH])
    pg.valid = pg.keep("valid", [P, NT])
    pg.kv_blocks = pg.keep("kv_blocks", [P, KC, P + HH])
    pg.first = pg.keep("first", [P, NT], I32)
    pg.last = pg.keep("last", [P, NT], I32)
    pg.starts = pg.keep("starts", [P, NT, 8])
    pg.sums = pg.keep("sums", [P, NT, ROW])
    pg.gate = pg.keep("gate", [P, NT, EXPERTS])
    pg.xpad = pg.dram("xpad", [NPAD, C]).ap()
    pg.xn_d = pg.dram("xn_d", [NPAD, C]).ap()
    pg.xb_d = pg.dram("xb_d", [NPAD, C]).ap()
    pg.xT_d = pg.dram("xT_d", [KC, P, NPAD]).ap()
    pg.mix_d = pg.dram("mix_d", [NPAD, C]).ap()
    pg.x2_d = pg.dram("x2_d", [NPAD, C]).ap()
    pg.x3T_d = pg.dram("x3T_d", [KC, P, NPAD]).ap()
    s_zero, s_mask, s_pad = pg.sem("s_zero"), pg.sem("s_mask"), pg.sem("s_pad")
    with nc.Block() as block:
        @block.gpsimd
        def _(pool):
            nc.gpsimd.memset(pg.zeros[:, :], 0.0).then_inc(s_zero, 1)
            nc.gpsimd.memset(pg.ones_row[:, :], 1.0).then_inc(s_mask, 1)
            nc.gpsimd.memset(pg.ident[:, :], 0.0).then_inc(s_mask, 1)
            nc.gpsimd.memset(pg.headmask[:, :], 1.0).then_inc(s_mask, 1)
            nc.gpsimd.memset(pg.valid[:, :], 1.0).then_inc(s_mask, 1)
            pool.wait_ge(s_mask, 4)
            nc.gpsimd.affine_select(out=pg.ident[:, :], in_=pg.ident[:, :], compare_op=ALU.not_equal, fill=1.0,
                                    base=0, pattern=[[-1, P]], channel_multiplier=1).then_inc(s_mask, 1)
            nc.gpsimd.affine_select(out=pg.headmask[:, :], in_=pg.headmask[:, :], compare_op=ALU.is_ge, fill=0.0,
                                    base=0, pattern=[[-HD, HH]], channel_multiplier=1).then_inc(s_mask, 1)
            pool.wait_ge(s_mask, 6)
            nc.gpsimd.affine_select(out=pg.headmask[:, :], in_=pg.headmask[:, :], compare_op=ALU.is_ge, fill=0.0,
                                    base=HD - 1, pattern=[[HD, HH]], channel_multiplier=-1).then_inc(s_mask, 1)
            nc.gpsimd.affine_select(out=pg.valid[:, :], in_=pg.valid[:, :], compare_op=ALU.is_ge, fill=0.0,
                                    base=N_NODES - 1, pattern=[[-P, NT]], channel_multiplier=-1).then_inc(s_mask, 1)
            pool.wait_ge(s_mask, 8)

        @block.sync
        def _(sp):
            sp.dma_start(pg.xpad[0:N_NODES, :], a["x"]).then_inc(s_pad, 16)
            sp.wait_ge(s_zero, 1)
            sp.dma_start(pg.xpad[N_NODES:NPAD, :], pg.zeros[0:NPAD - N_NODES, 0:C]).then_inc(s_pad, 16)
            sp.wait_ge(s_pad, 32)


def norm_statistics(nc, dve, ch, turns, rows, stats, mv, var, var_ready, std, std_ready, count):
    for j in range(ST):
        ch.add(nc.vector.bn_stats(out=stats[:, j, :], in_=rows[:, j, :]))
    ch.wait()
    dve.sem_inc(turns, 1)
    for j in range(ST):
        ch.add(nc.vector.bn_aggr(out=mv[:, j, :], in_=stats[:, j, :]))
    ch.wait()
    nc.vector.tensor_scalar_add(var[:, :], mv[:, :, 1], LN_EPS).then_inc(var_ready, 1)
    dve.wait_ge(std_ready, count)
    ch(nc.vector.reciprocal(var[:, :], std[:, :]))


NORM_STEPS = 2 * ST + 1


def normalise(nc, ch, out, rows, mv, rstd):
    for j in range(ST):
        ch.add(nc.vector.tensor_scalar(out=out[:, j, :], in0=rows[:, j, :], scalar1=mv[:, j, 0:1],
                                       scalar2=rstd[:, j:j + 1], op0=ALU.subtract, op1=ALU.mult))
    ch.wait()


UNITS = [(q, min(4, KC * ST - q)) for q in range(0, KC * ST, 4)]
NU = len(UNITS)


def transpose_rows(nc, pe, rows, ident, tp, tp_ready, tp_free, count):
    for u, (q0, nq) in enumerate(UNITS):
        pe.wait_ge(tp_free, count + u + 1)
        for q in range(q0, q0 + nq):
            h, j = q // ST, q % ST
            last = nc.tensor.transpose(tp[u % 2][:, (q - q0) * P:(q - q0 + 1) * P],
                                       rows[:, j, h * P:(h + 1) * P], ident[:, :])
        last.then_inc(tp_ready, 1)


def copy_blocks(nc, act, out, tp, tp_ready, tp_free, out_ready, count, tp_start=0):
    flat = out[:, :, :].rearrange("p h n -> p (h n)")
    for u, (q0, nq) in enumerate(UNITS):
        act.wait_ge(tp_ready, count + u + 1 + tp_start)
        nc.scalar.activation(flat[:, q0 * P:(q0 + nq) * P], tp[u % 2][:, 0:nq * P], ACT.Copy).then_inc(tp_free, 1)
    act.wait_ge(tp_free, count + NU + 2)
    act.sem_inc(out_ready, 1)


def stage_norm(pg):
    nc, a = pg.nc, pg.a
    with ExitStack() as st:
        sb = lambda n, s, d=F32: st.enter_context(nc.sbuf_tensor("n_" + n, s, d))
        pb = lambda n, s, d=F32: st.enter_context(nc.psum_tensor("n_" + n, s, d))
        x_in, xn, xb = sb("x_in", [P, ST, C]), sb("xn", [P, ST, C]), sb("xb", [P, ST, C])
        xT = sb("xT", [P, KC, SN])
        b_edge = sb("b_edge", [P, C])
        wkv = sb("wkv", [P, KC, 2 * C])
        stats, mv = sb("stats", [P, ST, 6]), sb("mv", [P, ST, 2])
        std, rstd = sb("std", [P, ST]), sb("rstd", [P, ST])
        kneg, kexp, kf = (sb(n, [P, ST, C]) for n in ("kneg", "kexp", "kf"))
        vf = sb("vf", [P, ST, KC, P + 1])
        tp = [pb(f"tp{i}", [P, 512]) for i in range(2)]
        kp = [pb(f"kp{i}", [P, C]) for i in range(2)]
        vp = [pb(f"vp{i}", [P, C]) for i in range(2)]
        kv = pb("kv", [P, KC * (P + 1)])
        rows_ready, rows_free = pg.sem("n_rows_ready"), pg.sem("n_rows_free")
        w_ready, steps = pg.sem("n_w_ready"), pg.sem("n_steps")
        var_ready, std_ready = pg.sem("n_var_ready"), pg.sem("n_std_ready")
        xn_ready, xn_free = pg.sem("n_xn_ready"), pg.sem("n_xn_free")
        stored = pg.sem("n_stored")
        tp_ready, tp_free = pg.sem("n_tp_ready"), pg.sem("n_tp_free")
        xT_ready, xT_free, xT_stored = pg.sem("n_xT_ready"), pg.sem("n_xT_free"), pg.sem("n_xT_stored")
        kvp_ready = pg.sem("n_kvp_ready")
        kneg_ready, kexp_ready = pg.sem("n_kneg_ready"), pg.sem("n_kexp_ready")
        kf_ready, vf_ready, kv_used = pg.sem("n_kf_ready"), pg.sem("n_vf_ready"), pg.sem("n_kv_used")
        kv_done = pg.sem("n_kv_done")
        with nc.Block() as block:
            @block.sync
            def _(sp):
                sp.dma_start(wkv[:, :, :], a["mix_wqkvT"][:, C:3 * C].rearrange("(h p) n -> p h n", p=P)).then_inc(w_ready, 16)
                sp.dma_start(b_edge[:, :], a["b_edge"].rearrange("(o c) -> o c", o=1).to_broadcast([P, C])).then_inc(w_ready, 16)
                with sp.Fori(0, STEPS) as i:
                    sp.wait_ge(rows_free, i + 1)
                    sp.dma_start(x_in[:, :, :], node_rows(pg.xpad, i)).then_inc(rows_ready, 16)

            @block.gpsimd
            def _(pool):
                pool.sem_inc(xn_free, 1)
                pool.sem_inc(xT_stored, 1)
                with pool.Fori(0, STEPS) as i:
                    pool.wait_ge(xn_ready, i + 1)
                    pool.dma_start(node_rows(pg.xn_d, i), xn[:, :, :]).then_inc(stored, 16)
                    pool.dma_start(node_rows(pg.xb_d, i), xb[:, :, :]).then_inc(stored, 16)
                    pool.wait_ge(xT_ready, i + 1)
                    pool.dma_start(feat_cols(pg.xT_d, i), xT[:, :, :]).then_inc(stored, 16)
                    pool.wait_ge(stored, i * 48 + 48)
                    pool.sem_inc(xn_free, 1)
                    pool.sem_inc(xT_stored, 1)

            @block.vector
            def _(dve):
                dve.sem_inc(rows_free, 1)
                dve.wait_ge(w_ready, 32)
                K = NORM_STEPS + ST
                with dve.Fori(0, STEPS) as i:
                    ch = Chain(dve, steps, i * K)
                    dve.wait_ge(rows_ready, i * 16 + 16)
                    norm_statistics(nc, dve, ch, pg.turns, x_in, stats, mv, rstd, var_ready, std, std_ready, i + 1)
                    dve.wait_ge(xn_free, i + 1)
                    normalise(nc, ch, xn, x_in, mv, rstd)
                    assert ch.n == K
                    dve.sem_inc(rows_free, 1)
                    nc.vector.tensor_tensor(out=xb[:, :, :], in0=xn[:, :, :],
                                            in1=b_edge[:, :].unsqueeze(1).to_broadcast([P, ST, C]),
                                            op=ALU.add).then_inc(xn_ready, 1)
                    for j in range(ST):
                        dve.wait_ge(kvp_ready, i * ST + j + 1)
                        if j == 0:
                            dve.wait_ge(kv_used, i + 1)
                        nc.vector.tensor_scalar_min(kneg[:, j, :], kp[j % 2][:, :], 0.0).then_inc(kneg_ready, 1)
                        dve.wait_ge(kexp_ready, i * ST + j + 1)
                        nc.vector.scalar_tensor_tensor(out=kf[:, j, :], in0=kp[j % 2][:, :], scalar=0.0,
                                                       in1=kexp[:, j, :], op0=ALU.max, op1=ALU.add).then_inc(kf_ready, 1)
                dve.wait_ge(kv_done, 1)
                kvs = kv[:, :].rearrange("p (h n) -> p h n", h=KC)
                hm = pg.headmask[:, :]
                for h in range(KC):
                    nc.vector.tensor_tensor(
                        out=pg.kv_blocks[:, h, 0:P].rearrange("p (g d) -> p g d", g=HH),
                        in0=kvs[:, h, 0:P].rearrange("p (g d) -> p g d", g=HH),
                        in1=hm.unsqueeze(2).to_broadcast([P, HH, HD]), op=ALU.mult)
                    nc.vector.tensor_scalar(out=pg.kv_blocks[:, h, P:P + HH], in0=hm, scalar1=kvs[:, h, P:P + 1],
                                            scalar2=None, op0=ALU.mult)

            @block.scalar
            def _(act):
                act.sem_inc(tp_free, 2)
                with act.Fori(0, STEPS) as i:
                    act.wait_ge(var_ready, i + 1)
                    nc.scalar.activation(std[:, :], rstd[:, :], ACT.Sqrt).then_inc(std_ready, 1)
                    act.wait_ge(xT_stored, i + 1)
                    act.wait_ge(xT_free, i + 1)
                    copy_blocks(nc, act, xT, tp, tp_ready, tp_free, xT_ready, i * NU)
                    for j in range(ST):
                        act.wait_ge(kvp_ready, i * ST + j + 1)
                        if j == 0:
                            act.wait_ge(kv_used, i + 1)
                        nc.scalar.activation(vf[:, j, :, 0:P], vp[j % 2][:, :].rearrange("p (h n) -> p h n", h=KC),
                                             ACT.Copy).then_inc(vf_ready, 1)
                        for h in range(KC):
                            nc.scalar.activation(vf[:, j, h, P:P + 1], pg.valid[:, bass.ds(i * ST + j, 1)],
                                                 ACT.Copy).then_inc(vf_ready, 1)
                        act.wait_ge(kneg_ready, i * ST + j + 1)
                        nc.scalar.activation(kexp[:, j, :], kneg[:, j, :], ACT.Exp).then_inc(kexp_ready, 1)

            @block.tensor
            def _(pe):
                pe.wait_ge(w_ready, 32)
                pe.sem_inc(xT_free, 1)
                pe.sem_inc(kv_used, 1)
                nc.tensor.matmul(kv[:, :], pg.zeros[:, 0:P], pg.zeros[:, 0:KC * (P + 1)], start=True, stop=True)
                with pe.Fori(0, STEPS) as i:
                    pe.wait_ge(xn_ready, i + 1)
                    transpose_rows(nc, pe, xn, pg.ident, tp, tp_ready, tp_free, i * NU)
                    pe.wait_ge(xT_ready, i + 1)
                    for j in range(ST):
                        if j >= 2:
                            pe.wait_ge(kf_ready, i * ST + j - 1)
                            pe.wait_ge(vf_ready, (i * ST + j - 1) * 3)
                        for o, out in enumerate((kp, vp)):
                            for c in range(KC):
                                last = nc.tensor.matmul(out[j % 2][:, :], xT[:, c, j * P:(j + 1) * P],
                                                        wkv[:, c, o * C:(o + 1) * C], start=(c == 0), stop=(c == KC - 1))
                        last.then_inc(kvp_ready, 1)
                    pe.wait_ge(kf_ready, i * ST + ST)
                    pe.wait_ge(vf_ready, (i * ST + ST) * 3)
                    pe.sem_inc(xT_free, 1)
                    for j in range(ST):
                        for h in range(KC):
                            last = nc.tensor.matmul(kv[:, h * (P + 1):(h + 1) * (P + 1)], kf[:, j, h * P:(h + 1) * P],
                                                    vf[:, j, h, :], start=False, stop=True, skip_group_check=True)
                    last.then_inc(kv_used, 1)
                pe.wait_ge(kv_used, STEPS + 1)
                pe.sem_inc(kv_done, 1)


GT = G_EDGES // P
GB = 8
GR = GT // P
RUN = GT + NT
SLOTS = 2


SORT_BATCHES = 88
MIX_BATCHES = GT // GB - SORT_BATCHES


def scatter_batches(pg, pool, name, first, count, ready=None):
    nc = pg.nc
    copied = pg.sem(name + "_copied")
    sent = [pg.sem(f"{name}_sent{b}") for b in range(SLOTS)]

    def batch(i, b, fresh):
        k = i * SLOTS + b
        if ready is not None:
            pool.wait_ge(ready, first + k + 1)
        if not fresh:
            pool.wait_ge(sent[b], i * (16 * GB))
        nc.gpsimd.tensor_copy(pg.place[b][:, :], pg.place_col[:, bass.ds((first + k) * GB, GB)]).then_inc(copied, 1)
        nc.gpsimd.tensor_copy(pg.source[b][:, :], pg.src_col[:, bass.ds((first + k) * GB, GB)]).then_inc(copied, 1)
        pool.wait_ge(copied, k * 2 + 2)
        pool.sem_inc(pg.turns, 1)
        for t in range(GB):
            pool.indirect_dma_start(out=pg.sorted_d, out_offset=bass.IndirectOffsetOnAxis(ap=pg.place[b][:, t:t + 1], axis=0),
                                    in_=pg.source[b][:, t:t + 1], in_offset=None).then_inc(sent[b], 16)

    for b in range(SLOTS):
        batch(0, b, True)
    with pool.Fori(1, count // SLOTS) as i:
        for b in range(SLOTS):
            batch(i, b, False)
    for b in range(SLOTS):
        pool.wait_ge(sent[b], 16 * GB * (count // SLOTS))


def stage_sort(pg):
    nc, a = pg.nc, pg.a
    pg.sorted_d = pg.dram("sorted_d", [P * RUN, 1], I32).ap()
    lo_d = pg.dram("lo_d", [G_EDGES], BF16).ap()
    with ExitStack() as st:
        sb = lambda n, s, d=F32: st.enter_context(nc.sbuf_tensor("s_" + n, s, d))
        pb = lambda n, s, d=F32: st.enter_context(nc.psum_tensor("s_" + n, s, d))
        src_i, key_i, tmp_i = (sb(n, [P, GT], I32) for n in ("src_i", "key_i", "tmp_i"))
        src_f, lo_f, hi_f = (sb(n, [P, GT]) for n in ("src_f", "lo_f", "hi_f"))
        lo_b = sb("lo_b", [P, GT], BF16)
        src_col, place_col = pg.src_col, pg.place_col
        lo_col, hi_col = sb("lo_col", [P, GT], BF16), sb("hi_col", [P, GT], BF16)
        iota_p = sb("iota_p", [P, 1])
        iota_lo = sb("iota_lo", [P, P], BF16)
        iota_hi = sb("iota_hi", [P, NT], BF16)
        before = sb("before", [P, P])
        before_b = sb("before_b", [P, P], BF16)
        ones = sb("ones", [P, P])
        counts, totals, starts, first_f, last_f, seed = (
            sb(n, [P, NT]) for n in ("counts", "totals", "starts", "first_f", "last_f", "seed"))
        lo_row = [sb(f"lo_row{i}", [P, GB, P], BF16) for i in range(SLOTS)]
        one_lo = [sb(f"one_lo{i}", [P, GB, P], BF16) for i in range(SLOTS)]
        one_hi = [sb(f"one_hi{i}", [P, GB, NT], BF16) for i in range(SLOTS)]
        one_loT = [sb(f"one_loT{i}", [P, GB, P]) for i in range(SLOTS)]
        same = [sb(f"same{i}", [P, GB, P], BF16) for i in range(SLOTS)]
        seen = [sb(f"seen{i}", [P, NT]) for i in range(2)]
        ranked = sb("ranked", [P, GB, NT])
        place_f = sb("place_f", [P, GB])
        tp = [pb(f"tp{i}", [P, 512]) for i in range(2)]
        total = pb("total", [P, NT])
        live = pb("live", [P, NT])
        rank = [pb(f"rank{i}", [P, GB, NT]) for i in range(SLOTS)]
        loaded, steps, const = pg.sem("s_loaded"), pg.sem("s_steps"), pg.sem("s_const")
        keys_ready, src_ready = pg.sem("s_keys_ready"), pg.sem("s_src_ready")
        lo_stored = pg.sem("s_lo_stored")
        tp_ready, tp_free, cols_ready = pg.sem("s_tp_ready"), pg.sem("s_tp_free"), pg.sem("s_cols_ready")
        hot_ready, hot_used = pg.sem("s_hot_ready"), pg.sem("s_hot_used")
        counted, prefix_ready, prefix_in = pg.sem("s_counted"), pg.sem("s_prefix_ready"), pg.sem("s_prefix_in")
        first_ready, seeded = pg.sem("s_first_ready"), pg.sem("s_seeded")
        row_ready = [pg.sem(f"s_row_ready{i}") for i in range(SLOTS)]
        row_free = pg.sem("s_row_free")
        live_ready, seen_ready = pg.sem("s_live_ready"), pg.sem("s_seen_ready")
        sets_ready, sets_used = pg.sem("s_sets_ready"), pg.sem("s_sets_used")
        rank_ready, rank_free = pg.sem("s_rank_ready"), pg.sem("s_rank_free")
        place_ready = pg.sem("s_place_ready")
        NB = GT // GB
        PAIRS = NB // SLOTS
        with nc.Block() as block:
            @block.sync
            def _(sp):
                sp.dma_start(key_i[:, :], a["g_edges"][1, :].rearrange("(p c) -> p c", p=P)).then_inc(loaded, 16)
                sp.dma_start(src_i[:, :], a["g_edges"][0, :].rearrange("(p c) -> p c", p=P)).then_inc(loaded, 16)
                sp.wait_ge(keys_ready, 1)
                sp.dma_start(lo_d.rearrange("(p c) -> p c", p=P), lo_b[:, :]).then_inc(lo_stored, 16)
                sp.wait_ge(lo_stored, 16)
                with sp.Fori(0, PAIRS) as i:
                    for b in range(SLOTS):
                        sp.wait_ge(row_free, i * SLOTS + b + 1)
                        rows = lo_d[bass.ds((i * SLOTS + b) * GB * P, GB * P)]
                        sp.dma_start(lo_row[b][:, :, :].rearrange("p t e -> p (t e)"),
                                     rows.rearrange("(o n) -> o n", o=1).to_broadcast([P, GB * P])).then_inc(row_ready[b], 16)

            @block.gpsimd
            def _(pool):
                nc.gpsimd.iota(iota_p[:, :], pattern=[[0, 1]], base=0, channel_multiplier=1,
                               allow_small_or_imprecise_dtypes=True).then_inc(const, 1)
                nc.gpsimd.iota(iota_lo[:, :], pattern=[[1, P]], base=0, channel_multiplier=0,
                               allow_small_or_imprecise_dtypes=True).then_inc(const, 1)
                nc.gpsimd.iota(iota_hi[:, :], pattern=[[1, NT]], base=0, channel_multiplier=0,
                               allow_small_or_imprecise_dtypes=True).then_inc(const, 1)
                nc.gpsimd.iota(pg.node_id[:, :], pattern=[[P, NT]], base=0, channel_multiplier=1).then_inc(const, 1)
                nc.gpsimd.memset(ones[:, :], 1.0).then_inc(const, 1)
                pool.wait_ge(const, 5)
                nc.gpsimd.affine_select(out=before[:, :], in_=ones[:, :], compare_op=ALU.is_ge, fill=0.0,
                                        base=-1, pattern=[[1, P]], channel_multiplier=-1).then_inc(const, 1)
                pool.wait_ge(const, 6)
                nc.gpsimd.tensor_copy(before_b[:, :], before[:, :]).then_inc(const, 1)
                scatter_batches(pg, pool, "s", 0, SORT_BATCHES, place_ready)

            @block.vector
            def _(dve):
                ch = Chain(dve, steps)
                dve.wait_ge(loaded, 32)
                ch.add(nc.vector.tensor_scalar_min(src_f[:, :], src_i[:, :], float(N_NODES - 1)))
                ch(nc.vector.tensor_scalar_min(tmp_i[:, :], key_i[:, :], float(N_NODES)))
                ch(nc.vector.tensor_single_scalar(key_i[:, :], tmp_i[:, :], P - 1, op=ALU.bitwise_and))
                ch.add(nc.vector.tensor_copy(lo_f[:, :], key_i[:, :]))
                ch(nc.vector.tensor_copy(lo_b[:, :], key_i[:, :]))
                dve.sem_inc(keys_ready, 1)
                ch(nc.vector.tensor_single_scalar(key_i[:, :], tmp_i[:, :], 7, op=ALU.logical_shift_right))
                ch(nc.vector.tensor_copy(hi_f[:, :], key_i[:, :]))
                dve.sem_inc(src_ready, 1)
                dve.sem_inc(row_free, SLOTS)
                dve.sem_inc(rank_free, SLOTS)
                dve.wait_ge(const, 7)
                dve.wait_ge(cols_ready, 1)
                base = ch.n

                def one_hots(b, tile):
                    nc.vector.tensor_tensor(out=one_lo[b][:, :, :], in0=iota_lo[:, :].unsqueeze(1).to_broadcast([P, GB, P]),
                                            in1=lo_col[:, bass.ds(tile, GB)].unsqueeze(2).to_broadcast([P, GB, P]),
                                            op=ALU.is_equal).then_inc(hot_ready, 1)
                    nc.vector.tensor_tensor(out=one_hi[b][:, :, :], in0=iota_hi[:, :].unsqueeze(1).to_broadcast([P, GB, NT]),
                                            in1=hi_col[:, bass.ds(tile, GB)].unsqueeze(2).to_broadcast([P, GB, NT]),
                                            op=ALU.is_equal).then_inc(hot_ready, 1)

                with dve.Fori(0, PAIRS) as i:
                    for b in range(SLOTS):
                        dve.wait_ge(hot_used, i * SLOTS + b + 1)
                        one_hots(b, (i * SLOTS + b) * GB)
                dve.wait_ge(counted, 1)
                ch(nc.vector.tensor_scalar_add(counts[:, :], total[:, :], 1.0))
                dve.sem_inc(prefix_in, 1)
                dve.wait_ge(prefix_ready, 1)
                ch(nc.vector.tensor_copy(totals[:, :], total[:, :]))
                ch(nc.vector.tensor_tensor_scan(out=starts[:, :], data0=ones[:, 0:NT], data1=totals[:, :], initial=0.0,
                                                op0=ALU.mult, op1=ALU.add))
                ch(nc.vector.tensor_tensor(out=starts[:, :], in0=starts[:, :], in1=totals[:, :], op=ALU.subtract))
                ch(nc.vector.tensor_tensor(out=first_f[:, :], in0=starts[:, :], in1=live[:, :], op=ALU.add))
                ch(nc.vector.tensor_copy(pg.first[:, :], first_f[:, :]))
                ch(nc.vector.tensor_scalar_add(seed[:, :], first_f[:, :], 1.0))
                dve.sem_inc(first_ready, 1)
                ch(nc.vector.tensor_tensor(out=last_f[:, :], in0=first_f[:, :], in1=counts[:, :], op=ALU.add))
                ch(nc.vector.tensor_scalar_add(pg.last[:, :], last_f[:, :], -1.0))
                base += 9

                def prepare(ch, n, b, turn):
                    dve.wait_ge(sets_used, n + 1)
                    one_hots(b, n * GB)
                    dve.wait_ge(row_ready[b], turn * 16 + 16)
                    ch.add(nc.vector.tensor_tensor(out=same[b][:, :, :], in0=lo_row[b][:, :, :],
                                                   in1=lo_col[:, bass.ds(n * GB, GB)].unsqueeze(2).to_broadcast([P, GB, P]),
                                                   op=ALU.is_equal))
                    ch(nc.vector.tensor_scalar(out=one_loT[b][:, :, :], in0=lo_row[b][:, :, :], scalar1=iota_p[:, 0:1],
                                               scalar2=None, op0=ALU.is_equal))
                    dve.sem_inc(row_free, 1)
                    nc.vector.tensor_tensor(out=same[b][:, :, :], in0=same[b][:, :, :],
                                            in1=before_b[:, :].unsqueeze(1).to_broadcast([P, GB, P]),
                                            op=ALU.mult).then_inc(sets_ready, 1)

                def finish(ch, n, b):
                    dve.wait_ge(rank_ready, n + 1)
                    ch(nc.vector.tensor_tensor(out=ranked[:, :, :], in0=rank[b][:, :, :], in1=one_hi[b][:, :, :], op=ALU.mult))
                    dve.sem_inc(rank_free, 1)
                    ch(nc.vector.tensor_reduce(out=place_f[:, :], in_=ranked[:, :, :], axis=AX, op=ALU.add))
                    nc.vector.tensor_copy(place_col[:, bass.ds(n * GB, GB)], place_f[:, :]).then_inc(place_ready, 1)

                K = 4
                prepare(Chain(dve, steps, base), 0, 0, 0)
                base += 2
                with dve.Fori(0, PAIRS - 1) as i:
                    ch = Chain(dve, steps, base + i * SLOTS * K)
                    prepare(ch, i * 2 + 1, 1, i)
                    finish(ch, i * 2, 0)
                    prepare(ch, i * 2 + 2, 0, i + 1)
                    finish(ch, i * 2 + 1, 1)
                    assert ch.n == SLOTS * K
                ch = Chain(dve, steps, base + (PAIRS - 1) * SLOTS * K)
                prepare(ch, NB - 1, 1, PAIRS - 1)
                finish(ch, NB - 2, 0)
                finish(ch, NB - 1, 1)

            @block.scalar
            def _(act):
                act.sem_inc(tp_free, 2)
                n = 0
                for dst in (src_col, lo_col, hi_col):
                    for b in range(GR):
                        act.wait_ge(tp_ready, n + 1)
                        nc.scalar.activation(dst[:, :].rearrange("p (r b) -> p b r", b=GR)[:, b, :], tp[n % 2][:, 0:P],
                                             ACT.Copy).then_inc(tp_free, 1)
                        n += 1
                act.wait_ge(tp_free, n + 2)
                act.sem_inc(cols_ready, 1)
                with act.Fori(0, NB) as i:
                    for t in range(GB):
                        act.wait_ge(live_ready, i * GB + t + 1)
                        nc.scalar.activation(seen[t % 2][:, :], live[:, :], ACT.Copy).then_inc(seen_ready, 1)

            @block.tensor
            def _(pe):
                pe.wait_ge(src_ready, 1)
                pe.sem_inc(hot_used, SLOTS)
                pe.sem_inc(sets_used, SLOTS)
                n = 0
                for src in (src_f, lo_f, hi_f):
                    for b in range(GR):
                        pe.wait_ge(tp_free, n + 1)
                        nc.tensor.transpose(tp[n % 2][:, 0:P], src[:, b * P:(b + 1) * P], pg.ident[:, :]).then_inc(tp_ready, 1)
                        n += 1
                nc.tensor.matmul(total[:, :], pg.zeros[:, 0:P], pg.zeros[:, 0:NT], start=True, stop=True)
                with pe.Fori(0, PAIRS) as i:
                    for b in range(SLOTS):
                        pe.wait_ge(hot_ready, (i * SLOTS + b) * 2 + 2)
                        for t in range(GB):
                            last = nc.tensor.matmul(total[:, :], one_lo[b][:, t, :], one_hi[b][:, t, :],
                                                    start=False, stop=True, skip_group_check=True)
                        last.then_inc(hot_used, 1)
                pe.wait_ge(hot_used, SLOTS + NB)
                pe.sem_inc(counted, 1)
                pe.wait_ge(prefix_in, 1)
                nc.tensor.matmul(total[:, :], ones[:, :], counts[:, :], start=True, stop=True)
                nc.tensor.matmul(live[:, :], before[:, :], counts[:, :], start=True, stop=True).then_inc(prefix_ready, 1)
                pe.wait_ge(first_ready, 1)
                nc.tensor.matmul(live[:, :], pg.ident[:, :], seed[:, :], start=True, stop=True).then_inc(live_ready, 1)
                with pe.Fori(0, PAIRS) as i:
                    for b in range(SLOTS):
                        n = i * SLOTS + b
                        pe.wait_ge(hot_ready, n * 2 + (2 * NB + 2))
                        pe.wait_ge(sets_ready, n + 1)
                        pe.wait_ge(rank_free, n + 1)
                        for t in range(GB):
                            pe.wait_ge(seen_ready, n * GB + t + 1)
                            nc.tensor.matmul(live[:, :], one_lo[b][:, t, :], one_hi[b][:, t, :],
                                             start=False, stop=True, skip_group_check=True).then_inc(live_ready, 1)
                            nc.tensor.matmul(rank[b][:, t, :], one_loT[b][:, t, :], seen[t % 2][:, :], start=True, stop=False)
                            last = nc.tensor.matmul(rank[b][:, t, :], same[b][:, t, :], one_hi[b][:, t, :], start=False, stop=True)
                        last.then_inc(rank_ready, 1)
                        pe.sem_inc(sets_used, 1)


EB = 8
EG = -(-N_EDGES // (P * EB))
E_FULL = N_EDGES // (P * EB)
E_TAIL = (N_EDGES - E_FULL * P * EB) // EB
EQ = EB // 2


def edge_groups(ap, tail=False):
    n = E_FULL * P * EB
    if tail:
        return ap[n:N_EDGES].rearrange("(p t) -> p t", t=EB)
    return ap[0:n].rearrange("(g p t) -> p g t", p=P, t=EB)


def stage_edges(pg):
    nc, a = pg.nc, pg.a
    with ExitStack() as st:
        sb = lambda n, s, d=F32: st.enter_context(nc.sbuf_tensor("e_" + n, s, d))
        pb = lambda n, s, d=F32: st.enter_context(nc.psum_tensor("e_" + n, s, d))
        src_raw, src_i = sb("src_raw", [P, EG, EB], I32), sb("src_i", [P, EG, EB], I32)
        dst_i, tile_i = sb("dst_i", [P, EG, EB], I32), sb("tile_i", [P, EG, EB], I32)
        dst_f, tile_f = sb("dst_f", [P, EG, EB]), sb("tile_f", [P, EG, EB])
        ext, ext_n, ext_row = sb("ext", [P, 2, EG]), sb("ext_n", [EG, 2]), sb("ext_row", [1, 2, EG])
        more, more_sum, more_before = sb("more", [1, EG]), sb("more_sum", [1, EG]), sb("more_before", [1, EG])
        table = sb("table", [1, 3, EG], I32)
        nodes = sb("nodes", [P, NPAD])
        w_edge = sb("w_edge", [P, C])
        index = [sb(f"index{b}", [P, EB], I32) for b in range(2)]
        xg = [sb(f"xg{b}", [P, EB, C]) for b in range(2)]
        ea = [sb(f"ea{b}", [P, EB, E_DIM]) for b in range(2)]
        eaT = [sb(f"eaT{b}", [P, EB, P]) for b in range(2)]
        msg = [sb(f"msg{b}", [P, EB, C]) for b in range(2)]
        hot = [sb(f"hot{b}", [P, EB, P]) for b in range(2)]
        hotx = sb("hotx", [P, EB, P])
        tp = [pb(f"tp{h}", [P, EB // 2, P]) for h in range(2)]
        pre = [pb(f"pre{q}", [P, 2, C]) for q in range(EQ)]
        part = [pb(f"part{b}", [P, C]) for b in range(2)]
        idx_init, idx_loaded, w_ready = pg.sem("e_idx_init"), pg.sem("e_idx_loaded"), pg.sem("e_w_ready")
        steps, src_ready, dst_fixed = pg.sem("e_steps"), pg.sem("e_src_ready"), pg.sem("e_dst_fixed")
        ext_ready, extT_ready, row_in, row_out = (pg.sem(n) for n in ("e_ext_ready", "e_extT_ready", "e_row_in", "e_row_out"))
        table_ready, nodes_ready = pg.sem("e_table_ready"), pg.sem("e_nodes_ready")
        dstf_ready = pg.sem("e_dstf_ready")
        index_ready, index_used = pg.sem("e_index_ready"), pg.sem("e_turns")
        gathered = [pg.sem(f"e_gathered{b}") for b in range(2)]
        ea_ready = [pg.sem(f"e_ea_ready{b}") for b in range(2)]
        tp_ready, eaT_ready, pre_ready = pg.sem("e_tp_ready"), pg.sem("e_eaT_ready"), pg.sem("e_pre_ready")
        msg_added, relu_done = pg.sem("e_msg_added"), pg.sem("e_relu_done")
        hot_ready, summed, added = pg.sem("e_hot_ready"), pg.sem("e_summed"), pg.sem("e_added")
        hotx_ready, summedx, addedx = pg.sem("e_hotx_ready"), pg.sem("e_summedx"), pg.sem("e_addedx")
        with nc.Block() as block:
            @block.sync
            def _(sp):
                sp.dma_start(w_edge[:, :], a["w_edge"]).then_inc(w_ready, 16)
                sp.wait_ge(idx_init, 2)
                sp.dma_start(dst_i[:, 0:E_FULL, :], edge_groups(a["dst"])).then_inc(idx_loaded, 16)
                sp.dma_start(src_raw[:, 0:E_FULL, :], edge_groups(a["src"])).then_inc(idx_loaded, 16)
                sp.dma_start(dst_i[0:E_TAIL, E_FULL, :], edge_groups(a["dst"], True)).then_inc(idx_loaded, 16)
                sp.dma_start(src_raw[0:E_TAIL, E_FULL, :], edge_groups(a["src"], True)).then_inc(idx_loaded, 16)

                def load(i, b, tail):
                    sp.wait_ge(tp_ready, (i * 2 + b) * 2 + 2)
                    if tail:
                        rows = a["edge_attr"][E_FULL * P * EB:N_EDGES, :].rearrange("(p t) d -> p t d", t=EB)
                        sp.dma_start(ea[b][0:E_TAIL, :, :], rows).then_inc(ea_ready[b], 16)
                    else:
                        rows = a["edge_attr"][bass.ds((i * 2 + b) * (P * EB), P * EB), :].rearrange("(p t) d -> p t d", t=EB)
                        sp.dma_start(ea[b][:, :, :], rows).then_inc(ea_ready[b], 16)

                with sp.Fori(0, EG // 2 - 1) as i:
                    load(i, 0, False)
                    load(i, 1, False)
                load(EG // 2 - 1, 0, False)
                load(EG // 2 - 1, 1, True)

            @block.gpsimd
            def _(pool):
                nc.gpsimd.memset(dst_i[:, :, :], N_NODES - 1).then_inc(idx_init, 1)
                nc.gpsimd.memset(src_raw[:, :, :], 0).then_inc(idx_init, 1)
                nc.gpsimd.iota(nodes[:, :], pattern=[[1, NPAD]], base=0, channel_multiplier=0,
                               allow_small_or_imprecise_dtypes=True).then_inc(nodes_ready, 1)
                nc.gpsimd.memset(pg.agg[:, :, :], 0.0).then_inc(nodes_ready, 1)
                pool.wait_ge(dstf_ready, 1)
                nc.gpsimd.affine_select(out=dst_f[:, EG - 1, :], in_=dst_f[:, EG - 1, :], compare_op=ALU.is_ge,
                                        fill=-1.0, base=E_TAIL - 1, pattern=[[0, EB]], channel_multiplier=-1).then_inc(dst_fixed, 1)
                pool.wait_ge(src_ready, 1)
                with pool.Fori(0, EG // 2) as i:
                    for b in range(2):
                        g = i * 2 + b
                        pool.wait_ge(msg_added, g * EQ + EQ)
                        nc.gpsimd.tensor_copy(index[b][:, :], src_i[:, bass.ds(g, 1), :].rearrange("p o t -> p (o t)")).then_inc(index_ready, 1)
                        pool.wait_ge(index_ready, g + 1)
                        pool.sem_inc(index_used, 1)
                        for t in range(EB):
                            pool.indirect_dma_start(out=xg[b][:, t, :], out_offset=None, in_=pg.xb_d,
                                                    in_offset=bass.IndirectOffsetOnAxis(ap=index[b][:, t:t + 1], axis=0)
                                                    ).then_inc(gathered[b], 16)

            @block.scalar
            def _(act):
                act.sem_inc(eaT_ready, 2)
                with act.Fori(0, EG // 2) as i:
                    for b in range(2):
                        g = i * 2 + b
                        for h in range(2):
                            act.wait_ge(tp_ready, g * 2 + h + 5)
                            nc.scalar.activation(eaT[b][:, h * (EB // 2):(h + 1) * (EB // 2), :], tp[h][:, :, :],
                                                 ACT.Copy).then_inc(eaT_ready, 1)
                        act.wait_ge(msg_added, g * EQ + 3 * EQ)
                        nc.scalar.activation(msg[b][:, :, :], msg[b][:, :, :], ACT.Relu).then_inc(relu_done, 1)

            @block.vector
            def _(dve):
                ch = Chain(dve, steps)
                dve.sem_inc(msg_added, 2 * EQ)
                dve.sem_inc(added, 2)
                dve.wait_ge(idx_loaded, 64)
                ch.add(nc.vector.tensor_copy(dst_f[:, :, :], dst_i[:, :, :]))
                ch(nc.vector.tensor_scalar_min(src_i[:, :, :], src_raw[:, :, :], float(N_NODES - 1)))
                dve.sem_inc(src_ready, 1)
                dve.sem_inc(dstf_ready, 1)
                ch(nc.vector.tensor_single_scalar(tile_i[:, :, :], dst_i[:, :, :], 7, op=ALU.logical_shift_right))
                ch(nc.vector.tensor_scalar_min(tile_f[:, :, :], tile_i[:, :, :], float(NT - 1)))
                ch.add(nc.vector.tensor_reduce(out=ext[:, 0, :], in_=tile_f[:, :, :], axis=AX, op=ALU.min))
                ch(nc.vector.tensor_reduce(out=ext[:, 1, :], in_=tile_f[:, :, :], axis=AX, op=ALU.max))
                dve.sem_inc(ext_ready, 1)
                dve.wait_ge(extT_ready, 1)
                ch(nc.vector.tensor_reduce(out=ext_n[:, 0:1], in_=pre[0][0:EG, 0, 0:P], axis=AX, op=ALU.min))
                ch(nc.vector.tensor_reduce(out=ext_n[:, 1:2], in_=pre[0][0:EG, 1, 0:P], axis=AX, op=ALU.max))
                dve.sem_inc(row_in, 1)
                dve.wait_ge(row_out, 1)
                ch(nc.vector.tensor_copy(ext_row[:, :, :], pre[1][0:1, :, 0:EG]))
                ch(nc.vector.tensor_tensor(out=more[:, :], in0=ext_row[:, 1, :], in1=ext_row[:, 0, :], op=ALU.subtract))
                ch(nc.vector.tensor_tensor_scan(out=more_sum[:, :], data0=pg.ones_row[:, 0:EG], data1=more[:, :], initial=0.0,
                                                op0=ALU.mult, op1=ALU.add))
                ch(nc.vector.tensor_tensor(out=more_before[:, :], in0=more_sum[:, :], in1=more[:, :], op=ALU.subtract))
                ch.add(nc.vector.tensor_copy(table[:, 0, :], ext_row[:, 0, :]))
                ch.add(nc.vector.tensor_copy(table[:, 1, :], more[:, :]))
                ch(nc.vector.tensor_copy(table[:, 2, :], more_before[:, :]))
                dve.sem_inc(table_ready, 1)
                dve.wait_ge(dst_fixed, 1)
                dve.wait_ge(nodes_ready, 2)

                def one_hot(out, g, tile):
                    return nc.vector.tensor_tensor(
                        out=out[:, :, :], in0=nodes[:, bass.ds(tile * P, P)].unsqueeze(1).to_broadcast([P, EB, P]),
                        in1=dst_f[:, bass.ds(g, 1), :].rearrange("p o t -> p (o t)").unsqueeze(2).to_broadcast([P, EB, P]),
                        op=ALU.is_equal)

                def messages(i, b):
                    g = i * 2 + b
                    dve.wait_ge(summed, g + 1)
                    first = dve.value_load(table[0:1, 0, bass.ds(g, 1)], min_val=0, max_val=NT - 1)
                    one_hot(hot[b], g, first).then_inc(hot_ready, 1)
                    dve.wait_ge(gathered[b], i * (16 * EB) + 16 * EB)
                    for q in range(EQ):
                        dve.wait_ge(pre_ready, g * EQ + q + 1)
                        nc.vector.tensor_tensor(out=msg[b][:, 2 * q:2 * q + 2, :], in0=pre[q][:, :, :],
                                                in1=xg[b][:, 2 * q:2 * q + 2, :], op=ALU.add).then_inc(msg_added, 1)

                def add_part(out_tile, b):
                    acc = pg.agg[:, bass.ds(out_tile, 1), :].rearrange("p o c -> p (o c)")
                    return nc.vector.tensor_tensor(out=acc, in0=acc, in1=part[b][:, :], op=ALU.add)

                def add_group(g, b):
                    first = dve.value_load(table[0:1, 0, bass.ds(g, 1)], min_val=0, max_val=NT - 1)
                    further = dve.value_load(table[0:1, 1, bass.ds(g, 1)], min_val=0, max_val=NT - 1)
                    before = dve.value_load(table[0:1, 2, bass.ds(g, 1)], min_val=0, max_val=EG * NT)
                    dve.wait_ge(summed, g + 3)
                    add_part(first, b).then_inc(added, 1)
                    dve.wait_ge(added, g + 3)
                    dve.sem_inc(pg.turns, 1)
                    with dve.If(further > 0):
                        with dve.Fori(0, further) as j:
                            tile = nc.s_assert_within(first + 1 + j, 0, NT - 1, skip_runtime_bounds_check_because=
                                                      "the last tile of a group is at most NT - 1")
                            one_hot(hotx, g, tile).then_inc(hotx_ready, 1)
                            dve.wait_ge(summedx, before + j + 1)
                            add_part(tile, b).then_inc(addedx, 1)
                            dve.wait_ge(addedx, before + j + 1)

                messages(0, 0)
                messages(0, 1)
                add_group(0, 0)
                with dve.Fori(1, EG // 2) as i:
                    messages(i, 0)
                    add_group(i * 2 - 1, 1)
                    messages(i, 1)
                    add_group(i * 2, 0)
                add_group(EG - 1, 1)

            @block.tensor
            def _(pe):
                pe.sem_inc(tp_ready, 4)
                pe.sem_inc(summed, 2)
                pe.wait_ge(ext_ready, 1)
                for m in range(2):
                    last = nc.tensor.transpose(pre[0][0:EG, m, 0:P], ext[:, m, :], pg.ident[:, :])
                last.then_inc(extT_ready, 1)
                pe.wait_ge(row_in, 1)
                for m in range(2):
                    last = nc.tensor.transpose(pre[1][0:1, m, 0:EG], ext_n[:, m:m + 1], pg.ident[0:EG, 0:EG])
                last.then_inc(row_out, 1)
                pe.wait_ge(table_ready, 1)
                pe.wait_ge(w_ready, 16)

                def project(i, b):
                    g = i * 2 + b
                    pe.wait_ge(ea_ready[b], i * 16 + 16)
                    for h in range(2):
                        pe.wait_ge(eaT_ready, g * 2 + h + 1)
                        for t in range(EB // 2):
                            last = nc.tensor.transpose(tp[h][:, t, :], ea[b][:, h * (EB // 2) + t, :], pg.ident[:, :])
                        last.then_inc(tp_ready, 1)
                    for q in range(EQ):
                        if q % 2 == 0:
                            pe.wait_ge(eaT_ready, g * 2 + q // 2 + 3)
                        pe.wait_ge(msg_added, g * EQ + q + EQ + 1)
                        for t in range(2):
                            last = nc.tensor.matmul(pre[q][:, t, :], eaT[b][:, 2 * q + t, :], w_edge[:, :], start=True, stop=True)
                        last.then_inc(pre_ready, 1)

                def products(b, one_hots):
                    for t in range(EB):
                        last = nc.tensor.matmul(part[b][:, :], one_hots[:, t, :], msg[b][:, t, :], start=(t == 0), stop=(t == EB - 1))
                    return last

                def sum_group(g, b):
                    further = pe.value_load(table[0:1, 1, bass.ds(g, 1)], min_val=0, max_val=NT - 1)
                    before = pe.value_load(table[0:1, 2, bass.ds(g, 1)], min_val=0, max_val=EG * NT)
                    pe.wait_ge(hot_ready, g + 1)
                    pe.wait_ge(relu_done, g + 1)
                    pe.wait_ge(added, g + 1)
                    products(b, hot[b]).then_inc(summed, 1)
                    with pe.If(further > 0):
                        with pe.Fori(0, further) as j:
                            pe.wait_ge(hotx_ready, before + j + 1)
                            products(b, hotx).then_inc(summedx, 1)

                project(0, 0)
                project(0, 1)
                sum_group(0, 0)
                with pe.Fori(1, EG // 2) as i:
                    project(i, 0)
                    sum_group(i * 2 - 1, 1)
                    project(i, 1)
                    sum_group(i * 2, 0)
                sum_group(EG - 1, 1)


def row_of(ap, n):
    return ap.rearrange("(o c) -> o c", o=1).to_broadcast([P, n])


def col_of(ap):
    return ap.rearrange("(h p) -> p h", p=P)


def weights_of(ap):
    return ap.rearrange("(h p) n -> p h n", p=P)


def feature_major(nc, pe, out, wT, xT, out_ready, out_free, ready, free):
    n = 0
    for m in range(KC):
        for h in range(2):
            pe.wait_ge(out_free, free + n + 1)
            for c in range(KC):
                last = nc.tensor.matmul(out[n % 2][:, :], wT[:, c, m * P:(m + 1) * P], xT[:, c, h * HN:(h + 1) * HN],
                                        start=(c == 0), stop=(c == KC - 1))
            last.then_inc(out_ready, 1)
            n += 1


def stage_mix(pg):
    nc, a = pg.nc, pg.a
    with ExitStack() as st:
        sb = lambda n, s, d=F32: st.enter_context(nc.sbuf_tensor("m_" + n, s, d))
        pb = lambda n, s, d=F32: st.enter_context(nc.psum_tensor("m_" + n, s, d))
        wq, w1, w2 = (sb(n, [P, KC, C]) for n in ("wq", "w1", "w2"))
        b1 = sb("b1", [P, KC])
        b2, g1, be1, g2, be2 = (sb(n, [P, C]) for n in ("b2", "g1", "be1", "g2", "be2"))
        xT, xn = sb("xT", [P, KC, SN]), sb("xn", [P, ST, C])
        qneg, qexp, qT = (sb(n, [P, KC, SN]) for n in ("qneg", "qexp", "qT"))
        den, z = sb("den", [P, KC, HH]), sb("z", [P, KC, HH])
        t, x1, x1T, hT, y = sb("t", [P, ST, C]), sb("x1", [P, ST, C]), sb("x1T", [P, KC, SN]), sb("hT", [P, KC, SN]), sb("y", [P, ST, C])
        out = sb("out", [P, ST, C])
        stats, mv, std, rstd = sb("stats", [P, ST, 6]), sb("mv", [P, ST, 2]), sb("std", [P, ST]), sb("rstd", [P, ST])
        fm = [pb(f"fm{i}", [P, HN]) for i in range(2)]
        att = [pb(f"att{i}", [P, KC, P + HH]) for i in range(2)]
        tp = [pb(f"tp{i}", [P, 512]) for i in range(2)]
        yp = [pb(f"yp{i}", [P, C]) for i in range(2)]
        w_ready, loaded, in_free = pg.sem("m_w_ready"), pg.sem("m_loaded"), pg.sem("m_in_free")
        xn_free, xT_free = pg.sem("m_xn_free"), pg.sem("m_xT_free")
        steps, fm_ready, fm_free = pg.sem("m_steps"), pg.sem("m_fm_ready"), pg.sem("m_fm_free")
        qneg_ready, qexp_ready = pg.sem("m_qneg_ready"), pg.sem("m_qexp_ready")
        qT_ready, att_ready, att_free = pg.sem("m_qT_ready"), pg.sem("m_att_ready"), pg.sem("m_att_free")
        var_ready, std_ready, x1_ready = pg.sem("m_var_ready"), pg.sem("m_std_ready"), pg.sem("m_x1_ready")
        tp_ready, tp_free, x1T_ready = pg.sem("m_tp_ready"), pg.sem("m_tp_free"), pg.sem("m_x1T_ready")
        hT_ready, yp_ready, yp_free = pg.sem("m_hT_ready"), pg.sem("m_yp_ready"), pg.sem("m_yp_free")
        out_ready, out_stored, out_free = pg.sem("m_out_ready"), pg.sem("m_out_stored"), pg.sem("m_out_free")
        with nc.Block() as block:
            @block.sync
            def _(sp):
                sp.dma_start(wq[:, :, :], weights_of(a["mix_wqkvT"][:, 0:C])).then_inc(w_ready, 16)
                sp.dma_start(w1[:, :, :], weights_of(a["mix_w1T"])).then_inc(w_ready, 16)
                sp.dma_start(w2[:, :, :], weights_of(a["mix_w2T"])).then_inc(w_ready, 16)
                with nc.allow_non_contiguous_dma(reason="two vectors of 256"):
                    sp.dma_start(b1[:, :], col_of(a["mix_b1"])).then_inc(w_ready, 16)
                for d, v in ((b2, "mix_b2"), (g1, "mix_g1"), (be1, "mix_be1"), (g2, "mix_g2"), (be2, "mix_be2")):
                    sp.dma_start(d[:, :], row_of(a[v], C)).then_inc(w_ready, 16)

                def load(i):
                    sp.wait_ge(xT_free, i + 1)
                    sp.dma_start(xT[:, :, :], feat_cols(pg.xT_d, i)).then_inc(loaded, 16)
                    sp.wait_ge(xn_free, i + 1)
                    sp.dma_start(xn[:, :, :], node_rows(pg.xn_d, i)).then_inc(loaded, 16)

                def store(i):
                    sp.wait_ge(out_ready, i + 1)
                    sp.dma_start(node_rows(pg.mix_d, i), out[:, :, :]).then_inc(out_stored, 16)
                    sp.wait_ge(out_stored, i * 16 + 16)
                    sp.sem_inc(out_free, 1)

                sp.sem_inc(out_free, 1)
                load(0)
                with sp.Fori(0, STEPS - 1) as i:
                    load(i + 1)
                    store(i)
                store(STEPS - 1)

            @block.gpsimd
            def _(pool):
                scatter_batches(pg, pool, "m", SORT_BATCHES, MIX_BATCHES)

            @block.tensor
            def _(pe):
                pe.sem_inc(xT_free, 1)
                pe.wait_ge(w_ready, 9 * 16)
                with pe.Fori(0, STEPS) as i:
                    pe.wait_ge(loaded, i * 32 + 32)
                    feature_major(nc, pe, fm, wq, xT, fm_ready, fm_free, i * 8, i * 8)
                    pe.wait_ge(qT_ready, i * 4 + 4)
                    pe.sem_inc(xT_free, 1)
                    for j in range(ST):
                        pe.wait_ge(att_free, i * ST + j + 1)
                        for h in range(KC):
                            last = nc.tensor.matmul(att[j % 2][:, h, :], qT[:, h, j * P:(j + 1) * P], pg.kv_blocks[:, h, :],
                                                    start=True, stop=True)
                        last.then_inc(att_ready, 1)
                    pe.wait_ge(x1_ready, i + 1)
                    transpose_rows(nc, pe, x1, pg.ident, tp, tp_ready, tp_free, i * NU)
                    pe.wait_ge(x1T_ready, i + 1)
                    feature_major(nc, pe, fm, w1, x1T, fm_ready, fm_free, i * 8 + 4, i * 8 + 4)
                    pe.wait_ge(hT_ready, i * 4 + 4)
                    for j in range(ST):
                        pe.wait_ge(yp_free, i * ST + j + 1)
                        for c in range(KC):
                            last = nc.tensor.matmul(yp[j % 2][:, :], hT[:, c, j * P:(j + 1) * P], w2[:, c, :],
                                                    start=(c == 0), stop=(c == KC - 1))
                        last.then_inc(yp_ready, 1)

            @block.scalar
            def _(act):
                act.sem_inc(tp_free, 2)
                act.wait_ge(w_ready, 9 * 16)
                with act.Fori(0, STEPS) as i:
                    for n in range(4):
                        m, h = n // 2, n % 2
                        act.wait_ge(qneg_ready, i * 4 + n + 1)
                        nc.scalar.activation(qexp[:, m, h * HN:(h + 1) * HN], qneg[:, m, h * HN:(h + 1) * HN],
                                             ACT.Exp).then_inc(qexp_ready, 1)
                    act.wait_ge(var_ready, i * 2 + 1)
                    nc.scalar.activation(std[:, :], rstd[:, :], ACT.Sqrt).then_inc(std_ready, 1)
                    copy_blocks(nc, act, x1T, tp, tp_ready, tp_free, x1T_ready, i * NU)
                    for n in range(4):
                        m, h = n // 2, n % 2
                        act.wait_ge(fm_ready, i * 8 + 4 + n + 1)
                        nc.scalar.activation(hT[:, m, h * HN:(h + 1) * HN], fm[n % 2][:, :], ACT.Gelu,
                                             bias=b1[:, m:m + 1]).then_inc(hT_ready, 1)
                        act.wait_ge(hT_ready, i * 4 + n + 1)
                        act.sem_inc(fm_free, 1)
                    act.wait_ge(var_ready, i * 2 + 2)
                    nc.scalar.activation(std[:, :], rstd[:, :], ACT.Sqrt).then_inc(std_ready, 1)

            @block.vector
            def _(dve):
                dve.sem_inc(xn_free, 1)
                dve.sem_inc(fm_free, 2)
                dve.sem_inc(att_free, 2)
                dve.sem_inc(yp_free, 2)
                dve.wait_ge(w_ready, 9 * 16)
                K = 4 * ST + 2 * (NORM_STEPS + ST + 1) + 2 + ST

                def affine(ch, rows, gain, shift):
                    ch(nc.vector.tensor_tensor(out=rows[:, :, :], in0=rows[:, :, :],
                                               in1=gain[:, :].unsqueeze(1).to_broadcast([P, ST, C]), op=ALU.mult))
                    return nc.vector.tensor_tensor(out=rows[:, :, :], in0=rows[:, :, :],
                                                   in1=shift[:, :].unsqueeze(1).to_broadcast([P, ST, C]), op=ALU.add)

                with dve.Fori(0, STEPS) as i:
                    ch = Chain(dve, steps, i * K)
                    for n in range(4):
                        m, h = n // 2, n % 2
                        dve.wait_ge(fm_ready, i * 8 + n + 1)
                        nc.vector.tensor_scalar_min(qneg[:, m, h * HN:(h + 1) * HN], fm[n % 2][:, :], 0.0).then_inc(qneg_ready, 1)
                        dve.wait_ge(qexp_ready, i * 4 + n + 1)
                        nc.vector.scalar_tensor_tensor(out=qT[:, m, h * HN:(h + 1) * HN], in0=fm[n % 2][:, :], scalar=0.0,
                                                       in1=qexp[:, m, h * HN:(h + 1) * HN], op0=ALU.max, op1=ALU.add
                                                       ).then_inc(qT_ready, 1)
                        dve.wait_ge(qT_ready, i * 4 + n + 1)
                        dve.sem_inc(fm_free, 1)
                    for j in range(ST):
                        dve.wait_ge(att_ready, i * ST + j + 1)
                        ch(nc.vector.tensor_scalar_add(den[:, :, :], att[j % 2][:, :, P:P + HH], 1e-6))
                        ch(nc.vector.reciprocal(z[:, :, :], den[:, :, :]))
                        for h in range(KC):
                            nc.vector.tensor_tensor(out=t[:, j, h * P:(h + 1) * P].rearrange("p (g d) -> p g d", g=HH),
                                                    in0=att[j % 2][:, h, 0:P].rearrange("p (g d) -> p g d", g=HH),
                                                    in1=z[:, h, :].unsqueeze(2).to_broadcast([P, HH, HD]),
                                                    op=ALU.mult).then_inc(steps, 1)
                            ch.n += 1
                        ch.wait()
                        dve.sem_inc(att_free, 1)
                    dve.wait_ge(loaded, i * 32 + 32)
                    ch(nc.vector.tensor_tensor(out=t[:, :, :], in0=t[:, :, :], in1=xn[:, :, :], op=ALU.add))
                    dve.sem_inc(xn_free, 1)
                    norm_statistics(nc, dve, ch, pg.turns, t, stats, mv, rstd, var_ready, std, std_ready, i * 2 + 1)
                    normalise(nc, ch, x1, t, mv, rstd)
                    affine(ch, x1, g1, be1).then_inc(x1_ready, 1)
                    dve.wait_ge(x1_ready, i + 1)
                    ch(nc.vector.tensor_tensor(out=t[:, :, :], in0=x1[:, :, :],
                                               in1=b2[:, :].unsqueeze(1).to_broadcast([P, ST, C]), op=ALU.add))
                    for j in range(ST):
                        dve.wait_ge(yp_ready, i * ST + j + 1)
                        ch(nc.vector.tensor_tensor(out=y[:, j, :], in0=t[:, j, :], in1=yp[j % 2][:, :], op=ALU.add))
                        dve.sem_inc(yp_free, 1)
                    norm_statistics(nc, dve, ch, pg.turns, y, stats, mv, rstd, var_ready, std, std_ready, i * 2 + 2)
                    dve.wait_ge(out_free, i + 1)
                    normalise(nc, ch, out, y, mv, rstd)
                    affine(ch, out, g2, be2).then_inc(out_ready, 1)
                    dve.wait_ge(out_ready, i + 1)
                    assert ch.n == K



def stage_gnn(pg):
    nc, a = pg.nc, pg.a
    pg.table_d = pg.dram("table_d", [NPAD, ROW]).ap()
    with ExitStack() as st:
        sb = lambda n, s, d=F32: st.enter_context(nc.sbuf_tensor("g_" + n, s, d))
        pb = lambda n, s, d=F32: st.enter_context(nc.psum_tensor("g_" + n, s, d))
        h2T = sb("h2T", [P, KC, NPAD])
        w1, w2 = sb("w1", [P, KC, C]), sb("w2", [P, KC, C])
        b1, b2, gamma, beta = (sb(n, [P, KC]) for n in ("b1", "b2", "gamma", "beta"))
        gain = sb("gain", [P, 1])
        scale, shift = sb("scale", [P, KC]), sb("shift", [P, KC])
        bstats, bmv, bvar, bstd = sb("bstats", [P, KC, 2 * STEPS, 6]), sb("bmv", [P, KC, 2]), sb("bvar", [P, KC]), sb("bstd", [P, KC])
        rows, h0 = sb("rows", [P, ST, C]), sb("h0", [P, ST, C])
        xT, hT = sb("xT", [P, KC, SN]), sb("hT", [P, KC, SN])
        fm = [pb(f"fm{i}", [P, HN]) for i in range(2)]
        tp = [pb(f"tp{i}", [P, 512]) for i in range(2)]
        tb = [pb(f"tb{i}", [P, 512]) for i in range(2)]
        gp = pb("gp", [P, ST, GF])
        w_ready, loaded, rows_free = pg.sem("g_w_ready"), pg.sem("g_loaded"), pg.sem("g_rows_free")
        steps, h0_ready = pg.sem("g_steps"), pg.sem("g_h0_ready")
        tp_ready, tp_free, xT_ready = pg.sem("g_tp_ready"), pg.sem("g_tp_free"), pg.sem("g_xT_ready")
        fm_ready, fm_free, hT_ready, h2_ready = pg.sem("g_fm_ready"), pg.sem("g_fm_free"), pg.sem("g_hT_ready"), pg.sem("g_h2_ready")
        loops_out = pg.sem("g_loops_out")
        with nc.Block() as block:
            @block.gpsimd
            def _(pool):
                for t in range(NT):
                    pool.indirect_dma_start(out=pg.sorted_d, out_offset=bass.IndirectOffsetOnAxis(ap=pg.first[:, t:t + 1], axis=0),
                                            in_=pg.node_id[:, t:t + 1], in_offset=None).then_inc(loops_out, 16)
                pool.wait_ge(loops_out, 16 * NT)

            @block.sync
            def _(sp):
                sp.dma_start(w1[:, :, :], weights_of(a["gnn_w1"])).then_inc(w_ready, 16)
                sp.dma_start(w2[:, :, :], weights_of(a["gnn_w2"])).then_inc(w_ready, 16)
                with nc.allow_non_contiguous_dma(reason="vectors of 256"):
                    for d, v in ((b1, "gnn_b1"), (b2, "gnn_b2"), (gamma, "gnn_gamma"), (beta, "gnn_beta")):
                        sp.dma_start(d[:, :], col_of(a[v])).then_inc(w_ready, 16)
                sp.dma_start(gain[:, :], a["gnn_eps"].to_broadcast([P, 1])).then_inc(w_ready, 16)
                with sp.Fori(0, STEPS) as i:
                    sp.wait_ge(rows_free, i + 1)
                    sp.dma_start(rows[:, :, :], node_rows(pg.xn_d, i)).then_inc(loaded, 16)

            @block.vector
            def _(dve):
                dve.sem_inc(rows_free, 1)
                dve.wait_ge(w_ready, 7 * 16)
                ch = Chain(dve, steps)
                ch(nc.vector.tensor_scalar_add(gain[:, :], gain[:, :], 1.0))
                with dve.Fori(0, STEPS) as i:
                    dve.wait_ge(loaded, i * 16 + 16)
                    dve.wait_ge(tp_ready, i * NU + 1)
                    nc.vector.scalar_tensor_tensor(out=h0[:, :, :], in0=rows[:, :, :], scalar=gain[:, 0:1],
                                                   in1=pg.agg[:, bass.ds(i * ST, ST), :], op0=ALU.mult, op1=ALU.add
                                                   ).then_inc(h0_ready, 1)
                    dve.wait_ge(h0_ready, i + 1)
                    dve.sem_inc(rows_free, 1)
                dve.wait_ge(h2_ready, 4 * STEPS)
                for m in range(KC):
                    for k in range(2 * STEPS):
                        ch.add(nc.vector.bn_stats(out=bstats[:, m, k, :], in_=h2T[:, m, k * HN:min((k + 1) * HN, N_NODES)]))
                ch.wait()
                for m in range(KC):
                    ch.add(nc.vector.bn_aggr(out=bmv[:, m, :], in_=bstats[:, m, :, :].rearrange("p k s -> p (k s)")))
                ch.wait()
                ch(nc.vector.tensor_scalar_add(bvar[:, :], bmv[:, :, 1], 1e-5))
                dve.sem_inc(h0_ready, 1)
                dve.wait_ge(h2_ready, 4 * STEPS + 1)
                ch(nc.vector.reciprocal(bvar[:, :], bstd[:, :]))
                ch(nc.vector.tensor_tensor(out=scale[:, :], in0=bvar[:, :], in1=gamma[:, :], op=ALU.mult))
                ch(nc.vector.tensor_tensor(out=shift[:, :], in0=bmv[:, :, 0], in1=scale[:, :], op=ALU.mult))
                ch(nc.vector.tensor_tensor(out=shift[:, :], in0=beta[:, :], in1=shift[:, :], op=ALU.subtract))

            @block.scalar
            def _(act):
                act.sem_inc(tp_free, 2)
                act.sem_inc(fm_free, 2)
                act.wait_ge(w_ready, 7 * 16)
                with act.Fori(0, STEPS) as i:
                    copy_blocks(nc, act, xT, tp, tp_ready, tp_free, xT_ready, i * NU, tp_start=1)
                    for n in range(4):
                        m, h = n // 2, n % 2
                        act.wait_ge(fm_ready, i * 8 + n + 1)
                        nc.scalar.activation(hT[:, m, h * HN:(h + 1) * HN], fm[n % 2][:, :], ACT.Relu,
                                             bias=b1[:, m:m + 1]).then_inc(fm_free, 1)
                    act.wait_ge(fm_free, i * 8 + 6)
                    act.sem_inc(hT_ready, 1)
                    for n in range(4):
                        m, h = n // 2, n % 2
                        act.wait_ge(fm_ready, i * 8 + n + 5)
                        nc.scalar.activation(h2T[:, m, bass.ds(i * SN + h * HN, HN)], fm[n % 2][:, :], ACT.Identity,
                                             bias=b2[:, m:m + 1]).then_inc(fm_free, 1)
                    act.wait_ge(fm_free, i * 8 + 10)
                    act.sem_inc(h2_ready, 4)
                act.wait_ge(h0_ready, STEPS + 1)
                nc.scalar.activation(bstd[:, :], bvar[:, :], ACT.Sqrt).then_inc(h2_ready, 1)

            @block.tensor
            def _(pe):
                pe.sem_inc(tp_ready, 1)
                pe.wait_ge(w_ready, 7 * 16)
                with pe.Fori(0, STEPS) as i:
                    pe.wait_ge(h0_ready, i + 1)
                    transpose_rows(nc, pe, h0, pg.ident, tp, tp_ready, tp_free, i * NU)
                    pe.wait_ge(xT_ready, i + 1)
                    feature_major(nc, pe, fm, w1, xT, fm_ready, fm_free, i * 8, i * 8)
                    pe.wait_ge(hT_ready, i + 1)
                    feature_major(nc, pe, fm, w2, hT, fm_ready, fm_free, i * 8 + 4, i * 8 + 4)

        x_in, mix, x2 = sb("x_in", [P, ST, C]), sb("mix", [P, ST, C]), sb("x2", [P, ST, C])
        x3, x3T, rT = sb("x3", [P, ST, C]), xT, hT
        stats, mv, std, rstd = sb("stats", [P, ST, 6]), sb("mv", [P, ST, 2]), sb("std", [P, ST]), sb("rstd", [P, ST])
        wg = sb("wg", [P, KC, GF])
        att_s, att_d = sb("att_s", [P, GF]), sb("att_d", [P, GF])
        trow, prod = sb("trow", [P, ST, ROW]), sb("prod", [P, ST, GF])
        w3_ready, in_ready, x_in_free = pg.sem("j_w_ready"), pg.sem("j_in_ready"), pg.sem("j_x_in_free")
        jsteps, rT_ready, rT_used = pg.sem("j_steps"), pg.sem("j_rT_ready"), pg.sem("j_rT_used")
        bp_ready, bp_free = pg.sem("j_bp_ready"), pg.sem("j_bp_free")
        var_ready, std_ready, x2_ready, x3_ready = pg.sem("j_var_ready"), pg.sem("j_std_ready"), pg.sem("j_x2_ready"), pg.sem("j_x3_ready")
        out_free, stored = pg.sem("j_out_free"), pg.sem("j_stored")
        tq_ready, tq_free, x3T_ready = pg.sem("j_tq_ready"), pg.sem("j_tq_free"), pg.sem("j_x3T_ready")
        gp_ready, trow_ready = pg.sem("j_gp_ready"), pg.sem("j_trow_ready")
        with nc.Block() as block:
            @block.sync
            def _(sp):
                sp.dma_start(wg[:, :, :], weights_of(a["w_gat"])).then_inc(w3_ready, 16)
                sp.dma_start(att_s[:, :], row_of(a["att_src"].rearrange("h e -> (h e)"), GF)).then_inc(w3_ready, 16)
                sp.dma_start(att_d[:, :], row_of(a["att_dst"].rearrange("h e -> (h e)"), GF)).then_inc(w3_ready, 16)
                with sp.Fori(0, STEPS) as i:
                    sp.wait_ge(x_in_free, i + 1)
                    sp.dma_start(x_in[:, :, :], node_rows(pg.xpad, i)).then_inc(in_ready, 16)
                    sp.dma_start(mix[:, :, :], node_rows(pg.mix_d, i)).then_inc(in_ready, 16)

            @block.gpsimd
            def _(pool):
                pool.sem_inc(out_free, 1)
                with pool.Fori(0, STEPS) as i:
                    pool.wait_ge(x2_ready, i + 1)
                    pool.dma_start(node_rows(pg.x2_d, i), x2[:, :, :]).then_inc(stored, 16)
                    pool.wait_ge(x3T_ready, i + 1)
                    pool.dma_start(feat_cols(pg.x3T_d, i), x3T[:, :, :]).then_inc(stored, 16)
                    pool.wait_ge(trow_ready, i + 1)
                    pool.dma_start(node_rows(pg.table_d, i), trow[:, :, :]).then_inc(stored, 16)
                    pool.wait_ge(stored, i * 48 + 48)
                    pool.sem_inc(out_free, 1)

            @block.scalar
            def _(act):
                act.sem_inc(tq_free, 2)
                act.sem_inc(bp_free, 2)
                with act.Fori(0, STEPS) as i:
                    act.wait_ge(rT_used, i + 1)
                    for m in range(KC):
                        nc.scalar.activation(rT[:, m, :], h2T[:, m, bass.ds(i * SN, SN)], ACT.Relu,
                                             bias=shift[:, m:m + 1], scale=scale[:, m:m + 1]).then_inc(rT_ready, 1)
                    act.wait_ge(var_ready, i + 1)
                    nc.scalar.activation(std[:, :], rstd[:, :], ACT.Sqrt).then_inc(std_ready, 1)
                    act.wait_ge(out_free, i + 1)
                    copy_blocks(nc, act, x3T, tp, tq_ready, tq_free, x3T_ready, i * NU)

            @block.tensor
            def _(pe):
                pe.sem_inc(rT_used, 1)
                pe.wait_ge(w3_ready, 48)
                with pe.Fori(0, STEPS) as i:
                    pe.wait_ge(rT_ready, i * 2 + 2)
                    for u, (q0, nq) in enumerate(UNITS):
                        pe.wait_ge(bp_free, i * NU + u + 1)
                        for q in range(q0, q0 + nq):
                            last = nc.tensor.transpose(tb[u % 2][:, (q - q0) * P:(q - q0 + 1) * P],
                                                       rT[:, q % KC, (q // KC) * P:(q // KC + 1) * P], pg.ident[:, :])
                        last.then_inc(bp_ready, 1)
                    pe.wait_ge(x2_ready, i + 1)
                    pe.sem_inc(rT_used, 1)
                    pe.wait_ge(x3_ready, i + 1)
                    transpose_rows(nc, pe, x3, pg.ident, tp, tq_ready, tq_free, i * NU)
                    pe.wait_ge(x3T_ready, i + 1)
                    pe.wait_ge(out_free, i + 1)
                    for j in range(ST):
                        for c in range(KC):
                            last = nc.tensor.matmul(gp[:, j, :], x3T[:, c, j * P:(j + 1) * P], wg[:, c, :],
                                                    start=(c == 0), stop=(c == KC - 1))
                    last.then_inc(gp_ready, 1)

            @block.vector
            def _(dve):
                dve.sem_inc(x_in_free, 1)
                dve.wait_ge(w3_ready, 48)
                ch = Chain(dve, jsteps)
                ch(nc.vector.memset(pg.starts[:, :, :], 0.0))
                ch(nc.vector.memset(pg.starts[:, :, 0:1], 1.0))
                K = NU + 1 + NORM_STEPS + ST + 4
                with dve.Fori(0, STEPS) as i:
                    ch = Chain(dve, jsteps, i * K + 2)
                    dve.wait_ge(in_ready, i * 32 + 32)
                    dve.wait_ge(out_free, i + 1)
                    x2f = x2[:, :, :].rearrange("p j c -> p (j c)")
                    xf = x_in[:, :, :].rearrange("p j c -> p (j c)")
                    for u, (q0, nq) in enumerate(UNITS):
                        dve.wait_ge(bp_ready, i * NU + u + 1)
                        ch(nc.vector.tensor_tensor(out=x2f[:, q0 * P:(q0 + nq) * P], in0=xf[:, q0 * P:(q0 + nq) * P],
                                                   in1=tb[u % 2][:, 0:nq * P], op=ALU.add))
                        dve.sem_inc(bp_free, 1)
                    ch(nc.vector.tensor_tensor(out=x2[:, :, :], in0=x2[:, :, :], in1=mix[:, :, :], op=ALU.add))
                    dve.sem_inc(x2_ready, 1)
                    dve.sem_inc(x_in_free, 1)
                    norm_statistics(nc, dve, ch, pg.turns, x2, stats, mv, rstd, var_ready, std, std_ready, i + 1)
                    normalise(nc, ch, x3, x2, mv, rstd)
                    dve.sem_inc(x3_ready, 1)
                    dve.wait_ge(gp_ready, i + 1)
                    ch(nc.vector.tensor_copy(trow[:, :, 0:GF], gp[:, :, :]))
                    for att, out in ((att_s, trow[:, :, GF:ROW]), (att_d, pg.starts[:, bass.ds(i * ST, ST), 1:1 + HEADS])):
                        if att is att_d:
                            ch.wait()
                        ch(nc.vector.tensor_tensor(out=prod[:, :, :], in0=trow[:, :, 0:GF],
                                                   in1=att[:, :].unsqueeze(1).to_broadcast([P, ST, GF]), op=ALU.mult))
                        red = nc.vector.tensor_reduce(out=out, in_=prod[:, :, :].rearrange("p j (h e) -> p j h e", h=HEADS),
                                                      axis=AX, op=ALU.add)
                        if att is att_s:
                            ch(red)
                        else:
                            red.then_inc(trow_ready, 1)
                            dve.wait_ge(trow_ready, i + 1)
                    assert ch.n == K, ch.n


GC = 29
assert RUN % GC == 0 and (RUN // GC) % 2 == 1


def stage_attend(pg):
    nc, a = pg.nc, pg.a
    starts_d = pg.dram("starts_d", [P * RUN, 8]).ap()
    sums_d = pg.dram("sums_d", [P * RUN, ROW]).ap()
    with ExitStack() as st:
        sb = lambda n, s, d=F32: st.enter_context(nc.sbuf_tensor("a_" + n, s, d))
        pb = lambda n, s, d=F32: st.enter_context(nc.psum_tensor("a_" + n, s, d))
        order = sb("order", [P, RUN], I32)
        rows = sb("rows", [P, RUN, ROW])
        index = [sb(f"index{b}", [P, GC], I32) for b in range(2)]
        got = [sb(f"got{b}", [P, GC, ROW]) for b in range(2)]
        est = ExitStack()
        zeroed, scattered, loaded = pg.sem("a_zeroed"), pg.sem("a_scattered"), pg.sem("a_loaded")
        index_ready = pg.sem("a_index_ready")
        copied = [pg.sem(f"a_copied{b}") for b in range(2)]
        gathered = [pg.sem(f"a_gathered{b}") for b in range(2)]
        NG = RUN // GC
        with nc.Block() as block:
            @block.sync
            def _(sp):
                sp.dma_start(order[:, :], pg.sorted_d.rearrange("(p c) o -> p (c o)", p=P)).then_inc(loaded, 16)
                z = pg.zeros[:, 0:296].unsqueeze(1).to_broadcast([P, 29, 296])
                sp.dma_start(starts_d.rearrange("(p c) k -> p (c k)", p=P).rearrange("p (r z) -> p r z", z=296), z).then_inc(zeroed, 16)

                def keep(i, b):
                    sp.wait_ge(gathered[b], i * (16 * GC) + 16 * GC)
                    sp.dma_start(rows[:, bass.ds((i * 2 + b) * GC, GC), :], got[b][:, :, :]).then_inc(copied[b], 16)

                with sp.Fori(0, NG // 2) as i:
                    keep(i, 0)
                    keep(i, 1)
                keep(NG // 2, 0)
                for b in range(2):
                    sp.wait_ge(copied[b], 16 * (NG // 2 + 1 - b))

            @block.gpsimd
            def _(pool):
                pool.wait_ge(zeroed, 16)
                for t in range(NT):
                    pool.indirect_dma_start(out=starts_d, out_offset=bass.IndirectOffsetOnAxis(ap=pg.first[:, t:t + 1], axis=0),
                                            in_=pg.starts[:, t, :], in_offset=None).then_inc(scattered, 16)
                pool.wait_ge(loaded, 16)

                def gather(i, b, first=False):
                    n = i * 2 + b
                    if not first:
                        pool.wait_ge(copied[b], i * 16)
                    nc.gpsimd.tensor_copy(index[b][:, :], order[:, bass.ds(n * GC, GC)]).then_inc(index_ready, 1)
                    pool.wait_ge(index_ready, n + 1)
                    pool.sem_inc(pg.turns, 1)
                    for t in range(GC):
                        pool.indirect_dma_start(out=got[b][:, t, :], out_offset=None, in_=pg.table_d,
                                                in_offset=bass.IndirectOffsetOnAxis(ap=index[b][:, t:t + 1], axis=0)
                                                ).then_inc(gathered[b], 16)

                gather(0, 0, True)
                gather(0, 1, True)
                with pool.Fori(1, NG // 2) as i:
                    gather(i, 0)
                    gather(i, 1)
                gather(NG // 2, 0)
                pool.wait_ge(scattered, 16 * NT)

            experts(pg, block, est)

        est.close()
        heads = sb("heads", [P, RUN, 8])
        keep, fresh, junk = sb("keep", [P, RUN]), sb("fresh", [P, RUN]), sb("junk", [P, RUN])
        top, decay = sb("top", [P, RUN, HEADS]), sb("decay", [P, RUN, HEADS])
        give = sb("give", [P, 2, ROW])
        giveT = sb("giveT", [ROW, 2, P])
        carryT = sb("carryT", [ROW, P + 1])
        carry = sb("carry", [P, ROW])
        whole = sb("whole", [P, 1])
        tp = pb("tp", [P, 2, P])
        cp = pb("cp", [P, ROW])
        steps, give_ready, giveT_ready = pg.sem("a_steps"), pg.sem("a_give_ready"), pg.sem("a_giveT_ready")
        carryT_ready, carry_ready = pg.sem("a_carryT_ready"), pg.sem("a_carry_ready")
        exp_in, exp_out = pg.sem("a_exp_in"), pg.sem("a_exp_out")
        heads_ready = pg.sem("a_heads_ready")
        sums_ready, sums_out, fetched = pg.sem("a_sums_ready"), pg.sem("a_sums_out"), pg.sem("a_fetched")
        CARRIES = (HEADS, HEADS, ROW)
        with nc.Block() as block:
            @block.tensor
            def _(pe):
                for n, w in enumerate(CARRIES):
                    pe.wait_ge(give_ready, n + 1)
                    for m in range(2):
                        last = nc.tensor.transpose(tp[0:w, m, :], give[:, m, 0:w], pg.ident[:, :])
                    last.then_inc(giveT_ready, 1)
                    pe.wait_ge(carryT_ready, n + 1)
                    nc.tensor.transpose(cp[:, 0:w], carryT[0:w, 0:P], pg.ident[0:w, 0:w]).then_inc(carry_ready, 1)

            @block.scalar
            def _(act):
                act.wait_ge(exp_in, 1)
                nc.scalar.activation(decay[:, :, :], decay[:, :, :], ACT.Exp).then_inc(exp_out, 1)
                act.wait_ge(exp_in, 2)
                nc.scalar.activation(rows[:, :, GF:ROW], rows[:, :, GF:ROW], ACT.Exp).then_inc(exp_out, 1)
                act.wait_ge(exp_in, 3)
                nc.scalar.activation(give[:, 0, 0:HEADS], give[:, 0, 0:HEADS], ACT.Exp).then_inc(exp_out, 1)

            @block.vector
            def _(dve):
                ch = Chain(dve, steps)
                V = nc.vector

                def hand_on(n, op0, op1, initial):
                    w = CARRIES[n]
                    dve.sem_inc(give_ready, 1)
                    dve.wait_ge(giveT_ready, n + 1)
                    ch(V.tensor_copy(giveT[0:w, :, :], tp[0:w, :, :]))
                    ch(V.memset(carryT[0:w, 0:1], initial))
                    ch(V.tensor_tensor_scan(out=carryT[0:w, 1:P + 1], data0=giveT[0:w, 0, :], data1=giveT[0:w, 1, :],
                                            initial=initial, op0=op0, op1=op1))
                    dve.sem_inc(carryT_ready, 1)
                    dve.wait_ge(carry_ready, n + 1)
                    ch(V.tensor_copy(carry[:, 0:w], cp[:, 0:w]))

                dve.wait_ge(heads_ready, 16)
                ch.add(V.tensor_scalar(out=keep[:, :], in0=heads[:, :, 0], scalar1=-1.0, scalar2=1.0, op0=ALU.mult, op1=ALU.add))
                ch(V.tensor_scalar(out=fresh[:, :], in0=heads[:, :, 0], scalar1=-BIG, scalar2=None, op0=ALU.mult))
                ch(V.tensor_reduce(out=whole[:, :], in_=keep[:, :], axis=AX, op=ALU.min))
                for h in range(HEADS):
                    ch(V.tensor_tensor_scan(out=junk[:, :], data0=keep[:, :], data1=heads[:, :, 1 + h], initial=0.0,
                                            op0=ALU.mult, op1=ALU.add))
                    ch(V.tensor_copy(give[:, 1, h:h + 1], junk[:, RUN - 1:RUN]))
                ch(V.tensor_copy(give[:, 0, 0:HEADS], whole[:, 0:1].to_broadcast([P, HEADS])))
                hand_on(0, ALU.mult, ALU.add, 0.0)
                for h in range(HEADS):
                    ch.add(V.tensor_tensor_scan(out=heads[:, :, 1 + h], data0=keep[:, :], data1=heads[:, :, 1 + h],
                                                initial=carry[:, h:h + 1], op0=ALU.mult, op1=ALU.add))
                ch.wait()
                logits = rows[:, :, GF:ROW]
                ch(V.tensor_tensor(out=logits, in0=logits, in1=heads[:, :, 1:1 + HEADS], op=ALU.add))
                ch(V.scalar_tensor_tensor(out=logits, in0=logits, scalar=0.2, in1=logits, op0=ALU.mult, op1=ALU.max))
                for h in range(HEADS):
                    ch(V.tensor_tensor_scan(out=junk[:, :], data0=fresh[:, :], data1=rows[:, :, GF + h], initial=-BIG,
                                            op0=ALU.add, op1=ALU.max))
                    ch(V.tensor_copy(give[:, 1, h:h + 1], junk[:, RUN - 1:RUN]))
                ch(V.tensor_scalar(out=give[:, 0, 0:HEADS], in0=whole[:, 0:1].to_broadcast([P, HEADS]), scalar1=-1.0,
                                   scalar2=BIG, op0=ALU.add, op1=ALU.mult))
                hand_on(1, ALU.add, ALU.max, -BIG)
                for h in range(HEADS):
                    ch.add(V.tensor_tensor_scan(out=top[:, :, h], data0=fresh[:, :], data1=rows[:, :, GF + h],
                                                initial=carry[:, h:h + 1], op0=ALU.add, op1=ALU.max))
                ch.wait()
                ch.add(V.tensor_tensor(out=decay[:, 1:RUN, :], in0=top[:, 0:RUN - 1, :], in1=top[:, 1:RUN, :], op=ALU.subtract))
                ch.add(V.tensor_tensor(out=decay[:, 0, :], in0=carry[:, 0:HEADS], in1=top[:, 0, :], op=ALU.subtract))
                ch(V.tensor_tensor(out=give[:, 0, 0:HEADS], in0=carry[:, 0:HEADS], in1=top[:, RUN - 1, :], op=ALU.subtract))
                ch.add(V.tensor_scalar_min(give[:, 0, 0:HEADS], give[:, 0, 0:HEADS], 0.0))
                ch(V.tensor_scalar_min(decay[:, :, :], decay[:, :, :], 0.0))
                dve.sem_inc(exp_in, 1)
                ch(V.tensor_tensor(out=logits, in0=logits, in1=top[:, :, :], op=ALU.subtract))
                dve.sem_inc(exp_in, 2)
                dve.wait_ge(exp_out, 1)
                ch(V.tensor_tensor(out=decay[:, :, :], in0=decay[:, :, :],
                                   in1=keep[:, :].unsqueeze(2).to_broadcast([P, RUN, HEADS]), op=ALU.mult))
                dve.wait_ge(exp_out, 2)
                feats = rows[:, :, 0:GF].rearrange("p c (h e) -> p c h e", h=HEADS)
                ch(V.tensor_tensor(out=feats, in0=feats, in1=logits.unsqueeze(3).to_broadcast([P, RUN, HEADS, EXPERTS]),
                                   op=ALU.mult))
                head = lambda c: c // EXPERTS if c < GF else c - GF
                for c in range(ROW):
                    ch(V.tensor_tensor_scan(out=junk[:, :], data0=decay[:, :, head(c)], data1=rows[:, :, c], initial=0.0,
                                            op0=ALU.mult, op1=ALU.add))
                    ch(V.tensor_copy(give[:, 1, c:c + 1], junk[:, RUN - 1:RUN]))
                dve.wait_ge(exp_out, 3)
                ch(V.tensor_scalar(out=give[:, 0, GF:ROW], in0=give[:, 0, 0:HEADS], scalar1=whole[:, 0:1], scalar2=None, op0=ALU.mult))
                ch(V.tensor_copy(give[:, 0, 0:GF].rearrange("p (h e) -> p h e", h=HEADS),
                                 give[:, 0, GF:ROW].unsqueeze(2).to_broadcast([P, HEADS, EXPERTS])))
                hand_on(2, ALU.mult, ALU.add, 0.0)
                for c in range(ROW):
                    ch.add(V.tensor_tensor_scan(out=rows[:, :, c], data0=decay[:, :, head(c)], data1=rows[:, :, c],
                                                initial=carry[:, c:c + 1], op0=ALU.mult, op1=ALU.add))
                ch.wait()
                dve.sem_inc(sums_ready, 1)

            @block.sync
            def _(sp):
                sp.dma_start(heads[:, :, :], starts_d.rearrange("(p c) k -> p c k", p=P)).then_inc(heads_ready, 16)
                sp.wait_ge(sums_ready, 1)
                sp.dma_start(sums_d.rearrange("(p c) k -> p c k", p=P), rows[:, :, :]).then_inc(sums_out, 16)

            @block.gpsimd
            def _(pool):
                pool.wait_ge(sums_out, 16)
                for t in range(NT):
                    pool.indirect_dma_start(out=pg.sums[:, t, :], out_offset=None, in_=sums_d,
                                            in_offset=bass.IndirectOffsetOnAxis(ap=pg.last[:, t:t + 1], axis=0)).then_inc(fetched, 16)
                pool.wait_ge(fetched, 16 * NT)


def stage_gate(pg):
    nc, a = pg.nc, pg.a
    with ExitStack() as st:
        sb = lambda n, s, d=F32: st.enter_context(nc.sbuf_tensor("t_" + n, s, d))
        bias, gain, shift = (sb(n, [P, GF]) for n in ("bias", "gain", "shift"))
        den, agg, sq = sb("den", [P, NT, HEADS]), sb("agg", [P, NT, GF]), sb("sq", [P, NT, GF])
        mean, var, std = sb("mean", [P, NT]), sb("var", [P, NT]), sb("std", [P, NT])
        score, ahead, cmp = sb("score", [P, NT, EXPERTS]), sb("ahead", [P, NT, EXPERTS]), sb("cmp", [P, NT])
        most, total = sb("most", [P, NT]), sb("total", [P, NT])
        loaded, steps = pg.sem("t_loaded"), pg.sem("t_steps")
        var_ready, std_ready, exp_in, exp_out = pg.sem("t_var_ready"), pg.sem("t_std_ready"), pg.sem("t_exp_in"), pg.sem("t_exp_out")
        with nc.Block() as block:
            @block.sync
            def _(sp):
                for d, v in ((bias, "b_gat"), (gain, "ln_gamma"), (shift, "ln_beta")):
                    sp.dma_start(d[:, :], row_of(a[v], GF)).then_inc(loaded, 16)
                sp.wait_ge(loaded, 48)

            @block.scalar
            def _(act):
                act.wait_ge(var_ready, 1)
                nc.scalar.activation(std[:, :], var[:, :], ACT.Sqrt).then_inc(std_ready, 1)
                act.wait_ge(exp_in, 1)
                nc.scalar.activation(score[:, :, :], score[:, :, :], ACT.Exp).then_inc(exp_out, 1)

            @block.vector
            def _(dve):
                ch = Chain(dve, steps)
                V = nc.vector
                nodes = lambda v: v[:, :].unsqueeze(1).to_broadcast([P, NT, GF])
                wide = lambda v, n: v[:, :].unsqueeze(2).to_broadcast([P, NT, n])
                dve.wait_ge(loaded, 48)
                ch(V.tensor_scalar_add(den[:, :, :], pg.sums[:, :, GF:ROW], 1e-16))
                ch(V.reciprocal(den[:, :, :], den[:, :, :]))
                ch(V.tensor_tensor(out=agg[:, :, :].rearrange("p t (h e) -> p t h e", h=HEADS),
                                   in0=pg.sums[:, :, 0:GF].rearrange("p t (h e) -> p t h e", h=HEADS),
                                   in1=den[:, :, :].unsqueeze(3).to_broadcast([P, NT, HEADS, EXPERTS]), op=ALU.mult))
                ch(V.tensor_tensor(out=agg[:, :, :], in0=agg[:, :, :], in1=nodes(bias), op=ALU.add))
                ch(V.tensor_reduce(out=mean[:, :], in_=agg[:, :, :], axis=AX, op=ALU.add))
                ch(V.tensor_scalar_mul(mean[:, :], mean[:, :], 1.0 / GF))
                ch(V.tensor_tensor(out=agg[:, :, :], in0=agg[:, :, :], in1=wide(mean, GF), op=ALU.subtract))
                ch(V.tensor_tensor(out=sq[:, :, :], in0=agg[:, :, :], in1=agg[:, :, :], op=ALU.mult))
                ch(V.tensor_reduce(out=var[:, :], in_=sq[:, :, :], axis=AX, op=ALU.add))
                ch(V.tensor_scalar(out=var[:, :], in0=var[:, :], scalar1=1.0 / GF, scalar2=LN_EPS, op0=ALU.mult, op1=ALU.add))
                dve.sem_inc(var_ready, 1)
                dve.wait_ge(std_ready, 1)
                ch(V.reciprocal(var[:, :], std[:, :]))
                ch(V.tensor_tensor(out=agg[:, :, :], in0=agg[:, :, :], in1=wide(var, GF), op=ALU.mult))
                ch(V.tensor_tensor(out=agg[:, :, :], in0=agg[:, :, :], in1=nodes(gain), op=ALU.mult))
                ch(V.tensor_tensor(out=agg[:, :, :], in0=agg[:, :, :], in1=nodes(shift), op=ALU.add))
                ch(V.tensor_reduce(out=score[:, :, :], in_=agg[:, :, :].rearrange("p t (h e) -> p t e h", h=HEADS), axis=AX, op=ALU.add))
                ch(V.tensor_scalar_mul(score[:, :, :], score[:, :, :], 1.0 / HEADS))
                ch(V.memset(ahead[:, :, :], 0.0))
                for e in range(EXPERTS):
                    for o in range(EXPERTS):
                        if o != e:
                            ch(V.tensor_tensor(out=cmp[:, :], in0=score[:, :, o], in1=score[:, :, e],
                                               op=ALU.is_ge if o < e else ALU.is_gt))
                            ch(V.tensor_tensor(out=ahead[:, :, e], in0=ahead[:, :, e], in1=cmp[:, :], op=ALU.add))
                ch(V.tensor_scalar(out=ahead[:, :, :], in0=ahead[:, :, :], scalar1=1.5, scalar2=None, op0=ALU.is_lt))
                ch(V.tensor_reduce(out=most[:, :], in_=score[:, :, :], axis=AX, op=ALU.max))
                ch(V.tensor_tensor(out=score[:, :, :], in0=score[:, :, :], in1=wide(most, EXPERTS), op=ALU.subtract))
                dve.sem_inc(exp_in, 1)
                dve.wait_ge(exp_out, 1)
                ch(V.tensor_tensor(out=score[:, :, :], in0=score[:, :, :], in1=ahead[:, :, :], op=ALU.mult))
                ch(V.tensor_reduce(out=total[:, :], in_=score[:, :, :], axis=AX, op=ALU.add))
                ch(V.reciprocal(total[:, :], total[:, :]))
                ch(V.tensor_tensor(out=pg.gate[:, :, :], in0=score[:, :, :], in1=wide(total, EXPERTS), op=ALU.mult))


def experts(pg, block, st):
    nc, a = pg.nc, pg.a
    pg.y_d = pg.dram("y_d", [EXPERTS, NPAD, C]).ap()
    sb = lambda n, s, d=F32: st.enter_context(nc.sbuf_tensor("x_" + n, s, d))
    pb = lambda n, s, d=F32: st.enter_context(nc.psum_tensor("x_" + n, s, d))
    w1, w2 = sb("w1", [P, EXPERTS, KC, FF]), sb("w2", [P, EXPERTS, FC, C])
    b1, b2 = sb("b1", [P, EXPERTS, FC]), sb("b2", [P, EXPERTS, C])
    xT = sb("xT", [P, KC, SN])
    hT = [sb(f"hT{b}", [P, FC, SN]) for b in range(2)]
    y = [sb(f"y{b}", [P, ST, C]) for b in range(2)]
    hp = [pb(f"hp{i}", [P, HN]) for i in range(4)]
    yp = [pb(f"yp{i}", [P, C]) for i in range(4)]
    w_ready, xT_ready = pg.sem("x_w_ready"), pg.sem("x_xT_ready")
    hp_ready, hp_free, hT_ready, hT_used = pg.sem("x_hp_ready"), pg.sem("x_hp_free"), pg.sem("x_hT_ready"), pg.sem("x_hT_used")
    yp_ready, yp_free, y_ready = pg.sem("x_yp_ready"), pg.sem("x_yp_free"), pg.sem("x_y_ready")
    y_stored = [pg.sem(f"x_y_stored{b}") for b in range(2)]
    y_free, xT_used = pg.sem("x_y_free"), pg.sem("x_xT_used")
    UN = FC * 2

    @block.scalar
    def _(act):
        for e in range(EXPERTS):
            act.dma_start(w1[:, e, :, :], weights_of(a["ffn_w1"][e])).then_inc(w_ready, 16)
            act.dma_start(w2[:, e, :, :], a["ffn_w2"][e].rearrange("(f p) n -> p f n", p=P)).then_inc(w_ready, 16)
            with nc.allow_non_contiguous_dma(reason="vectors of 512"):
                act.dma_start(b1[:, e, :], a["ffn_b1"][e].rearrange("(f p) -> p f", p=P)).then_inc(w_ready, 16)
            act.dma_start(b2[:, e, :], row_of(a["ffn_b2"][e], C)).then_inc(w_ready, 16)
        act.dma_start(xT[:, :, :], feat_cols(pg.x3T_d, 0)).then_inc(xT_ready, 16)
        act.sem_inc(hp_free, 4)
        act.sem_inc(y_free, 2)
        act.wait_ge(w_ready, 4 * EXPERTS * 16)

        def store(i, e):
            k = i * EXPERTS + e
            act.wait_ge(y_ready, k + 1)
            act.dma_start(node_rows(pg.y_d[e], i), y[e % 2][:, :, :]).then_inc(y_stored[e % 2], 16)

        def hidden(i, e):
            act.wait_ge(hT_used, i * EXPERTS + e + 1)
            for n in range(UN):
                f, h = n // 2, n % 2
                k = (i * EXPERTS + e) * UN + n + 1
                act.wait_ge(hp_ready, k)
                nc.scalar.activation(hT[e % 2][:, f, h * HN:(h + 1) * HN], hp[n % 4][:, :], ACT.Gelu,
                                     bias=b1[:, e, f:f + 1]).then_inc(hT_ready, 1)
                act.wait_ge(hT_ready, k)
                act.sem_inc(hp_free, 1)

        def step(i, first, last):
            for e in range(EXPERTS):
                hidden(i, e)
                if e == EXPERTS - 1 and not last:
                    act.dma_start(xT[:, :, :], feat_cols(pg.x3T_d, i + 1)).then_inc(xT_ready, 16)
                if e > 0 or not first:
                    p = (e - 1) % EXPERTS
                    k = i * EXPERTS + e - 1
                    act.wait_ge(y_ready, k + 1)
                    act.dma_start(node_rows(pg.y_d[p], i if e else i - 1), y[p % 2][:, :, :]).then_inc(y_stored[p % 2], 16)
                    act.wait_ge(y_stored[p % 2], ((k // 2) if first else i * (EXPERTS // 2) + (e - 1) // 2) * 16 + 16)
                    act.sem_inc(y_free, 1)

        step(0, True, False)
        with act.Fori(1, STEPS - 1) as i:
            step(i, False, False)
        step(STEPS - 1, False, True)
        store(STEPS - 1, EXPERTS - 1)
        act.wait_ge(y_stored[1], STEPS * EXPERTS // 2 * 16)

    @block.tensor
    def _(pe):
        pe.sem_inc(hT_used, 2)
        pe.wait_ge(w_ready, 4 * EXPERTS * 16)

        def up(i, e):
            for n in range(UN):
                f, h = n // 2, n % 2
                pe.wait_ge(hp_free, (i * EXPERTS + e) * UN + n + 1)
                for c in range(KC):
                    last = nc.tensor.matmul(hp[n % 4][:, :], w1[:, e, c, f * P:(f + 1) * P],
                                            xT[:, c, h * HN:(h + 1) * HN], start=(c == 0), stop=(c == KC - 1))
                last.then_inc(hp_ready, 1)

        def down(i, e):
            k = i * EXPERTS + e
            pe.wait_ge(hT_ready, k * UN + UN)
            for j in range(ST):
                pe.wait_ge(yp_free, k * ST + j + 1)
                for f in range(FC):
                    last = nc.tensor.matmul(yp[(e * ST + j) % 4][:, :], hT[e % 2][:, f, j * P:(j + 1) * P], w2[:, e, f, :],
                                            start=(f == 0), stop=(f == FC - 1))
                last.then_inc(yp_ready, 1)
            pe.wait_ge(yp_ready, k * ST + ST)
            pe.sem_inc(hT_used, 1)

        def step(i, first):
            pe.wait_ge(xT_ready, i * 16 + 16)
            for e in range(EXPERTS):
                up(i, e)
                if e > 0:
                    down(i, e - 1)
            down(i, EXPERTS - 1)

        with pe.Fori(0, STEPS) as i:
            step(i, False)

    @block.vector
    def _(dve):
        dve.sem_inc(yp_free, 4)
        dve.wait_ge(w_ready, 4 * EXPERTS * 16)
        with dve.Fori(0, STEPS) as i:
            for e in range(EXPERTS):
                k = i * EXPERTS + e
                dve.wait_ge(y_free, k + 1)
                for j in range(ST):
                    dve.wait_ge(yp_ready, k * ST + j + 1)
                    nc.vector.tensor_tensor(out=y[e % 2][:, j, :], in0=yp[(e * ST + j) % 4][:, :], in1=b2[:, e, :],
                                            op=ALU.add).then_inc(yp_free, 1)
                dve.wait_ge(yp_free, k * ST + ST + 4)
                dve.sem_inc(y_ready, 1)


def stage_combine(pg, out):
    nc, a = pg.nc, pg.a
    with ExitStack() as st:
        sb = lambda n, s, d=F32: st.enter_context(nc.sbuf_tensor("c_" + n, s, d))
        y = [sb(f"y{b}", [P, EXPERTS, ST, C]) for b in range(2)]
        acc = [sb(f"acc{b}", [P, ST, C]) for b in range(2)]
        y_ready = [pg.sem(f"c_y_ready{b}") for b in range(2)]
        y_free, done, added = pg.sem("c_y_free"), pg.sem("c_done"), pg.sem("c_added")
        saved = [pg.sem(f"c_saved{b}") for b in range(2)]
        final = pg.sem("c_final")
        with nc.Block() as block:
            @block.sync
            def _(sp):
                for i in range(STEPS):
                    if i >= 2:
                        sp.wait_ge(done, i - 1)
                        sp.wait_ge(saved[i % 2], (i // 2) * 16)
                    for e in range(EXPERTS):
                        sp.dma_start(y[i % 2][:, e, :, :], node_rows(pg.y_d[e], i)).then_inc(y_ready[i % 2], 16)
                    sp.dma_start(acc[i % 2][:, :, :], node_rows(pg.x2_d, i)).then_inc(y_ready[i % 2], 16)

            @block.vector
            def _(dve):
                n = 0
                for i in range(STEPS):
                    dve.wait_ge(y_ready[i % 2], (i // 2 + 1) * 16 * (EXPERTS + 1))
                    for e in range(EXPERTS):
                        for j in range(ST):
                            nc.vector.scalar_tensor_tensor(
                                out=acc[i % 2][:, j, :], in0=y[i % 2][:, e, j, :], scalar=pg.gate[:, i * ST + j, e:e + 1],
                                in1=acc[i % 2][:, j, :], op0=ALU.mult, op1=ALU.add).then_inc(added, 1)
                            n += 1
                        dve.wait_ge(added, n)
                    dve.sem_inc(done, 1)

            @block.scalar
            def _(act):
                for i in range(STEPS):
                    act.wait_ge(done, i + 1)
                    full = min(ST, (N_NODES - i * SN) // P)
                    act.dma_start(out[i * SN:i * SN + full * P, :].rearrange("(j p) c -> p j c", p=P),
                                  acc[i % 2][:, 0:full, :]).then_inc(saved[i % 2], 16)
                rest = N_NODES - (NT - 1) * P
                act.dma_start(out[N_NODES - rest:N_NODES, :], acc[(STEPS - 1) % 2][0:rest, ST - 1, :]).then_inc(final, 16)
                act.wait_ge(saved[0], (STEPS + 1) // 2 * 16)
                act.wait_ge(saved[1], STEPS // 2 * 16)
                act.wait_ge(final, 16)


def gps_layer_kernel(nc, out, **args):
    with ExitStack() as stack:
        pg = Program(nc, args, stack)
        setup(pg)
        stage_norm(pg)
        pg.end_stage()
        with ExitStack() as st:
            hold = lambda n, s, d: st.enter_context(nc.sbuf_tensor(n, s, d))
            pg.src_col, pg.place_col = hold("src_col", [P, GT], I32), hold("place_col", [P, GT], I32)
            pg.place = [hold(f"place{i}", [P, GB], I32) for i in range(SLOTS)]
            pg.source = [hold(f"source{i}", [P, GB], I32) for i in range(SLOTS)]
            pg.node_id = hold("node_id", [P, NT], I32)
            stage_sort(pg)
            pg.end_stage()
            pg.agg = hold("agg", [P, NT, C], F32)
            stage_edges(pg)
            pg.end_stage()
            stage_mix(pg)
            pg.end_stage()
            stage_gnn(pg)
            pg.end_stage()
        stage_attend(pg)
        pg.end_stage()
        stage_gate(pg)
        stage_combine(pg, out)


def kernel(**inputs):
    import concourse.bacc as _bacc
    from concourse.bass_utils import run_bass_kernel_spmd as _run

    nc = _bacc.Bacc("TRN2", target_bir_lowering=False, num_devices=1)
    arrays, aps = {}, {}
    for name, value in layout(inputs).items():
        arrays[name] = value
        aps[name] = nc.dram_tensor(name, value.shape, mybir.dt.from_np(value.dtype), kind="ExternalInput").ap()
    out = nc.dram_tensor("out", (N_NODES, C), F32, kind="ExternalOutput").ap()
    gps_layer_kernel(nc, out, **aps)
    return _run(nc, [arrays], core_ids=[0]).results[0]["out"]


def layout(v):
    t = lambda m: np.ascontiguousarray(np.asarray(m).T)
    n = lambda m: np.ascontiguousarray(np.asarray(m))
    return {
        "x": n(v["x"]), "src": n(v["src"]), "dst": n(v["dst"]), "edge_attr": n(v["edge_attr_128"]),
        "w_edge": n(v["L0_gnn_W_edge"]), "b_edge": n(v["L0_gnn_b_edge"]),
        "gnn_w1": n(v["L0_gnn_W1"]), "gnn_b1": n(v["L0_gnn_b1"]), "gnn_w2": n(v["L0_gnn_W2"]),
        "gnn_b2": n(v["L0_gnn_b2"]), "gnn_eps": n(v["L0_gnn_eps"]).reshape(1, 1),
        "gnn_gamma": n(v["L0_gnn_gamma"]), "gnn_beta": n(v["L0_gnn_beta"]),
        "mix_wqkvT": t(v["L0_mix_Wqkv"]), "mix_g1": n(v["L0_mix_ln1_g"]), "mix_be1": n(v["L0_mix_ln1_b"]),
        "mix_w1T": t(v["L0_mix_W1"]), "mix_b1": n(v["L0_mix_b1"]), "mix_w2T": t(v["L0_mix_W2"]),
        "mix_b2": n(v["L0_mix_b2"]), "mix_g2": n(v["L0_mix_ln2_g"]), "mix_be2": n(v["L0_mix_ln2_b"]),
        "w_gat": n(v["L0_ffn_W_gat"]), "att_src": n(v["L0_ffn_att_src"]), "att_dst": n(v["L0_ffn_att_dst"]),
        "b_gat": n(v["L0_ffn_b_gat"]), "ln_gamma": n(v["L0_ffn_ln_gamma"]), "ln_beta": n(v["L0_ffn_ln_beta"]),
        "ffn_w1": n(v["L0_ffn_W1"]), "ffn_b1": n(v["L0_ffn_b1"]), "ffn_w2": n(v["L0_ffn_W2"]),
        "ffn_b2": n(v["L0_ffn_b2"]), "g_edges": n(v["L0_ffn_edge_index"]),
    }
```

```python
import numpy as np
import concourse.bass as bass
from concourse import mybir
from contextlib import ExitStack

F32 = mybir.dt.float32
BF16 = mybir.dt.bfloat16
I32 = mybir.dt.int32
ALU = mybir.AluOpType
ACT = mybir.ActivationFunctionType
AX = mybir.AxisListType.X

P = 128
N_NODES = 6250
C = 256
KC = C // P
N_EDGES = 100000
E_DIM = 128
G_EDGES = 131072
NT = -(-N_NODES // P)
NPAD = NT * P
ST = 7
STEPS = NT // ST
SN = ST * P
HN = SN // 2
LN_EPS = 1e-5
HD = 32
HH = P // HD
EXPERTS = 4
HEADS = 4
GF = HEADS * EXPERTS
FF = 512
FC = FF // P
ROW = GF + HEADS
STATE = ROW + HEADS
START = 1 + HEADS
BIG = 1.0e30


class Chain:

    def __init__(self, eng, sem, base=0):
        self.eng, self.sem, self.base, self.n = eng, sem, base, 0

    def add(self, ins):
        self.n += 1
        ins.then_inc(self.sem, 1)

    def wait(self):
        self.eng.wait_ge(self.sem, self.base + self.n)

    def __call__(self, ins):
        self.add(ins)
        self.wait()


class Program:

    def __init__(self, nc, args, stack):
        self.nc, self.a, self.stack = nc, args, stack
        self.turns = stack.enter_context(nc.semaphore("turns"))
        self.sems = []

    def sem(self, name):
        self.sems.append(self.nc.alloc_semaphore(name=name))
        return self.sems[-1]

    def end_stage(self):
        self.nc.clear_and_free_semaphores(self.sems)
        self.nc.all_engine_barrier()
        self.sems = []

    def dram(self, name, shape, dtype=F32):
        return self.nc.dram_tensor(name, shape, dtype)

    def keep(self, name, shape, dtype=F32):
        return self.stack.enter_context(self.nc.sbuf_tensor(name, shape, dtype))


def node_rows(ap, i):
    return ap[bass.ds(i * SN, SN), :].rearrange("(j p) c -> p j c", p=P)


def feat_cols(ap, i):
    return ap[:, :, bass.ds(i * SN, SN)].rearrange("h p n -> p h n")


def setup(pg):
    nc, a = pg.nc, pg.a
    pg.ident = pg.keep("ident", [P, P])
    pg.ones_row = pg.keep("ones_row", [1, P])
    pg.zeros = pg.keep("zeros", [P, 512])
    pg.headmask = pg.keep("headmask", [P, HH])
    pg.valid = pg.keep("valid", [P, NT])
    pg.kv_blocks = pg.keep("kv_blocks", [P, KC, P + HH])
    pg.first = pg.keep("first", [P, NT], I32)
    pg.last = pg.keep("last", [P, NT], I32)
    pg.starts = pg.keep("starts", [P, NT, START])
    pg.sums = pg.keep("sums", [P, NT, ROW])
    pg.run_end = pg.keep("run_end", [P, STATE])
    pg.whole = pg.keep("whole", [P, 1])
    pg.sums_d = pg.dram("sums_d", [P * RUN, STATE]).ap()
    pg.gate = pg.keep("gate", [P, NT, EXPERTS])
    pg.xpad = pg.dram("xpad", [NPAD, C]).ap()
    pg.xn_d = pg.dram("xn_d", [NPAD, C]).ap()
    pg.xb_d = pg.dram("xb_d", [NPAD, C]).ap()
    pg.xT_d = pg.dram("xT_d", [KC, P, NPAD]).ap()
    pg.mix_d = pg.dram("mix_d", [NPAD, C]).ap()
    pg.x2_d = pg.dram("x2_d", [NPAD, C]).ap()
    pg.x3T_d = pg.dram("x3T_d", [KC, P, NPAD]).ap()
    s_zero, s_mask, s_pad = pg.sem("s_zero"), pg.sem("s_mask"), pg.sem("s_pad")
    with nc.Block() as block:
        @block.gpsimd
        def _(pool):
            nc.gpsimd.memset(pg.zeros[:, :], 0.0).then_inc(s_zero, 1)
            nc.gpsimd.memset(pg.ones_row[:, :], 1.0).then_inc(s_mask, 1)
            nc.gpsimd.memset(pg.ident[:, :], 0.0).then_inc(s_mask, 1)
            nc.gpsimd.memset(pg.headmask[:, :], 1.0).then_inc(s_mask, 1)
            nc.gpsimd.memset(pg.valid[:, :], 1.0).then_inc(s_mask, 1)
            pool.wait_ge(s_mask, 4)
            nc.gpsimd.affine_select(out=pg.ident[:, :], in_=pg.ident[:, :], compare_op=ALU.not_equal, fill=1.0,
                                    base=0, pattern=[[-1, P]], channel_multiplier=1).then_inc(s_mask, 1)
            nc.gpsimd.affine_select(out=pg.headmask[:, :], in_=pg.headmask[:, :], compare_op=ALU.is_ge, fill=0.0,
                                    base=0, pattern=[[-HD, HH]], channel_multiplier=1).then_inc(s_mask, 1)
            pool.wait_ge(s_mask, 6)
            nc.gpsimd.affine_select(out=pg.headmask[:, :], in_=pg.headmask[:, :], compare_op=ALU.is_ge, fill=0.0,
                                    base=HD - 1, pattern=[[HD, HH]], channel_multiplier=-1).then_inc(s_mask, 1)
            nc.gpsimd.affine_select(out=pg.valid[:, :], in_=pg.valid[:, :], compare_op=ALU.is_ge, fill=0.0,
                                    base=N_NODES - 1, pattern=[[-P, NT]], channel_multiplier=-1).then_inc(s_mask, 1)
            pool.wait_ge(s_mask, 8)

        @block.sync
        def _(sp):
            sp.dma_start(pg.xpad[0:N_NODES, :], a["x"]).then_inc(s_pad, 16)
            sp.wait_ge(s_zero, 1)
            sp.dma_start(pg.xpad[N_NODES:NPAD, :], pg.zeros[0:NPAD - N_NODES, 0:C]).then_inc(s_pad, 16)
            sp.wait_ge(s_pad, 32)


def norm_statistics(nc, dve, ch, turns, rows, stats, mv, var, var_ready, std, std_ready, count):
    for j in range(ST):
        ch.add(nc.vector.bn_stats(out=stats[:, j, :], in_=rows[:, j, :]))
    ch.wait()
    dve.sem_inc(turns, 1)
    for j in range(ST):
        ch.add(nc.vector.bn_aggr(out=mv[:, j, :], in_=stats[:, j, :]))
    ch.wait()
    nc.vector.tensor_scalar_add(var[:, :], mv[:, :, 1], LN_EPS).then_inc(var_ready, 1)
    dve.wait_ge(std_ready, count)
    ch(nc.vector.reciprocal(var[:, :], std[:, :]))


NORM_STEPS = 2 * ST + 1


def normalise(nc, ch, out, rows, mv, rstd):
    for j in range(ST):
        ch.add(nc.vector.tensor_scalar(out=out[:, j, :], in0=rows[:, j, :], scalar1=mv[:, j, 0:1],
                                       scalar2=rstd[:, j:j + 1], op0=ALU.subtract, op1=ALU.mult))
    ch.wait()


UNITS = [(q, min(4, KC * ST - q)) for q in range(0, KC * ST, 4)]
NU = len(UNITS)


def transpose_rows(nc, pe, rows, ident, tp, tp_ready, tp_free, count):
    for u, (q0, nq) in enumerate(UNITS):
        pe.wait_ge(tp_free, count + u + 1)
        for q in range(q0, q0 + nq):
            h, j = q // ST, q % ST
            last = nc.tensor.transpose(tp[u % 2][:, (q - q0) * P:(q - q0 + 1) * P],
                                       rows[:, j, h * P:(h + 1) * P], ident[:, :])
        last.then_inc(tp_ready, 1)


def copy_blocks(nc, act, out, tp, tp_ready, tp_free, out_ready, count):
    flat = out[:, :, :].rearrange("p h n -> p (h n)")
    for u, (q0, nq) in enumerate(UNITS):
        act.wait_ge(tp_ready, count + u + 1)
        nc.scalar.activation(flat[:, q0 * P:(q0 + nq) * P], tp[u % 2][:, 0:nq * P], ACT.Copy).then_inc(tp_free, 1)
    act.wait_ge(tp_free, count + NU + 2)
    act.sem_inc(out_ready, 1)


def stage_norm(pg):
    nc, a = pg.nc, pg.a
    with ExitStack() as st:
        sb = lambda n, s, d=F32: st.enter_context(nc.sbuf_tensor("n_" + n, s, d))
        pb = lambda n, s, d=F32: st.enter_context(nc.psum_tensor("n_" + n, s, d))
        x_in, xn, xb = sb("x_in", [P, ST, C]), sb("xn", [P, ST, C]), sb("xb", [P, ST, C])
        xT = sb("xT", [P, KC, SN])
        b_edge = sb("b_edge", [P, C])
        wkv = sb("wkv", [P, KC, 2 * C])
        stats, mv = sb("stats", [P, ST, 6]), sb("mv", [P, ST, 2])
        std, rstd = sb("std", [P, ST]), sb("rstd", [P, ST])
        kneg, kexp, kf = (sb(n, [P, ST, C]) for n in ("kneg", "kexp", "kf"))
        vf = sb("vf", [P, ST, KC, P + 1])
        tp = [pb(f"tp{i}", [P, 512]) for i in range(2)]
        kp = [pb(f"kp{i}", [P, C]) for i in range(2)]
        vp = [pb(f"vp{i}", [P, C]) for i in range(2)]
        kv = pb("kv", [P, KC * (P + 1)])
        rows_ready, rows_free = pg.sem("n_rows_ready"), pg.sem("n_rows_free")
        w_ready, steps = pg.sem("n_w_ready"), pg.sem("n_steps")
        var_ready, std_ready = pg.sem("n_var_ready"), pg.sem("n_std_ready")
        xn_ready, xn_free = pg.sem("n_xn_ready"), pg.sem("n_xn_free")
        stored = pg.sem("n_stored")
        tp_ready, tp_free = pg.sem("n_tp_ready"), pg.sem("n_tp_free")
        xT_ready, xT_free, xT_stored = pg.sem("n_xT_ready"), pg.sem("n_xT_free"), pg.sem("n_xT_stored")
        kvp_ready = pg.sem("n_kvp_ready")
        kneg_ready, kexp_ready = pg.sem("n_kneg_ready"), pg.sem("n_kexp_ready")
        kf_ready, vf_ready, kv_used = pg.sem("n_kf_ready"), pg.sem("n_vf_ready"), pg.sem("n_kv_used")
        kv_done = pg.sem("n_kv_done")
        with nc.Block() as block:
            @block.sync
            def _(sp):
                sp.dma_start(wkv[:, :, :], a["mix_wqkvT"][:, C:3 * C].rearrange("(h p) n -> p h n", p=P)).then_inc(w_ready, 16)
                sp.dma_start(b_edge[:, :], a["b_edge"].rearrange("(o c) -> o c", o=1).to_broadcast([P, C])).then_inc(w_ready, 16)
                with sp.Fori(0, STEPS) as i:
                    sp.wait_ge(rows_free, i + 1)
                    sp.dma_start(x_in[:, :, :], node_rows(pg.xpad, i)).then_inc(rows_ready, 16)

            @block.gpsimd
            def _(pool):
                pool.sem_inc(xn_free, 1)
                pool.sem_inc(xT_stored, 1)
                with pool.Fori(0, STEPS) as i:
                    pool.wait_ge(xn_ready, i + 1)
                    pool.dma_start(node_rows(pg.xn_d, i), xn[:, :, :]).then_inc(stored, 16)
                    pool.dma_start(node_rows(pg.xb_d, i), xb[:, :, :]).then_inc(stored, 16)
                    pool.wait_ge(xT_ready, i + 1)
                    pool.dma_start(feat_cols(pg.xT_d, i), xT[:, :, :]).then_inc(stored, 16)
                    pool.wait_ge(stored, i * 48 + 48)
                    pool.sem_inc(xn_free, 1)
                    pool.sem_inc(xT_stored, 1)

            @block.vector
            def _(dve):
                dve.sem_inc(rows_free, 1)
                dve.wait_ge(w_ready, 32)
                K = NORM_STEPS + ST
                with dve.Fori(0, STEPS) as i:
                    ch = Chain(dve, steps, i * K)
                    dve.wait_ge(rows_ready, i * 16 + 16)
                    norm_statistics(nc, dve, ch, pg.turns, x_in, stats, mv, rstd, var_ready, std, std_ready, i + 1)
                    dve.wait_ge(xn_free, i + 1)
                    normalise(nc, ch, xn, x_in, mv, rstd)
                    assert ch.n == K
                    dve.sem_inc(rows_free, 1)
                    nc.vector.tensor_tensor(out=xb[:, :, :], in0=xn[:, :, :],
                                            in1=b_edge[:, :].unsqueeze(1).to_broadcast([P, ST, C]),
                                            op=ALU.add).then_inc(xn_ready, 1)
                    for j in range(ST):
                        dve.wait_ge(kvp_ready, i * ST + j + 1)
                        if j == 0:
                            dve.wait_ge(kv_used, i + 1)
                        nc.vector.tensor_scalar_min(kneg[:, j, :], kp[j % 2][:, :], 0.0).then_inc(kneg_ready, 1)
                        dve.wait_ge(kexp_ready, i * ST + j + 1)
                        nc.vector.scalar_tensor_tensor(out=kf[:, j, :], in0=kp[j % 2][:, :], scalar=0.0,
                                                       in1=kexp[:, j, :], op0=ALU.max, op1=ALU.add).then_inc(kf_ready, 1)
                dve.wait_ge(kv_done, 1)
                kvs = kv[:, :].rearrange("p (h n) -> p h n", h=KC)
                hm = pg.headmask[:, :]
                for h in range(KC):
                    nc.vector.tensor_tensor(
                        out=pg.kv_blocks[:, h, 0:P].rearrange("p (g d) -> p g d", g=HH),
                        in0=kvs[:, h, 0:P].rearrange("p (g d) -> p g d", g=HH),
                        in1=hm.unsqueeze(2).to_broadcast([P, HH, HD]), op=ALU.mult)
                    nc.vector.tensor_scalar(out=pg.kv_blocks[:, h, P:P + HH], in0=hm, scalar1=kvs[:, h, P:P + 1],
                                            scalar2=None, op0=ALU.mult)

            @block.scalar
            def _(act):
                act.sem_inc(tp_free, 2)
                with act.Fori(0, STEPS) as i:
                    act.wait_ge(var_ready, i + 1)
                    nc.scalar.activation(std[:, :], rstd[:, :], ACT.Sqrt).then_inc(std_ready, 1)
                    act.wait_ge(xT_stored, i + 1)
                    act.wait_ge(xT_free, i + 1)
                    copy_blocks(nc, act, xT, tp, tp_ready, tp_free, xT_ready, i * NU)
                    for j in range(ST):
                        act.wait_ge(kvp_ready, i * ST + j + 1)
                        if j == 0:
                            act.wait_ge(kv_used, i + 1)
                        nc.scalar.activation(vf[:, j, :, 0:P], vp[j % 2][:, :].rearrange("p (h n) -> p h n", h=KC),
                                             ACT.Copy).then_inc(vf_ready, 1)
                        for h in range(KC):
                            nc.scalar.activation(vf[:, j, h, P:P + 1], pg.valid[:, bass.ds(i * ST + j, 1)],
                                                 ACT.Copy).then_inc(vf_ready, 1)
                        act.wait_ge(kneg_ready, i * ST + j + 1)
                        nc.scalar.activation(kexp[:, j, :], kneg[:, j, :], ACT.Exp).then_inc(kexp_ready, 1)

            @block.tensor
            def _(pe):
                pe.wait_ge(w_ready, 32)
                pe.sem_inc(xT_free, 1)
                pe.sem_inc(kv_used, 1)
                nc.tensor.matmul(kv[:, :], pg.zeros[:, 0:P], pg.zeros[:, 0:KC * (P + 1)], start=True, stop=True)
                with pe.Fori(0, STEPS) as i:
                    pe.wait_ge(xn_ready, i + 1)
                    transpose_rows(nc, pe, xn, pg.ident, tp, tp_ready, tp_free, i * NU)
                    pe.wait_ge(xT_ready, i + 1)
                    for j in range(ST):
                        if j >= 2:
                            pe.wait_ge(kf_ready, i * ST + j - 1)
                            pe.wait_ge(vf_ready, (i * ST + j - 1) * 3)
                        for o, out in enumerate((kp, vp)):
                            for c in range(KC):
                                last = nc.tensor.matmul(out[j % 2][:, :], xT[:, c, j * P:(j + 1) * P],
                                                        wkv[:, c, o * C:(o + 1) * C], start=(c == 0), stop=(c == KC - 1))
                        last.then_inc(kvp_ready, 1)
                    pe.wait_ge(kf_ready, i * ST + ST)
                    pe.wait_ge(vf_ready, (i * ST + ST) * 3)
                    pe.sem_inc(xT_free, 1)
                    for j in range(ST):
                        for h in range(KC):
                            last = nc.tensor.matmul(kv[:, h * (P + 1):(h + 1) * (P + 1)], kf[:, j, h * P:(h + 1) * P],
                                                    vf[:, j, h, :], start=False, stop=True, skip_group_check=True)
                    last.then_inc(kv_used, 1)
                pe.wait_ge(kv_used, STEPS + 1)
                pe.sem_inc(kv_done, 1)


GT = G_EDGES // P
GB = 8
GR = GT // P
RUN = GT + NT
SLOTS = 2


SORT_BATCHES = 88
MIX_BATCHES = 34
GNN_BATCHES = GT // GB - SORT_BATCHES - MIX_BATCHES


def scatter_batches(pg, pool, name, first, count, ready=None):
    nc = pg.nc
    copied = pg.sem(name + "_copied")
    sent = [pg.sem(f"{name}_sent{b}") for b in range(SLOTS)]

    def batch(i, b, fresh):
        k = i * SLOTS + b
        if ready is not None:
            pool.wait_ge(ready, first + k + 1)
        if not fresh:
            pool.wait_ge(sent[b], i * (16 * GB))
        nc.gpsimd.tensor_copy(pg.place[b][:, :], pg.place_col[:, bass.ds((first + k) * GB, GB)]).then_inc(copied, 1)
        nc.gpsimd.tensor_copy(pg.source[b][:, :], pg.src_col[:, bass.ds((first + k) * GB, GB)]).then_inc(copied, 1)
        pool.wait_ge(copied, k * 2 + 2)
        pool.sem_inc(pg.turns, 1)
        for t in range(GB):
            pool.indirect_dma_start(out=pg.sorted_d, out_offset=bass.IndirectOffsetOnAxis(ap=pg.place[b][:, t:t + 1], axis=0),
                                    in_=pg.source[b][:, t:t + 1], in_offset=None).then_inc(sent[b], 16)

    for b in range(SLOTS):
        batch(0, b, True)
    with pool.Fori(1, count // SLOTS) as i:
        for b in range(SLOTS):
            batch(i, b, False)
    for b in range(SLOTS):
        pool.wait_ge(sent[b], 16 * GB * (count // SLOTS))


def stage_sort(pg):
    nc, a = pg.nc, pg.a
    pg.sorted_d = pg.dram("sorted_d", [P * RUN, 1], I32).ap()
    lo_d = pg.dram("lo_d", [G_EDGES], BF16).ap()
    with ExitStack() as st:
        sb = lambda n, s, d=F32: st.enter_context(nc.sbuf_tensor("s_" + n, s, d))
        pb = lambda n, s, d=F32: st.enter_context(nc.psum_tensor("s_" + n, s, d))
        src_i, key_i, tmp_i = (sb(n, [P, GT], I32) for n in ("src_i", "key_i", "tmp_i"))
        src_f, lo_f, hi_f = (sb(n, [P, GT]) for n in ("src_f", "lo_f", "hi_f"))
        lo_b = sb("lo_b", [P, GT], BF16)
        src_col, place_col = pg.src_col, pg.place_col
        lo_col, hi_col = sb("lo_col", [P, GT], BF16), sb("hi_col", [P, GT], BF16)
        iota_p = sb("iota_p", [P, 1])
        iota_lo = sb("iota_lo", [P, P], BF16)
        iota_hi = sb("iota_hi", [P, NT], BF16)
        before = sb("before", [P, P])
        before_b = sb("before_b", [P, P], BF16)
        ones = sb("ones", [P, P])
        counts, totals, starts, first_f, last_f, seed = (
            sb(n, [P, NT]) for n in ("counts", "totals", "starts", "first_f", "last_f", "seed"))
        lo_row = [sb(f"lo_row{i}", [P, GB, P], BF16) for i in range(SLOTS)]
        one_lo = [sb(f"one_lo{i}", [P, GB, P], BF16) for i in range(SLOTS)]
        one_hi = [sb(f"one_hi{i}", [P, GB, NT], BF16) for i in range(SLOTS)]
        one_loT = [sb(f"one_loT{i}", [P, GB, P]) for i in range(SLOTS)]
        same = [sb(f"same{i}", [P, GB, P], BF16) for i in range(SLOTS)]
        seen = [sb(f"seen{i}", [P, NT]) for i in range(2)]
        ranked = sb("ranked", [P, GB, NT])
        place_f = sb("place_f", [P, GB])
        tp = [pb(f"tp{i}", [P, 512]) for i in range(2)]
        total = pb("total", [P, NT])
        live = pb("live", [P, NT])
        rank = [pb(f"rank{i}", [P, GB, NT]) for i in range(SLOTS)]
        loaded, steps, const = pg.sem("s_loaded"), pg.sem("s_steps"), pg.sem("s_const")
        keys_ready, src_ready = pg.sem("s_keys_ready"), pg.sem("s_src_ready")
        lo_stored = pg.sem("s_lo_stored")
        tp_ready, tp_free, cols_ready = pg.sem("s_tp_ready"), pg.sem("s_tp_free"), pg.sem("s_cols_ready")
        hot_ready, hot_used = pg.sem("s_hot_ready"), pg.sem("s_hot_used")
        counted, prefix_ready, prefix_in = pg.sem("s_counted"), pg.sem("s_prefix_ready"), pg.sem("s_prefix_in")
        first_ready, seeded = pg.sem("s_first_ready"), pg.sem("s_seeded")
        row_ready = [pg.sem(f"s_row_ready{i}") for i in range(SLOTS)]
        row_free = pg.sem("s_row_free")
        live_ready, seen_ready = pg.sem("s_live_ready"), pg.sem("s_seen_ready")
        sets_ready, sets_used = pg.sem("s_sets_ready"), pg.sem("s_sets_used")
        rank_ready, rank_free = pg.sem("s_rank_ready"), pg.sem("s_rank_free")
        place_ready = pg.sem("s_place_ready")
        NB = GT // GB
        PAIRS = NB // SLOTS
        with nc.Block() as block:
            @block.sync
            def _(sp):
                sp.dma_start(key_i[:, :], a["g_edges"][1, :].rearrange("(p c) -> p c", p=P)).then_inc(loaded, 16)
                sp.dma_start(src_i[:, :], a["g_edges"][0, :].rearrange("(p c) -> p c", p=P)).then_inc(loaded, 16)
                sp.wait_ge(keys_ready, 1)
                sp.dma_start(lo_d.rearrange("(p c) -> p c", p=P), lo_b[:, :]).then_inc(lo_stored, 16)
                sp.wait_ge(lo_stored, 16)
                with sp.Fori(0, PAIRS) as i:
                    for b in range(SLOTS):
                        sp.wait_ge(row_free, i * SLOTS + b + 1)
                        rows = lo_d[bass.ds((i * SLOTS + b) * GB * P, GB * P)]
                        sp.dma_start(lo_row[b][:, :, :].rearrange("p t e -> p (t e)"),
                                     rows.rearrange("(o n) -> o n", o=1).to_broadcast([P, GB * P])).then_inc(row_ready[b], 16)

            @block.gpsimd
            def _(pool):
                nc.gpsimd.iota(iota_p[:, :], pattern=[[0, 1]], base=0, channel_multiplier=1,
                               allow_small_or_imprecise_dtypes=True).then_inc(const, 1)
                nc.gpsimd.iota(iota_lo[:, :], pattern=[[1, P]], base=0, channel_multiplier=0,
                               allow_small_or_imprecise_dtypes=True).then_inc(const, 1)
                nc.gpsimd.iota(iota_hi[:, :], pattern=[[1, NT]], base=0, channel_multiplier=0,
                               allow_small_or_imprecise_dtypes=True).then_inc(const, 1)
                nc.gpsimd.iota(pg.node_id[:, :], pattern=[[P, NT]], base=0, channel_multiplier=1).then_inc(const, 1)
                nc.gpsimd.memset(ones[:, :], 1.0).then_inc(const, 1)
                pool.wait_ge(const, 5)
                nc.gpsimd.affine_select(out=before[:, :], in_=ones[:, :], compare_op=ALU.is_ge, fill=0.0,
                                        base=-1, pattern=[[1, P]], channel_multiplier=-1).then_inc(const, 1)
                pool.wait_ge(const, 6)
                nc.gpsimd.tensor_copy(before_b[:, :], before[:, :]).then_inc(const, 1)
                scatter_batches(pg, pool, "s", 0, SORT_BATCHES, place_ready)

            @block.vector
            def _(dve):
                ch = Chain(dve, steps)
                dve.wait_ge(loaded, 32)
                ch.add(nc.vector.tensor_scalar_min(src_f[:, :], src_i[:, :], float(N_NODES - 1)))
                ch(nc.vector.tensor_scalar_min(tmp_i[:, :], key_i[:, :], float(N_NODES)))
                ch(nc.vector.tensor_single_scalar(key_i[:, :], tmp_i[:, :], P - 1, op=ALU.bitwise_and))
                ch.add(nc.vector.tensor_copy(lo_f[:, :], key_i[:, :]))
                ch(nc.vector.tensor_copy(lo_b[:, :], key_i[:, :]))
                dve.sem_inc(keys_ready, 1)
                ch(nc.vector.tensor_single_scalar(key_i[:, :], tmp_i[:, :], 7, op=ALU.logical_shift_right))
                ch(nc.vector.tensor_copy(hi_f[:, :], key_i[:, :]))
                dve.sem_inc(src_ready, 1)
                dve.sem_inc(row_free, SLOTS)
                dve.sem_inc(rank_free, SLOTS)
                dve.wait_ge(const, 7)
                dve.wait_ge(cols_ready, 1)
                base = ch.n

                def one_hots(b, tile):
                    nc.vector.tensor_tensor(out=one_lo[b][:, :, :], in0=iota_lo[:, :].unsqueeze(1).to_broadcast([P, GB, P]),
                                            in1=lo_col[:, bass.ds(tile, GB)].unsqueeze(2).to_broadcast([P, GB, P]),
                                            op=ALU.is_equal).then_inc(hot_ready, 1)
                    nc.vector.tensor_tensor(out=one_hi[b][:, :, :], in0=iota_hi[:, :].unsqueeze(1).to_broadcast([P, GB, NT]),
                                            in1=hi_col[:, bass.ds(tile, GB)].unsqueeze(2).to_broadcast([P, GB, NT]),
                                            op=ALU.is_equal).then_inc(hot_ready, 1)

                with dve.Fori(0, PAIRS) as i:
                    for b in range(SLOTS):
                        dve.wait_ge(hot_used, i * SLOTS + b + 1)
                        one_hots(b, (i * SLOTS + b) * GB)
                dve.wait_ge(counted, 1)
                ch(nc.vector.tensor_scalar_add(counts[:, :], total[:, :], 1.0))
                dve.sem_inc(prefix_in, 1)
                dve.wait_ge(prefix_ready, 1)
                ch(nc.vector.tensor_copy(totals[:, :], total[:, :]))
                ch(nc.vector.tensor_tensor_scan(out=starts[:, :], data0=ones[:, 0:NT], data1=totals[:, :], initial=0.0,
                                                op0=ALU.mult, op1=ALU.add))
                ch(nc.vector.tensor_tensor(out=starts[:, :], in0=starts[:, :], in1=totals[:, :], op=ALU.subtract))
                ch(nc.vector.tensor_tensor(out=first_f[:, :], in0=starts[:, :], in1=live[:, :], op=ALU.add))
                ch(nc.vector.tensor_copy(pg.first[:, :], first_f[:, :]))
                ch(nc.vector.tensor_scalar_add(seed[:, :], first_f[:, :], 1.0))
                dve.sem_inc(first_ready, 1)
                ch(nc.vector.tensor_tensor(out=last_f[:, :], in0=first_f[:, :], in1=counts[:, :], op=ALU.add))
                ch(nc.vector.tensor_scalar_add(pg.last[:, :], last_f[:, :], -1.0))
                base += 9

                def prepare(ch, n, b, turn):
                    dve.wait_ge(sets_used, n + 1)
                    one_hots(b, n * GB)
                    dve.wait_ge(row_ready[b], turn * 16 + 16)
                    ch.add(nc.vector.tensor_tensor(out=same[b][:, :, :], in0=lo_row[b][:, :, :],
                                                   in1=lo_col[:, bass.ds(n * GB, GB)].unsqueeze(2).to_broadcast([P, GB, P]),
                                                   op=ALU.is_equal))
                    ch(nc.vector.tensor_scalar(out=one_loT[b][:, :, :], in0=lo_row[b][:, :, :], scalar1=iota_p[:, 0:1],
                                               scalar2=None, op0=ALU.is_equal))
                    dve.sem_inc(row_free, 1)
                    nc.vector.tensor_tensor(out=same[b][:, :, :], in0=same[b][:, :, :],
                                            in1=before_b[:, :].unsqueeze(1).to_broadcast([P, GB, P]),
                                            op=ALU.mult).then_inc(sets_ready, 1)

                def finish(ch, n, b):
                    dve.wait_ge(rank_ready, n + 1)
                    ch(nc.vector.tensor_tensor(out=ranked[:, :, :], in0=rank[b][:, :, :], in1=one_hi[b][:, :, :], op=ALU.mult))
                    dve.sem_inc(rank_free, 1)
                    ch(nc.vector.tensor_reduce(out=place_f[:, :], in_=ranked[:, :, :], axis=AX, op=ALU.add))
                    nc.vector.tensor_copy(place_col[:, bass.ds(n * GB, GB)], place_f[:, :]).then_inc(place_ready, 1)

                K = 4
                prepare(Chain(dve, steps, base), 0, 0, 0)
                base += 2
                with dve.Fori(0, PAIRS - 1) as i:
                    ch = Chain(dve, steps, base + i * SLOTS * K)
                    prepare(ch, i * 2 + 1, 1, i)
                    finish(ch, i * 2, 0)
                    prepare(ch, i * 2 + 2, 0, i + 1)
                    finish(ch, i * 2 + 1, 1)
                    assert ch.n == SLOTS * K
                ch = Chain(dve, steps, base + (PAIRS - 1) * SLOTS * K)
                prepare(ch, NB - 1, 1, PAIRS - 1)
                finish(ch, NB - 2, 0)
                finish(ch, NB - 1, 1)

            @block.scalar
            def _(act):
                act.sem_inc(tp_free, 2)
                n = 0
                for dst in (src_col, lo_col, hi_col):
                    for b in range(GR):
                        act.wait_ge(tp_ready, n + 1)
                        nc.scalar.activation(dst[:, :].rearrange("p (r b) -> p b r", b=GR)[:, b, :], tp[n % 2][:, 0:P],
                                             ACT.Copy).then_inc(tp_free, 1)
                        n += 1
                act.wait_ge(tp_free, n + 2)
                act.sem_inc(cols_ready, 1)
                with act.Fori(0, NB) as i:
                    for t in range(GB):
                        act.wait_ge(live_ready, i * GB + t + 1)
                        nc.scalar.activation(seen[t % 2][:, :], live[:, :], ACT.Copy).then_inc(seen_ready, 1)

            @block.tensor
            def _(pe):
                pe.wait_ge(src_ready, 1)
                pe.sem_inc(hot_used, SLOTS)
                pe.sem_inc(sets_used, SLOTS)
                n = 0
                for src in (src_f, lo_f, hi_f):
                    for b in range(GR):
                        pe.wait_ge(tp_free, n + 1)
                        nc.tensor.transpose(tp[n % 2][:, 0:P], src[:, b * P:(b + 1) * P], pg.ident[:, :]).then_inc(tp_ready, 1)
                        n += 1
                nc.tensor.matmul(total[:, :], pg.zeros[:, 0:P], pg.zeros[:, 0:NT], start=True, stop=True)
                with pe.Fori(0, PAIRS) as i:
                    for b in range(SLOTS):
                        pe.wait_ge(hot_ready, (i * SLOTS + b) * 2 + 2)
                        for t in range(GB):
                            last = nc.tensor.matmul(total[:, :], one_lo[b][:, t, :], one_hi[b][:, t, :],
                                                    start=False, stop=True, skip_group_check=True)
                        last.then_inc(hot_used, 1)
                pe.wait_ge(hot_used, SLOTS + NB)
                pe.sem_inc(counted, 1)
                pe.wait_ge(prefix_in, 1)
                nc.tensor.matmul(total[:, :], ones[:, :], counts[:, :], start=True, stop=True)
                nc.tensor.matmul(live[:, :], before[:, :], counts[:, :], start=True, stop=True).then_inc(prefix_ready, 1)
                pe.wait_ge(first_ready, 1)
                nc.tensor.matmul(live[:, :], pg.ident[:, :], seed[:, :], start=True, stop=True).then_inc(live_ready, 1)
                with pe.Fori(0, PAIRS) as i:
                    for b in range(SLOTS):
                        n = i * SLOTS + b
                        pe.wait_ge(hot_ready, n * 2 + (2 * NB + 2))
                        pe.wait_ge(sets_ready, n + 1)
                        pe.wait_ge(rank_free, n + 1)
                        for t in range(GB):
                            pe.wait_ge(seen_ready, n * GB + t + 1)
                            nc.tensor.matmul(live[:, :], one_lo[b][:, t, :], one_hi[b][:, t, :],
                                             start=False, stop=True, skip_group_check=True).then_inc(live_ready, 1)
                            nc.tensor.matmul(rank[b][:, t, :], one_loT[b][:, t, :], seen[t % 2][:, :], start=True, stop=False)
                            last = nc.tensor.matmul(rank[b][:, t, :], same[b][:, t, :], one_hi[b][:, t, :], start=False, stop=True)
                        last.then_inc(rank_ready, 1)
                        pe.sem_inc(sets_used, 1)


EB = 8
EG = -(-N_EDGES // (P * EB))
E_FULL = N_EDGES // (P * EB)
E_TAIL = (N_EDGES - E_FULL * P * EB) // EB
WIN = 128
WINDOWS = -(-N_NODES // WIN)
EQ = EB // 2


def edge_groups(ap, tail=False):
    n = E_FULL * P * EB
    if tail:
        return ap[n:N_EDGES].rearrange("(p t) -> p t", t=EB)
    return ap[0:n].rearrange("(g p t) -> p g t", p=P, t=EB)


def stage_edges(pg):
    nc, a = pg.nc, pg.a
    with ExitStack() as st:
        sb = lambda n, s, d=F32: st.enter_context(nc.sbuf_tensor("e_" + n, s, d))
        pb = lambda n, s, d=F32: st.enter_context(nc.psum_tensor("e_" + n, s, d))
        src_raw, src_i = sb("src_raw", [P, EG, EB], I32), sb("src_i", [P, EG, EB], I32)
        dst_i, dst_f, node_f = sb("dst_i", [P, EG, EB], I32), sb("dst_f", [P, EG, EB]), sb("node_f", [P, EG, EB])
        ext, ext_n, ext_row = sb("ext", [P, 2, EG]), sb("ext_n", [EG, 2]), sb("ext_row", [1, 2, EG])
        more, more_sum, more_before = sb("more", [1, EG]), sb("more_sum", [1, EG]), sb("more_before", [1, EG])
        more_i = sb("more_i", [1, 2, EG], I32)
        table = sb("table", [1, 3, EG], I32)
        nodes = sb("nodes", [P, NPAD + WIN])
        w_edge = sb("w_edge", [P, C])
        index = [sb(f"index{b}", [P, EB], I32) for b in range(2)]
        xg = [sb(f"xg{b}", [P, EB, C]) for b in range(2)]
        ea = [sb(f"ea{b}", [P, EB, E_DIM]) for b in range(2)]
        eaT = [sb(f"eaT{b}", [P, EB, P]) for b in range(2)]
        msg = [sb(f"msg{b}", [P, EB, C]) for b in range(2)]
        hot = [sb(f"hot{b}", [P, EB, WIN]) for b in range(2)]
        hotx = sb("hotx", [P, EB, WIN])
        tp = [pb(f"tp{h}", [P, EB // 2, P]) for h in range(2)]
        pre = [pb(f"pre{q}", [P, 2, C]) for q in range(EQ)]
        part = [pb(f"part{b}", [P, 2, KC, WIN]) for b in range(2)]
        idx_init, idx_loaded, w_ready = pg.sem("e_idx_init"), pg.sem("e_idx_loaded"), pg.sem("e_w_ready")
        steps, src_ready, dst_fixed = pg.sem("e_steps"), pg.sem("e_src_ready"), pg.sem("e_dst_fixed")
        ext_ready, extT_ready, row_in, row_out = (pg.sem(n) for n in ("e_ext_ready", "e_extT_ready", "e_row_in", "e_row_out"))
        table_ready, nodes_ready = pg.sem("e_table_ready"), pg.sem("e_nodes_ready")
        dstf_ready = pg.sem("e_dstf_ready")
        index_ready, index_used = pg.sem("e_index_ready"), pg.sem("e_turns")
        gathered = [pg.sem(f"e_gathered{b}") for b in range(2)]
        ea_ready = [pg.sem(f"e_ea_ready{b}") for b in range(2)]
        tp_ready, eaT_ready, pre_ready = pg.sem("e_tp_ready"), pg.sem("e_eaT_ready"), pg.sem("e_pre_ready")
        msg_added, relu_done = pg.sem("e_msg_added"), pg.sem("e_relu_done")
        hot_ready, summed, added = pg.sem("e_hot_ready"), pg.sem("e_summed"), pg.sem("e_added")
        hotx_ready, summedx, addedx = pg.sem("e_hotx_ready"), pg.sem("e_summedx"), pg.sem("e_addedx")
        with nc.Block() as block:
            @block.sync
            def _(sp):
                sp.dma_start(w_edge[:, :], a["w_edge"]).then_inc(w_ready, 16)
                sp.wait_ge(idx_init, 2)
                sp.dma_start(dst_i[:, 0:E_FULL, :], edge_groups(a["dst"])).then_inc(idx_loaded, 16)
                sp.dma_start(src_raw[:, 0:E_FULL, :], edge_groups(a["src"])).then_inc(idx_loaded, 16)
                sp.dma_start(dst_i[0:E_TAIL, E_FULL, :], edge_groups(a["dst"], True)).then_inc(idx_loaded, 16)
                sp.dma_start(src_raw[0:E_TAIL, E_FULL, :], edge_groups(a["src"], True)).then_inc(idx_loaded, 16)

                def load(i, b, tail):
                    sp.wait_ge(tp_ready, (i * 2 + b) * 2 + 2)
                    if tail:
                        rows = a["edge_attr"][E_FULL * P * EB:N_EDGES, :].rearrange("(p t) d -> p t d", t=EB)
                        sp.dma_start(ea[b][0:E_TAIL, :, :], rows).then_inc(ea_ready[b], 16)
                    else:
                        rows = a["edge_attr"][bass.ds((i * 2 + b) * (P * EB), P * EB), :].rearrange("(p t) d -> p t d", t=EB)
                        sp.dma_start(ea[b][:, :, :], rows).then_inc(ea_ready[b], 16)

                with sp.Fori(0, EG // 2 - 1) as i:
                    load(i, 0, False)
                    load(i, 1, False)
                load(EG // 2 - 1, 0, False)
                load(EG // 2 - 1, 1, True)

            @block.gpsimd
            def _(pool):
                nc.gpsimd.memset(dst_i[:, :, :], N_NODES - 1).then_inc(idx_init, 1)
                nc.gpsimd.memset(src_raw[:, :, :], 0).then_inc(idx_init, 1)
                nc.gpsimd.iota(nodes[:, :], pattern=[[1, NPAD + WIN]], base=0, channel_multiplier=0,
                               allow_small_or_imprecise_dtypes=True).then_inc(nodes_ready, 1)
                nc.gpsimd.memset(pg.agg[:, :, :], 0.0).then_inc(nodes_ready, 1)
                pool.wait_ge(dstf_ready, 1)
                nc.gpsimd.affine_select(out=dst_f[:, EG - 1, :], in_=dst_f[:, EG - 1, :], compare_op=ALU.is_ge,
                                        fill=-1.0, base=E_TAIL - 1, pattern=[[0, EB]], channel_multiplier=-1).then_inc(dst_fixed, 1)
                pool.wait_ge(src_ready, 1)
                with pool.Fori(0, EG // 2) as i:
                    for b in range(2):
                        g = i * 2 + b
                        pool.wait_ge(msg_added, g * EQ + EQ)
                        nc.gpsimd.tensor_copy(index[b][:, :], src_i[:, bass.ds(g, 1), :].rearrange("p o t -> p (o t)")).then_inc(index_ready, 1)
                        pool.wait_ge(index_ready, g + 1)
                        pool.sem_inc(index_used, 1)
                        for t in range(EB):
                            pool.indirect_dma_start(out=xg[b][:, t, :], out_offset=None, in_=pg.xb_d,
                                                    in_offset=bass.IndirectOffsetOnAxis(ap=index[b][:, t:t + 1], axis=0)
                                                    ).then_inc(gathered[b], 16)

            @block.scalar
            def _(act):
                act.sem_inc(eaT_ready, 2)

                def copy_attributes(g, b):
                    for h in range(2):
                        act.wait_ge(tp_ready, g * 2 + h + 5)
                        nc.scalar.activation(eaT[b][:, h * EQ:(h + 1) * EQ, :], tp[h][:, :, :], ACT.Copy).then_inc(eaT_ready, 1)

                def rectify(g, b):
                    for h in range(2):
                        half = msg[b][:, h * EQ:(h + 1) * EQ, :]
                        act.wait_ge(msg_added, g * EQ + 2 * EQ + (h + 1) * EQ // 2)
                        nc.scalar.activation(half, half, ACT.Relu).then_inc(relu_done, 1)

                copy_attributes(0, 0)
                copy_attributes(1, 1)
                with act.Fori(0, EG // 2 - 1) as i:
                    for b in range(2):
                        rectify(i * 2 + b, b)
                        copy_attributes(i * 2 + (2 + b), b)
                rectify(EG - 2, 0)
                rectify(EG - 1, 1)

            @block.vector
            def _(dve):
                ch = Chain(dve, steps)
                dve.sem_inc(msg_added, 2 * EQ)
                dve.sem_inc(added, 2)
                dve.wait_ge(idx_loaded, 64)
                ch.add(nc.vector.tensor_copy(dst_f[:, :, :], dst_i[:, :, :]))
                ch(nc.vector.tensor_scalar_min(src_i[:, :, :], src_raw[:, :, :], float(N_NODES - 1)))
                dve.sem_inc(src_ready, 1)
                dve.sem_inc(dstf_ready, 1)
                ch(nc.vector.tensor_scalar(out=node_f[:, :, :], in0=dst_i[:, :, :], scalar1=0.0, scalar2=float(N_NODES - 1),
                                           op0=ALU.max, op1=ALU.min))
                ch.add(nc.vector.tensor_reduce(out=ext[:, 0, :], in_=node_f[:, :, :], axis=AX, op=ALU.min))
                ch(nc.vector.tensor_reduce(out=ext[:, 1, :], in_=node_f[:, :, :], axis=AX, op=ALU.max))
                dve.sem_inc(ext_ready, 1)
                dve.wait_ge(extT_ready, 1)
                ch(nc.vector.tensor_reduce(out=ext_n[:, 0:1], in_=pre[0][0:EG, 0, 0:P], axis=AX, op=ALU.min))
                ch(nc.vector.tensor_reduce(out=ext_n[:, 1:2], in_=pre[0][0:EG, 1, 0:P], axis=AX, op=ALU.max))
                dve.sem_inc(row_in, 1)
                dve.wait_ge(row_out, 1)
                ch(nc.vector.tensor_copy(ext_row[:, :, :], pre[1][0:1, :, 0:EG]))
                ch(nc.vector.tensor_tensor(out=more[:, :], in0=ext_row[:, 1, :], in1=ext_row[:, 0, :], op=ALU.subtract))
                ch(nc.vector.tensor_copy(more_i[:, 0, :], more[:, :]))
                ch(nc.vector.tensor_single_scalar(more_i[:, 1, :], more_i[:, 0, :], WIN.bit_length() - 1,
                                                  op=ALU.logical_shift_right))
                ch(nc.vector.tensor_copy(more[:, :], more_i[:, 1, :]))
                ch(nc.vector.tensor_tensor_scan(out=more_sum[:, :], data0=pg.ones_row[:, 0:EG], data1=more[:, :], initial=0.0,
                                                op0=ALU.mult, op1=ALU.add))
                ch(nc.vector.tensor_tensor(out=more_before[:, :], in0=more_sum[:, :], in1=more[:, :], op=ALU.subtract))
                ch.add(nc.vector.tensor_copy(table[:, 0, :], ext_row[:, 0, :]))
                ch.add(nc.vector.tensor_copy(table[:, 1, :], more[:, :]))
                ch(nc.vector.tensor_copy(table[:, 2, :], more_before[:, :]))
                dve.sem_inc(table_ready, 1)
                dve.wait_ge(dst_fixed, 1)
                dve.wait_ge(nodes_ready, 2)

                def one_hot(out, g, node):
                    return nc.vector.tensor_tensor(
                        out=out[:, :, :], in0=nodes[:, bass.ds(node, WIN)].unsqueeze(1).to_broadcast([P, EB, WIN]),
                        in1=dst_f[:, bass.ds(g, 1), :].rearrange("p o t -> p (o t)").unsqueeze(2).to_broadcast([P, EB, WIN]),
                        op=ALU.is_equal)

                def first_hot(g, b):
                    first = dve.value_load(table[0:1, 0, bass.ds(g, 1)], min_val=0, max_val=N_NODES - 1)
                    one_hot(hot[b], g, first).then_inc(hot_ready, 1)

                def messages(g, b, turn):
                    dve.wait_ge(gathered[b], turn * (16 * EB) + 16 * EB)
                    for q in range(EQ):
                        dve.wait_ge(pre_ready, g * EQ + q + 1)
                        nc.vector.tensor_tensor(out=msg[b][:, 2 * q:2 * q + 2, :], in0=pre[q][:, :, :],
                                                in1=xg[b][:, 2 * q:2 * q + 2, :], op=ALU.add).then_inc(msg_added, 1)

                def add_part(node, sums):
                    acc = pg.agg[:, :, bass.ds(node, WIN)]
                    return nc.vector.tensor_tensor(out=acc, in0=acc, in1=sums, op=ALU.add)

                window = lambda first, n: nc.s_assert_within(
                    first + n * WIN, 0, NPAD, skip_runtime_bounds_check_because=
                    "a group's last window starts at its largest destination or before")

                def finish_group(g, b, next_messages=None):
                    first = dve.value_load(table[0:1, 0, bass.ds(g, 1)], min_val=0, max_val=N_NODES - 1)
                    further = dve.value_load(table[0:1, 1, bass.ds(g, 1)], min_val=0, max_val=WINDOWS - 1)
                    before = dve.value_load(table[0:1, 2, bass.ds(g, 1)], min_val=0, max_val=EG * WINDOWS)
                    with dve.If(further > 0):
                        one_hot(hotx, g, window(first, 1)).then_inc(hotx_ready, 1)
                    if next_messages is not None:
                        messages(*next_messages)
                    dve.wait_ge(summed, g + 1)
                    add_part(first, part[b][:, 0, :, :]).then_inc(added, 1)
                    dve.wait_ge(added, g + 3)
                    dve.sem_inc(pg.turns, 1)
                    with dve.If(further > 0):
                        with dve.Fori(0, further) as j:
                            dve.wait_ge(summedx, before + j + 1)
                            dve.sem_inc(pg.turns, 1)
                            with dve.If(further > j + 1):
                                one_hot(hotx, g, window(first, j + 2)).then_inc(hotx_ready, 1)
                            add_part(window(first, j + 1), part[1 - b][:, 1, :, :]).then_inc(addedx, 1)
                            dve.wait_ge(addedx, before + j + 2)

                dve.sem_inc(addedx, 1)
                first_hot(0, 0)
                messages(0, 0, 0)
                with dve.Fori(0, EG // 2 - 1) as i:
                    for b in range(2):
                        g = i * 2 + b
                        first_hot(g + 1, 1 - b)
                        finish_group(g, b, (g + 1, 1 - b, i + b))
                first_hot(EG - 1, 1)
                finish_group(EG - 2, 0, (EG - 1, 1, EG // 2 - 1))
                finish_group(EG - 1, 1)

            @block.tensor
            def _(pe):
                pe.sem_inc(tp_ready, 4)
                pe.wait_ge(ext_ready, 1)
                for m in range(2):
                    last = nc.tensor.transpose(pre[0][0:EG, m, 0:P], ext[:, m, :], pg.ident[:, :])
                last.then_inc(extT_ready, 1)
                pe.wait_ge(row_in, 1)
                for m in range(2):
                    last = nc.tensor.transpose(pre[1][0:1, m, 0:EG], ext_n[:, m:m + 1], pg.ident[0:EG, 0:EG])
                last.then_inc(row_out, 1)
                pe.wait_ge(table_ready, 1)
                pe.wait_ge(w_ready, 16)

                def turn_attributes(i, b):
                    g = i * 2 + b
                    pe.wait_ge(ea_ready[b], i * 16 + 16)
                    for h in range(2):
                        pe.wait_ge(eaT_ready, g * 2 + h + 1)
                        for t in range(EQ):
                            last = nc.tensor.transpose(tp[h][:, t, :], ea[b][:, h * EQ + t, :], pg.ident[:, :])
                        last.then_inc(tp_ready, 1)

                def project(g, b):
                    for q in range(EQ):
                        if q % 2 == 0:
                            pe.wait_ge(eaT_ready, g * 2 + q // 2 + 3)
                        pe.wait_ge(msg_added, g * EQ + q + EQ + 1)
                        for t in range(2):
                            last = nc.tensor.matmul(pre[q][:, t, :], eaT[b][:, 2 * q + t, :], w_edge[:, :], start=True, stop=True)
                        last.then_inc(pre_ready, 1)

                def product(out, one_hots, b, h, t):
                    return nc.tensor.matmul(out[:, h, :], msg[b][:, t, h * P:(h + 1) * P], one_hots[:, t, :],
                                            start=(t == 0), stop=(t == EB - 1))

                def sum_group(g, b):
                    further = pe.value_load(table[0:1, 1, bass.ds(g, 1)], min_val=0, max_val=WINDOWS - 1)
                    before = pe.value_load(table[0:1, 2, bass.ds(g, 1)], min_val=0, max_val=EG * WINDOWS)
                    pe.wait_ge(hot_ready, g + 1)
                    pe.wait_ge(added, g + 1)
                    pe.wait_ge(addedx, before + 1)
                    for h in range(KC):
                        for t in range(EB):
                            if h == 0 and t % EQ == 0:
                                pe.wait_ge(relu_done, g * 2 + t // EQ + 1)
                            last = product(part[b][:, 0, :, :], hot[b], b, h, t)
                    last.then_inc(summed, 1)
                    with pe.If(further > 0):
                        with pe.Fori(0, further) as j:
                            pe.wait_ge(hotx_ready, before + j + 1)
                            pe.wait_ge(addedx, before + j + 1)
                            for h in range(KC):
                                for t in range(EB):
                                    last = product(part[1 - b][:, 1, :, :], hotx, b, h, t)
                            last.then_inc(summedx, 1)

                turn_attributes(0, 0)
                turn_attributes(0, 1)
                project(0, 0)
                with pe.Fori(0, EG // 2 - 1) as i:
                    for b in range(2):
                        project(i * 2 + (b + 1), 1 - b)
                        sum_group(i * 2 + b, b)
                        turn_attributes(i + 1, b)
                project(EG - 1, 1)
                sum_group(EG - 2, 0)
                sum_group(EG - 1, 1)


def row_of(ap, n):
    return ap.rearrange("(o c) -> o c", o=1).to_broadcast([P, n])


def col_of(ap):
    return ap.rearrange("(h p) -> p h", p=P)


def weights_of(ap):
    return ap.rearrange("(h p) n -> p h n", p=P)


def feature_block(nc, out, wT, xT, n):
    m, h = n // 2, n % 2
    for c in range(KC):
        last = nc.tensor.matmul(out[h][:, :], wT[:, c, m * P:(m + 1) * P], xT[:, c, h * HN:(h + 1) * HN],
                                start=(c == 0), stop=(c == KC - 1))
    return last


def apply_norm(nc, ch, out, rows, mv, rstd, gain, shift):
    for j in range(ST):
        ch.add(nc.vector.scalar_tensor_tensor(out=out[:, j, :], in0=rows[:, j, :], scalar=mv[:, j, 0:1], in1=gain[:, :],
                                              op0=ALU.subtract, op1=ALU.mult))
    ch.wait()
    for j in range(ST):
        ch.add(nc.vector.scalar_tensor_tensor(out=out[:, j, :], in0=out[:, j, :], scalar=rstd[:, j:j + 1], in1=shift[:, :],
                                              op0=ALU.mult, op1=ALU.add))
    ch.wait()


def stage_mix(pg):
    nc, a = pg.nc, pg.a
    with ExitStack() as st:
        sb = lambda n, s, d=F32: st.enter_context(nc.sbuf_tensor("m_" + n, s, d))
        pb = lambda n, s, d=F32: st.enter_context(nc.psum_tensor("m_" + n, s, d))
        wq, w1, w2 = (sb(n, [P, KC, C]) for n in ("wq", "w1", "w2"))
        b1 = sb("b1", [P, KC])
        b2, g1, be1, g2, be2 = (sb(n, [P, C]) for n in ("b2", "g1", "be1", "g2", "be2"))
        xT, xn = sb("xT", [P, KC, SN]), sb("xn", [P, ST, C])
        qpos, qexp, qT = (sb(n, [P, KC, SN]) for n in ("qpos", "qexp", "qT"))
        sums = sb("sums", [P, ST, KC, P + HH])
        z = sb("z", [P, ST, KC, HH])
        t, x1, rest, y, out = (sb(n, [P, ST, C]) for n in ("t", "x1", "rest", "y", "out"))
        x1T, hT = sb("x1T", [P, KC, SN]), sb("hT", [P, KC, SN])
        stats, mv, std, rstd = sb("stats", [P, ST, 6]), sb("mv", [P, ST, 2]), sb("std", [P, ST]), sb("rstd", [P, ST])
        fm = [pb(f"fm{i}", [P, HN]) for i in range(2)]
        att = [pb(f"att{i}", [P, KC, P + HH]) for i in range(2)]
        tp = [pb(f"tp{i}", [P, 512]) for i in range(2)]
        yp = [pb(f"yp{i}", [P, C]) for i in range(2)]
        w_ready, xT_loaded, xn_loaded = pg.sem("m_w_ready"), pg.sem("m_xT_loaded"), pg.sem("m_xn_loaded")
        steps, fm_ready, fm_free = pg.sem("m_steps"), pg.sem("m_fm_ready"), pg.sem("m_fm_free")
        q_ready, qT_ready = pg.sem("m_q_ready"), pg.sem("m_qT_ready")
        att_ready, att_free = pg.sem("m_att_ready"), pg.sem("m_att_free")
        sums_ready, sums_used = pg.sem("m_sums_ready"), pg.sem("m_sums_used")
        var_ready, std_ready, x1_ready = pg.sem("m_var_ready"), pg.sem("m_std_ready"), pg.sem("m_x1_ready")
        tp_ready, tp_free, x1T_ready = pg.sem("m_tp_ready"), pg.sem("m_tp_free"), pg.sem("m_x1T_ready")
        hT_ready, yp_ready, yp_free = pg.sem("m_hT_ready"), pg.sem("m_yp_ready"), pg.sem("m_yp_free")
        out_ready, out_stored, out_free = pg.sem("m_out_ready"), pg.sem("m_out_stored"), pg.sem("m_out_free")
        LAST = STEPS - 1
        hidden_base = lambda i: i * 8 + 8 if i is not LAST else LAST * 8 + 4
        second_root = lambda i: i * 2 + 3 if i is not LAST else LAST * 2 + 2
        with nc.Block() as block:
            @block.sync
            def _(sp):
                sp.dma_start(wq[:, :, :], weights_of(a["mix_wqkvT"][:, 0:C])).then_inc(w_ready, 16)
                sp.dma_start(w1[:, :, :], weights_of(a["mix_w1T"])).then_inc(w_ready, 16)
                sp.dma_start(w2[:, :, :], weights_of(a["mix_w2T"])).then_inc(w_ready, 16)
                with nc.allow_non_contiguous_dma(reason="two vectors of 256"):
                    sp.dma_start(b1[:, :], col_of(a["mix_b1"])).then_inc(w_ready, 16)
                for d, v in ((b2, "mix_b2"), (g1, "mix_g1"), (be1, "mix_be1"), (g2, "mix_g2"), (be2, "mix_be2")):
                    sp.dma_start(d[:, :], row_of(a[v], C)).then_inc(w_ready, 16)
                sp.sem_inc(out_free, 1)
                with sp.Fori(0, STEPS) as i:
                    sp.wait_ge(out_ready, i + 1)
                    sp.dma_start(node_rows(pg.mix_d, i), out[:, :, :]).then_inc(out_stored, 16)
                    sp.wait_ge(out_stored, i * 16 + 16)
                    sp.sem_inc(out_free, 1)

            @block.gpsimd
            def _(pool):
                scatter_batches(pg, pool, "m", SORT_BATCHES, MIX_BATCHES)

            @block.tensor
            def _(pe):
                pe.wait_ge(w_ready, 9 * 16)

                def queries(i, base):
                    pe.wait_ge(xT_loaded, i * 16 + 16)
                    for n in range(4):
                        pe.wait_ge(fm_free, base + (n + 1))
                        feature_block(nc, fm, wq, xT, n).then_inc(fm_ready, 1)

                def attention(i):
                    pe.wait_ge(qT_ready, i * 4 + 4)
                    for j in range(ST):
                        pe.wait_ge(att_free, i * ST + j + 1)
                        for h in range(KC):
                            last = nc.tensor.matmul(att[j % 2][:, h, :], qT[:, h, j * P:(j + 1) * P], pg.kv_blocks[:, h, :],
                                                    start=True, stop=True)
                        last.then_inc(att_ready, 1)

                def turn(i, ahead=True):
                    pe.wait_ge(x1_ready, i + 1)
                    transpose_rows(nc, pe, x1, pg.ident, tp, tp_ready, tp_free, i * NU)
                    pe.wait_ge(x1T_ready, i + 1)
                    for n in range(4):
                        pe.wait_ge(fm_free, hidden_base(i) + (n + 1))
                        feature_block(nc, fm, w1, x1T, n).then_inc(fm_ready, 1)
                    if ahead:
                        queries(i + 2, hidden_base(i) + 4)
                    pe.wait_ge(hT_ready, i * 4 + 4)
                    for j in range(ST):
                        pe.wait_ge(yp_free, i * ST + j + 1)
                        for c in range(KC):
                            last = nc.tensor.matmul(yp[j % 2][:, :], hT[:, c, j * P:(j + 1) * P], w2[:, c, :],
                                                    start=(c == 0), stop=(c == KC - 1))
                        last.then_inc(yp_ready, 1)
                    if ahead:
                        attention(i + 2)

                queries(0, 0)
                attention(0)
                queries(1, 4)
                attention(1)
                with pe.Fori(0, STEPS - 2) as i:
                    turn(i)
                turn(LAST - 1, False)
                turn(LAST, False)

            @block.scalar
            def _(act):
                act.sem_inc(tp_free, 2)
                act.sem_inc(fm_free, 2)
                act.sem_inc(att_free, 2)

                def load_xT(i):
                    act.dma_start(xT[:, :, :], feat_cols(pg.xT_d, i)).then_inc(xT_loaded, 16)

                def load_xn(i):
                    act.dma_start(xn[:, :, :], node_rows(pg.xn_d, i)).then_inc(xn_loaded, 16)

                def queries(i, base, first=False):
                    if not first:
                        act.wait_ge(qT_ready, i * 4)
                    for n in range(4):
                        m, h = n // 2, n % 2
                        act.wait_ge(fm_ready, base + (n + 1))
                        nc.scalar.activation(qexp[:, m, h * HN:(h + 1) * HN], fm[h][:, :], ACT.Exp).then_inc(q_ready, 1)
                        nc.scalar.activation(qpos[:, m, h * HN:(h + 1) * HN], fm[h][:, :], ACT.Relu).then_inc(q_ready, 1)
                        act.wait_ge(q_ready, i * 8 + (n * 2 + 2))
                        act.sem_inc(fm_free, 1)

                def attention(i):
                    act.wait_ge(sums_used, i + 1)
                    for j in range(ST):
                        act.wait_ge(att_ready, i * ST + j + 1)
                        nc.scalar.activation(sums[:, j, :, :], att[j % 2][:, :, :], ACT.Copy).then_inc(att_free, 1)
                    act.wait_ge(att_free, i * ST + ST + 2)
                    act.sem_inc(sums_ready, 1)

                def root(count):
                    act.wait_ge(var_ready, count)
                    nc.scalar.activation(std[:, :], rstd[:, :], ACT.Sqrt).then_inc(std_ready, 1)

                def turn(i, ahead, load_ahead):
                    for n in range(4):
                        m, h = n // 2, n % 2
                        act.wait_ge(fm_ready, hidden_base(i) + (n + 1))
                        nc.scalar.activation(hT[:, m, h * HN:(h + 1) * HN], fm[h][:, :], ACT.Gelu,
                                             bias=b1[:, m:m + 1]).then_inc(hT_ready, 1)
                        act.wait_ge(hT_ready, i * 4 + n + 1)
                        act.sem_inc(fm_free, 1)
                    if i is not LAST:
                        root(i * 2 + 2)
                    if ahead:
                        load_xn(i + 2)
                        queries(i + 2, hidden_base(i) + 4)
                        if load_ahead:
                            load_xT(i + 3)
                        attention(i + 2)
                    if i is not LAST:
                        copy_blocks(nc, act, x1T, tp, tp_ready, tp_free, x1T_ready, i * NU + NU)
                    root(second_root(i))

                load_xT(0)
                load_xn(0)
                act.wait_ge(w_ready, 9 * 16)
                queries(0, 0, True)
                load_xT(1)
                attention(0)
                root(1)
                load_xn(1)
                queries(1, 4)
                load_xT(2)
                attention(1)
                copy_blocks(nc, act, x1T, tp, tp_ready, tp_free, x1T_ready, 0)
                with act.Fori(0, STEPS - 3) as i:
                    turn(i, True, True)
                turn(STEPS - 3, True, False)
                turn(LAST - 1, False, False)
                turn(LAST, False, False)

            @block.vector
            def _(dve):
                dve.sem_inc(yp_free, 2)
                dve.sem_inc(sums_used, 1)
                dve.wait_ge(w_ready, 9 * 16)

                def queries(i, first=False):
                    if not first:
                        dve.wait_ge(att_ready, i * ST)
                    for n in range(4):
                        m, h = n // 2, n % 2
                        dve.wait_ge(q_ready, i * 8 + (n * 2 + 2))
                        nc.vector.scalar_tensor_tensor(out=qT[:, m, h * HN:(h + 1) * HN], in0=qexp[:, m, h * HN:(h + 1) * HN],
                                                       scalar=1.0, in1=qpos[:, m, h * HN:(h + 1) * HN], op0=ALU.min, op1=ALU.add
                                                       ).then_inc(qT_ready, 1)

                def first_norm(ch, i, count, first=False):
                    dve.wait_ge(sums_ready, i + 1)
                    ch(nc.vector.tensor_scalar_add(z[:, :, :, :], sums[:, :, :, P:P + HH], 1e-6))
                    ch(nc.vector.reciprocal(z[:, :, :, :], z[:, :, :, :]))
                    for h in range(KC):
                        ch.add(nc.vector.tensor_tensor(out=t[:, :, h * P:(h + 1) * P].rearrange("p j (g d) -> p j g d", g=HH),
                                                       in0=sums[:, :, h, 0:P].rearrange("p j (g d) -> p j g d", g=HH),
                                                       in1=z[:, :, h, :].unsqueeze(3).to_broadcast([P, ST, HH, HD]), op=ALU.mult))
                    ch.wait()
                    dve.sem_inc(sums_used, 1)
                    dve.wait_ge(xn_loaded, i * 16 + 16)
                    ch(nc.vector.tensor_tensor(out=t[:, :, :], in0=t[:, :, :], in1=xn[:, :, :], op=ALU.add))
                    norm_statistics(nc, dve, ch, pg.turns, t, stats, mv, rstd, var_ready, std, std_ready, count)
                    if not first:
                        dve.wait_ge(x1T_ready, i)
                    apply_norm(nc, ch, x1, t, mv, rstd, g1, be1)
                    dve.sem_inc(x1_ready, 1)

                def turn(base, i, ahead=True):
                    ch = Chain(dve, steps, base)
                    ch(nc.vector.tensor_tensor(out=rest[:, :, :], in0=x1[:, :, :],
                                               in1=b2[:, :].unsqueeze(1).to_broadcast([P, ST, C]), op=ALU.add))
                    if i is not LAST:
                        first_norm(ch, i + 1, i * 2 + 2)
                    if ahead:
                        queries(i + 2)
                    for j in range(ST):
                        dve.wait_ge(yp_ready, i * ST + j + 1)
                        ch(nc.vector.tensor_tensor(out=y[:, j, :], in0=rest[:, j, :], in1=yp[j % 2][:, :], op=ALU.add))
                        dve.sem_inc(yp_free, 1)
                    norm_statistics(nc, dve, ch, pg.turns, y, stats, mv, rstd, var_ready, std, std_ready, second_root(i))
                    dve.wait_ge(out_free, i + 1)
                    apply_norm(nc, ch, out, y, mv, rstd, g2, be2)
                    dve.sem_inc(out_ready, 1)
                    return ch.n

                queries(0, True)
                ch = Chain(dve, steps)
                first_norm(ch, 0, 1, True)
                queries(1)
                K = 1 + ch.n + ST + NORM_STEPS + 2 * ST
                with dve.Fori(0, STEPS - 2) as i:
                    n = turn(i * K + ch.n, i)
                    assert n == K
                turn(ch.n + (STEPS - 2) * K, LAST - 1, False)
                turn(ch.n + (STEPS - 1) * K, LAST, False)


def stage_gnn(pg):
    nc, a = pg.nc, pg.a
    pg.table_d = pg.dram("table_d", [NPAD, ROW]).ap()
    with ExitStack() as st:
        sb = lambda n, s, d=F32: st.enter_context(nc.sbuf_tensor("g_" + n, s, d))
        pb = lambda n, s, d=F32: st.enter_context(nc.psum_tensor("g_" + n, s, d))
        h2T = sb("h2T", [P, KC, NPAD])
        w1, w2 = sb("w1", [P, KC, C]), sb("w2", [P, KC, C])
        b1, b2, gamma, beta = (sb(n, [P, KC]) for n in ("b1", "b2", "gamma", "beta"))
        gain = sb("gain", [P, 1])
        scale, shift = sb("scale", [P, KC]), sb("shift", [P, KC])
        bstats, bmv, bvar, bstd = sb("bstats", [P, KC, 2 * STEPS, 6]), sb("bmv", [P, KC, 2]), sb("bvar", [P, KC]), sb("bstd", [P, KC])
        h0T = sb("h0T", [P, KC, SN])
        xT, hT = sb("xT", [P, KC, SN]), sb("hT", [P, KC, SN])
        fm = [pb(f"fm{i}", [P, HN]) for i in range(2)]
        tp = [pb(f"tp{i}", [P, 512]) for i in range(2)]
        tb = [pb(f"tb{i}", [P, 512]) for i in range(2)]
        gp = pb("gp", [P, ST, GF])
        w_ready, loaded, xT_free = pg.sem("g_w_ready"), pg.sem("g_loaded"), pg.sem("g_xT_free")
        steps, h0_ready, h0_used = pg.sem("g_steps"), pg.sem("g_h0_ready"), pg.sem("g_h0_used")
        bvar_ready = pg.sem("g_bvar_ready")
        fm_ready, fm_free, hT_ready, h2_ready = pg.sem("g_fm_ready"), pg.sem("g_fm_free"), pg.sem("g_hT_ready"), pg.sem("g_h2_ready")
        loops_out = pg.sem("g_loops_out")
        with nc.Block() as block:
            @block.gpsimd
            def _(pool):
                scatter_batches(pg, pool, "g", SORT_BATCHES + MIX_BATCHES, GNN_BATCHES)
                for t in range(NT):
                    pool.indirect_dma_start(out=pg.sorted_d, out_offset=bass.IndirectOffsetOnAxis(ap=pg.first[:, t:t + 1], axis=0),
                                            in_=pg.node_id[:, t:t + 1], in_offset=None).then_inc(loops_out, 16)
                pool.wait_ge(loops_out, 16 * NT)

            @block.sync
            def _(sp):
                sp.dma_start(w1[:, :, :], weights_of(a["gnn_w1"])).then_inc(w_ready, 16)
                sp.dma_start(w2[:, :, :], weights_of(a["gnn_w2"])).then_inc(w_ready, 16)
                with nc.allow_non_contiguous_dma(reason="vectors of 256"):
                    for d, v in ((b1, "gnn_b1"), (b2, "gnn_b2"), (gamma, "gnn_gamma"), (beta, "gnn_beta")):
                        sp.dma_start(d[:, :], col_of(a[v])).then_inc(w_ready, 16)
                sp.dma_start(gain[:, :], a["gnn_eps"].to_broadcast([P, 1])).then_inc(w_ready, 16)
                with sp.Fori(0, STEPS) as i:
                    sp.wait_ge(xT_free, i + 1)
                    sp.dma_start(xT[:, :, :], feat_cols(pg.xT_d, i)).then_inc(loaded, 16)

            @block.vector
            def _(dve):
                dve.sem_inc(xT_free, 1)
                dve.wait_ge(w_ready, 7 * 16)
                ch = Chain(dve, steps)
                ch(nc.vector.tensor_scalar_add(gain[:, :], gain[:, :], 1.0))
                with dve.Fori(0, STEPS) as i:
                    dve.wait_ge(loaded, i * 16 + 16)
                    dve.wait_ge(h0_used, i + 1)
                    nc.vector.scalar_tensor_tensor(out=h0T[:, :, :], in0=xT[:, :, :], scalar=gain[:, 0:1],
                                                   in1=pg.agg[:, :, bass.ds(i * SN, SN)], op0=ALU.mult, op1=ALU.add
                                                   ).then_inc(h0_ready, 1)
                    dve.wait_ge(h0_ready, i + 1)
                    dve.sem_inc(xT_free, 1)
                dve.wait_ge(h2_ready, 4 * STEPS)
                for m in range(KC):
                    for k in range(2 * STEPS):
                        ch.add(nc.vector.bn_stats(out=bstats[:, m, k, :], in_=h2T[:, m, k * HN:min((k + 1) * HN, N_NODES)]))
                ch.wait()
                for m in range(KC):
                    ch.add(nc.vector.bn_aggr(out=bmv[:, m, :], in_=bstats[:, m, :, :].rearrange("p k s -> p (k s)")))
                ch.wait()
                ch(nc.vector.tensor_scalar_add(bvar[:, :], bmv[:, :, 1], 1e-5))
                dve.sem_inc(bvar_ready, 1)
                dve.wait_ge(h2_ready, 4 * STEPS + 1)
                ch(nc.vector.reciprocal(bvar[:, :], bstd[:, :]))
                ch(nc.vector.tensor_tensor(out=scale[:, :], in0=bvar[:, :], in1=gamma[:, :], op=ALU.mult))
                ch(nc.vector.tensor_tensor(out=shift[:, :], in0=bmv[:, :, 0], in1=scale[:, :], op=ALU.mult))
                ch(nc.vector.tensor_tensor(out=shift[:, :], in0=beta[:, :], in1=shift[:, :], op=ALU.subtract))

            @block.scalar
            def _(act):
                act.sem_inc(fm_free, 2)
                act.wait_ge(w_ready, 7 * 16)
                with act.Fori(0, STEPS) as i:
                    for n in range(4):
                        m, h = n // 2, n % 2
                        act.wait_ge(fm_ready, i * 8 + n + 1)
                        nc.scalar.activation(hT[:, m, h * HN:(h + 1) * HN], fm[n % 2][:, :], ACT.Relu,
                                             bias=b1[:, m:m + 1]).then_inc(fm_free, 1)
                    act.wait_ge(fm_free, i * 8 + 6)
                    act.sem_inc(hT_ready, 1)
                    for n in range(4):
                        m, h = n // 2, n % 2
                        act.wait_ge(fm_ready, i * 8 + n + 5)
                        nc.scalar.activation(h2T[:, m, bass.ds(i * SN + h * HN, HN)], fm[n % 2][:, :], ACT.Identity,
                                             bias=b2[:, m:m + 1]).then_inc(fm_free, 1)
                    act.wait_ge(fm_free, i * 8 + 10)
                    act.sem_inc(h2_ready, 4)
                act.wait_ge(bvar_ready, 1)
                nc.scalar.activation(bstd[:, :], bvar[:, :], ACT.Sqrt).then_inc(h2_ready, 1)

            @block.tensor
            def _(pe):
                pe.sem_inc(h0_used, 1)
                pe.wait_ge(w_ready, 7 * 16)
                with pe.Fori(0, STEPS) as i:
                    pe.wait_ge(h0_ready, i + 1)
                    for n in range(4):
                        pe.wait_ge(fm_free, i * 8 + n + 1)
                        feature_block(nc, fm, w1, h0T, n).then_inc(fm_ready, 1)
                    pe.wait_ge(hT_ready, i + 1)
                    pe.sem_inc(h0_used, 1)
                    for n in range(4):
                        pe.wait_ge(fm_free, i * 8 + n + 5)
                        feature_block(nc, fm, w2, hT, n).then_inc(fm_ready, 1)

        x_in, mix, x2 = sb("x_in", [P, ST, C]), sb("mix", [P, ST, C]), sb("x2", [P, ST, C])
        x3, x3T, rT = sb("x3", [P, ST, C]), xT, hT
        stats, mv, std, rstd = sb("stats", [P, ST, 6]), sb("mv", [P, ST, 2]), sb("std", [P, ST]), sb("rstd", [P, ST])
        wg = sb("wg", [P, KC, GF])
        att_s, att_d = sb("att_s", [P, GF]), sb("att_d", [P, GF])
        trow, prod = sb("trow", [P, ST, ROW]), sb("prod", [P, ST, GF])
        w3_ready, in_ready, x_in_free = pg.sem("j_w_ready"), pg.sem("j_in_ready"), pg.sem("j_x_in_free")
        jsteps, rT_ready, rT_used = pg.sem("j_steps"), pg.sem("j_rT_ready"), pg.sem("j_rT_used")
        bp_ready, bp_free = pg.sem("j_bp_ready"), pg.sem("j_bp_free")
        var_ready, std_ready, x2_ready, x3_ready = pg.sem("j_var_ready"), pg.sem("j_std_ready"), pg.sem("j_x2_ready"), pg.sem("j_x3_ready")
        out_free, stored = pg.sem("j_out_free"), pg.sem("j_stored")
        tq_ready, tq_free, x3T_ready = pg.sem("j_tq_ready"), pg.sem("j_tq_free"), pg.sem("j_x3T_ready")
        gp_ready, trow_ready = pg.sem("j_gp_ready"), pg.sem("j_trow_ready")
        with nc.Block() as block:
            @block.sync
            def _(sp):
                sp.dma_start(wg[:, :, :], weights_of(a["w_gat"])).then_inc(w3_ready, 16)
                sp.dma_start(att_s[:, :], row_of(a["att_src"].rearrange("h e -> (h e)"), GF)).then_inc(w3_ready, 16)
                sp.dma_start(att_d[:, :], row_of(a["att_dst"].rearrange("h e -> (h e)"), GF)).then_inc(w3_ready, 16)
                with sp.Fori(0, STEPS) as i:
                    sp.wait_ge(x_in_free, i + 1)
                    sp.dma_start(x_in[:, :, :], node_rows(pg.xpad, i)).then_inc(in_ready, 16)
                    sp.dma_start(mix[:, :, :], node_rows(pg.mix_d, i)).then_inc(in_ready, 16)

            @block.gpsimd
            def _(pool):
                pool.sem_inc(out_free, 1)
                with pool.Fori(0, STEPS) as i:
                    pool.wait_ge(x2_ready, i + 1)
                    pool.dma_start(node_rows(pg.x2_d, i), x2[:, :, :]).then_inc(stored, 16)
                    pool.wait_ge(x3T_ready, i + 1)
                    pool.dma_start(feat_cols(pg.x3T_d, i), x3T[:, :, :]).then_inc(stored, 16)
                    pool.wait_ge(trow_ready, i + 1)
                    pool.dma_start(node_rows(pg.table_d, i), trow[:, :, :]).then_inc(stored, 16)
                    pool.wait_ge(stored, i * 48 + 48)
                    pool.sem_inc(out_free, 1)

            @block.scalar
            def _(act):
                act.sem_inc(tq_free, 2)
                act.sem_inc(bp_free, 2)
                with act.Fori(0, STEPS) as i:
                    act.wait_ge(rT_used, i + 1)
                    for m in range(KC):
                        nc.scalar.activation(rT[:, m, :], h2T[:, m, bass.ds(i * SN, SN)], ACT.Relu,
                                             bias=shift[:, m:m + 1], scale=scale[:, m:m + 1]).then_inc(rT_ready, 1)
                    act.wait_ge(var_ready, i + 1)
                    nc.scalar.activation(std[:, :], rstd[:, :], ACT.Sqrt).then_inc(std_ready, 1)
                    act.wait_ge(out_free, i + 1)
                    copy_blocks(nc, act, x3T, tp, tq_ready, tq_free, x3T_ready, i * NU)

            @block.tensor
            def _(pe):
                pe.sem_inc(rT_used, 1)
                pe.wait_ge(w3_ready, 48)
                with pe.Fori(0, STEPS) as i:
                    pe.wait_ge(rT_ready, i * 2 + 2)
                    for u, (q0, nq) in enumerate(UNITS):
                        pe.wait_ge(bp_free, i * NU + u + 1)
                        for q in range(q0, q0 + nq):
                            last = nc.tensor.transpose(tb[u % 2][:, (q - q0) * P:(q - q0 + 1) * P],
                                                       rT[:, q % KC, (q // KC) * P:(q // KC + 1) * P], pg.ident[:, :])
                        last.then_inc(bp_ready, 1)
                    pe.wait_ge(x2_ready, i + 1)
                    pe.sem_inc(rT_used, 1)
                    pe.wait_ge(x3_ready, i + 1)
                    transpose_rows(nc, pe, x3, pg.ident, tp, tq_ready, tq_free, i * NU)
                    pe.wait_ge(x3T_ready, i + 1)
                    pe.wait_ge(out_free, i + 1)
                    for j in range(ST):
                        for c in range(KC):
                            last = nc.tensor.matmul(gp[:, j, :], x3T[:, c, j * P:(j + 1) * P], wg[:, c, :],
                                                    start=(c == 0), stop=(c == KC - 1))
                    last.then_inc(gp_ready, 1)

            @block.vector
            def _(dve):
                dve.sem_inc(x_in_free, 1)
                dve.wait_ge(w3_ready, 48)
                ch = Chain(dve, jsteps)
                ch(nc.vector.memset(pg.starts[:, :, :], 0.0))
                ch(nc.vector.memset(pg.starts[:, :, 0:1], 1.0))
                K = NU + 1 + NORM_STEPS + ST + 4
                with dve.Fori(0, STEPS) as i:
                    ch = Chain(dve, jsteps, i * K + 2)
                    dve.wait_ge(in_ready, i * 32 + 32)
                    dve.wait_ge(out_free, i + 1)
                    x2f = x2[:, :, :].rearrange("p j c -> p (j c)")
                    xf = x_in[:, :, :].rearrange("p j c -> p (j c)")
                    for u, (q0, nq) in enumerate(UNITS):
                        dve.wait_ge(bp_ready, i * NU + u + 1)
                        ch(nc.vector.tensor_tensor(out=x2f[:, q0 * P:(q0 + nq) * P], in0=xf[:, q0 * P:(q0 + nq) * P],
                                                   in1=tb[u % 2][:, 0:nq * P], op=ALU.add))
                        dve.sem_inc(bp_free, 1)
                    ch(nc.vector.tensor_tensor(out=x2[:, :, :], in0=x2[:, :, :], in1=mix[:, :, :], op=ALU.add))
                    dve.sem_inc(x2_ready, 1)
                    dve.sem_inc(x_in_free, 1)
                    norm_statistics(nc, dve, ch, pg.turns, x2, stats, mv, rstd, var_ready, std, std_ready, i + 1)
                    normalise(nc, ch, x3, x2, mv, rstd)
                    dve.sem_inc(x3_ready, 1)
                    dve.wait_ge(gp_ready, i + 1)
                    ch(nc.vector.tensor_copy(trow[:, :, 0:GF], gp[:, :, :]))
                    for att, out in ((att_s, trow[:, :, GF:ROW]), (att_d, pg.starts[:, bass.ds(i * ST, ST), 1:1 + HEADS])):
                        if att is att_d:
                            ch.wait()
                        ch(nc.vector.tensor_tensor(out=prod[:, :, :], in0=trow[:, :, 0:GF],
                                                   in1=att[:, :].unsqueeze(1).to_broadcast([P, ST, GF]), op=ALU.mult))
                        red = nc.vector.tensor_reduce(out=out, in_=prod[:, :, :].rearrange("p j (h e) -> p j h e", h=HEADS),
                                                      axis=AX, op=ALU.add)
                        if att is att_s:
                            ch(red)
                        else:
                            red.then_inc(trow_ready, 1)
                            dve.wait_ge(trow_ready, i + 1)
                    assert ch.n == K, ch.n


GC = 29
NG = RUN // GC
assert RUN % GC == 0 and NG % 2 == 1 and NG >= STEPS * EXPERTS
PICK = 512 // (STATE + 1)


class HandOn:

    def __init__(self, pg, name, hand, give, giveT, carryT, carry):
        self.pg, self.hand, self.give, self.giveT, self.carryT, self.carry = pg, hand, give, giveT, carryT, carry
        self.give_ready, self.giveT_ready, self.carryT_ready, self.carry_ready = (
            pg.sem(f"{name}_{n}") for n in ("give_ready", "giveT_ready", "carryT_ready", "carry_ready"))

    def tensor(self, pe, n, w):
        nc, hand = self.pg.nc, self.hand
        pe.wait_ge(self.give_ready, n + 1)
        for m in range(2):
            last = nc.tensor.transpose(hand[0:w, m, :], self.give[:, m, 0:w], self.pg.ident[:, :])
        last.then_inc(self.giveT_ready, 1)
        pe.wait_ge(self.carryT_ready, n + 1)
        nc.tensor.transpose(hand[:, 2, 0:w], self.carryT[0:w, 0:P], self.pg.ident[0:w, 0:w]).then_inc(self.carry_ready, 1)

    def vector(self, dve, ch, n, w, op0, op1, initial):
        V, giveT, carryT = self.pg.nc.vector, self.giveT, self.carryT
        dve.sem_inc(self.give_ready, 1)
        dve.wait_ge(self.giveT_ready, n + 1)
        ch(V.tensor_copy(giveT[0:w, :, :], self.hand[0:w, 0:2, :]))
        ch(V.memset(carryT[0:w, 0:1], initial))
        ch(V.tensor_tensor_scan(out=carryT[0:w, 1:P + 1], data0=giveT[0:w, 0, :], data1=giveT[0:w, 1, :],
                                initial=initial, op0=op0, op1=op1))
        dve.sem_inc(self.carryT_ready, 1)
        dve.wait_ge(self.carry_ready, n + 1)
        ch(V.tensor_copy(self.carry[:, 0:w], self.hand[:, 2, 0:w]))


DEST_STEPS = 3 + 2 * HEADS + 1 + 4 + HEADS


def stage_attend(pg):
    nc, a = pg.nc, pg.a
    starts_d = pg.dram("starts_d", [P * RUN, START]).ap()
    with ExitStack() as st:
        sb = lambda n, s, d=F32: st.enter_context(nc.sbuf_tensor("a_" + n, s, d))
        pb = lambda n, s, d=F32: st.enter_context(nc.psum_tensor("a_" + n, s, d))
        order = sb("order", [P, RUN], I32)
        heads = sb("heads", [P, RUN, START])
        keep, fresh, junk = sb("keep", [P, RUN]), sb("fresh", [P, RUN]), sb("junk", [P, RUN])
        index = [sb(f"index{b}", [P, GC], I32) for b in range(2)]
        got = [sb(f"got{b}", [P, GC, ROW]) for b in range(2)]
        scaled = [sb(f"scaled{b}", [P, GC, STATE]) for b in range(2)]
        powers = sb("powers", [P, GC, 2 * HEADS])
        give, giveT = sb("give", [P, 2, ROW]), sb("giveT", [ROW, 2, P])
        carryT, carry = sb("carryT", [ROW, P + 1]), sb("carry", [P, ROW])
        hand = pb("hand", [P, 3, P])
        zeroed, scattered, loaded = pg.sem("a_zeroed"), pg.sem("a_scattered"), pg.sem("a_loaded")
        heads_ready, index_ready = pg.sem("a_heads_ready"), pg.sem("a_index_ready")
        gathered = [pg.sem(f"a_gathered{b}") for b in range(2)]
        got_used, exp_in, exp_out = pg.sem("a_got_used"), pg.sem("a_exp_in"), pg.sem("a_exp_out")
        scaled_ready = pg.sem("a_scaled_ready")
        stored = [pg.sem(f"a_stored{b}") for b in range(2)]
        hands = HandOn(pg, "a", hand, give, giveT, carryT, carry)
        steps = pg.sem("a_steps")
        CHUNK_STEPS = 11 + ROW
        with nc.Block() as block:
            @block.sync
            def _(sp):
                sp.dma_start(order[:, :], pg.sorted_d.rearrange("(p c) o -> p (c o)", p=P)).then_inc(loaded, 16)
                z = pg.zeros[:, 0:START * GC].unsqueeze(1).to_broadcast([P, NG, START * GC])
                sp.dma_start(starts_d.rearrange("(p c) k -> p (c k)", p=P).rearrange("p (r z) -> p r z", z=START * GC), z).then_inc(zeroed, 16)
                sp.wait_ge(scattered, 16 * NT)
                sp.dma_start(heads[:, :, :], starts_d.rearrange("(p c) k -> p c k", p=P)).then_inc(heads_ready, 16)

                def store(k, b):
                    sp.wait_ge(scaled_ready, k + 1)
                    sp.dma_start(pg.sums_d.rearrange("(p c) k -> p c k", p=P)[:, bass.ds(k * GC, GC), :],
                                 scaled[b][:, :, :]).then_inc(stored[b], 16)

                with sp.Fori(0, NG // 2) as i:
                    store(i * 2, 0)
                    store(i * 2 + 1, 1)
                store(NG - 1, 0)
                for b in range(2):
                    sp.wait_ge(stored[b], 16 * (NG // 2 + 1 - b))

            @block.gpsimd
            def _(pool):
                pool.wait_ge(zeroed, 16)
                for t in range(NT):
                    pool.indirect_dma_start(out=starts_d, out_offset=bass.IndirectOffsetOnAxis(ap=pg.first[:, t:t + 1], axis=0),
                                            in_=pg.starts[:, t, :], in_offset=None).then_inc(scattered, 16)
                pool.wait_ge(loaded, 16)

                def gather(i, b, first=False):
                    k = i * 2 + b
                    if not first:
                        pool.wait_ge(got_used, k - 1)
                    nc.gpsimd.tensor_copy(index[b][:, :], order[:, bass.ds(k * GC, GC)]).then_inc(index_ready, 1)
                    pool.wait_ge(index_ready, k + 1)
                    pool.sem_inc(pg.turns, 1)
                    for t in range(GC):
                        pool.indirect_dma_start(out=got[b][:, t, :], out_offset=None, in_=pg.table_d,
                                                in_offset=bass.IndirectOffsetOnAxis(ap=index[b][:, t:t + 1], axis=0)
                                                ).then_inc(gathered[b], 16)

                gather(0, 0, True)
                gather(0, 1, True)
                with pool.Fori(1, NG // 2) as i:
                    gather(i, 0)
                    gather(i, 1)
                gather(NG // 2, 0)

            def exponents(act, k):
                act.wait_ge(exp_in, k + 1)
                nc.scalar.activation(powers[:, :, :], powers[:, :, :], ACT.Exp).then_inc(exp_out, 1)

            def destination_logits(dve, ch):
                V = nc.vector
                dve.wait_ge(heads_ready, 16)
                ch.add(V.tensor_scalar(out=keep[:, :], in0=heads[:, :, 0], scalar1=-1.0, scalar2=1.0, op0=ALU.mult, op1=ALU.add))
                ch(V.tensor_scalar(out=fresh[:, :], in0=heads[:, :, 0], scalar1=-BIG, scalar2=None, op0=ALU.mult))
                ch(V.tensor_reduce(out=pg.whole[:, :], in_=keep[:, :], axis=AX, op=ALU.min))
                for h in range(HEADS):
                    ch(V.tensor_tensor_scan(out=junk[:, :], data0=keep[:, :], data1=heads[:, :, 1 + h], initial=0.0,
                                            op0=ALU.mult, op1=ALU.add))
                    ch(V.tensor_copy(give[:, 1, h:h + 1], junk[:, RUN - 1:RUN]))
                ch(V.tensor_copy(give[:, 0, 0:HEADS], pg.whole[:, 0:1].to_broadcast([P, HEADS])))
                hands.vector(dve, ch, 0, HEADS, ALU.mult, ALU.add, 0.0)
                for h in range(HEADS):
                    ch.add(V.tensor_tensor_scan(out=heads[:, :, 1 + h], data0=keep[:, :], data1=heads[:, :, 1 + h],
                                                initial=carry[:, h:h + 1], op0=ALU.mult, op1=ALU.add))
                ch.wait()

            def chunk(dve, ch, k, b, turn, first=False, fresh_slot=False):
                V = nc.vector
                cols = bass.ds(k * GC, GC)
                before, now = scaled[1 - b], scaled[b]
                logits, tops = got[b][:, :, GF:ROW], now[:, :, ROW:STATE]
                dve.wait_ge(gathered[b], turn * (16 * GC) + 16 * GC)
                if not fresh_slot:
                    dve.wait_ge(stored[b], turn * 16)
                ch(V.tensor_tensor(out=logits, in0=logits, in1=heads[:, cols, 1:1 + HEADS], op=ALU.add))
                ch(V.scalar_tensor_tensor(out=logits, in0=logits, scalar=0.2, in1=logits, op0=ALU.mult, op1=ALU.max))
                for h in range(HEADS):
                    ch.add(V.tensor_tensor_scan(out=now[:, :, ROW + h], data0=fresh[:, cols], data1=got[b][:, :, GF + h],
                                                initial=-BIG if first else before[:, GC - 1, ROW + h:ROW + h + 1],
                                                op0=ALU.add, op1=ALU.max))
                ch.wait()
                ch.add(V.tensor_tensor(out=powers[:, 1:GC, 0:HEADS], in0=tops[:, 0:GC - 1, :], in1=tops[:, 1:GC, :], op=ALU.subtract))
                if first:
                    ch.add(V.tensor_scalar(out=powers[:, 0, 0:HEADS], in0=tops[:, 0, :], scalar1=-1.0, scalar2=-BIG,
                                           op0=ALU.mult, op1=ALU.add))
                else:
                    ch.add(V.tensor_tensor(out=powers[:, 0, 0:HEADS], in0=before[:, GC - 1, ROW:STATE], in1=tops[:, 0, :], op=ALU.subtract))
                ch(V.tensor_tensor(out=powers[:, :, HEADS:], in0=logits, in1=tops, op=ALU.subtract))
                nc.vector.tensor_scalar_min(powers[:, :, :], powers[:, :, :], 0.0).then_inc(exp_in, 1)
                dve.wait_ge(exp_out, k + 1)
                ch.add(V.tensor_tensor(out=powers[:, :, 0:HEADS], in0=powers[:, :, 0:HEADS],
                                       in1=keep[:, cols].unsqueeze(2).to_broadcast([P, GC, HEADS]), op=ALU.mult))
                feats = got[b][:, :, 0:GF].rearrange("p c (h e) -> p c h e", h=HEADS)
                ch(V.tensor_tensor(out=feats, in0=feats, in1=powers[:, :, HEADS:].unsqueeze(3).to_broadcast([P, GC, HEADS, EXPERTS]),
                                   op=ALU.mult))
                for c in range(ROW):
                    h = c // EXPERTS if c < GF else c - GF
                    ch.add(V.tensor_tensor_scan(out=now[:, :, c], data0=powers[:, :, h],
                                                data1=got[b][:, :, c] if c < GF else powers[:, :, HEADS + h],
                                                initial=0.0 if first else before[:, GC - 1, c:c + 1], op0=ALU.mult, op1=ALU.add))
                ch.wait()
                dve.sem_inc(got_used, 1)
                dve.sem_inc(scaled_ready, 1)


            def scan_first(pe):
                hands.tensor(pe, 0, HEADS)

            before = DEST_STEPS

            def chunks_first(dve):
                ch = Chain(dve, steps)
                destination_logits(dve, ch)
                assert ch.n == before, ch.n

            def chunk_beside(dve, i, e, first=False):
                if first:
                    ch = Chain(dve, steps, before + e * CHUNK_STEPS)
                    chunk(dve, ch, e, e % 2, e // 2, e == 0, e < 2)
                else:
                    ch = Chain(dve, steps, before + (i * EXPERTS + e) * CHUNK_STEPS)
                    chunk(dve, ch, i * EXPERTS + e, e % 2, i * (EXPERTS // 2) + e // 2)
                assert ch.n == CHUNK_STEPS, ch.n

            def chunks_last(dve):
                done = STEPS * EXPERTS
                with dve.Fori(done // 2, NG // 2) as j:
                    for b in range(2):
                        chunk(dve, Chain(dve, steps, before + (j * 2 + b) * CHUNK_STEPS), j * 2 + b, b, j)
                ch = Chain(dve, steps, before + (NG - 1) * CHUNK_STEPS)
                chunk(dve, ch, NG - 1, 0, NG // 2)
                ch(nc.vector.tensor_copy(pg.run_end[:, :], scaled[0][:, GC - 1, :]))

            def exponents_last(act):
                with act.Fori(STEPS * EXPERTS, NG) as k:
                    exponents(act, k)

            experts(pg, block, st, scan_first, chunks_first, chunk_beside, chunks_last, exponents, exponents_last)


def stage_join(pg):
    nc = pg.nc
    last_d = pg.dram("last_d", [NT, P]).ap()
    with ExitStack() as st:
        sb = lambda n, s, d=F32: st.enter_context(nc.sbuf_tensor("o_" + n, s, d))
        pb = lambda n, s, d=F32: st.enter_context(nc.psum_tensor("o_" + n, s, d))
        local = sb("local", [P, NT, STATE])
        run_start, run_stop = sb("run_start", [P, 1]), sb("run_stop", [P, 1])
        last_f, first_f, lastT = sb("last_f", [P, NT]), sb("first_f", [P, NT]), sb("lastT", [NT, P])
        last_row, not_before, in_run = sb("last_row", [P, NPAD]), sb("not_before", [P, NPAD]), sb("in_run", [P, NPAD])
        give, giveT = sb("give", [P, 2, ROW]), sb("giveT", [ROW, 2, P])
        carryT, carry = sb("carryT", [ROW, P + 1]), sb("carry", [P, ROW])
        top = sb("top", [P, HEADS])
        scale = sb("scale", [P, 2 * HEADS])
        handed = sb("handed", [P, STATE + 1])
        ahead = sb("ahead", [P, NT, STATE + 1])
        starts_before = sb("starts_before", [P, NT])
        tops = sb("tops", [P, NT, HEADS])
        powers = sb("powers", [P, NT, 2 * HEADS])
        hand = pb("hand", [P, 3, P])
        picked = [pb(f"picked{b}", [P, PICK, STATE + 1]) for b in range(-(-NT // PICK))]
        hands = HandOn(pg, "o", hand, give, giveT, carryT, carry)
        run_ready, fetched, steps = pg.sem("o_run_ready"), pg.sem("o_fetched"), pg.sem("o_steps")
        last_ready, lastT_ready, lastT_out, row_ready = (
            pg.sem("o_" + n) for n in ("last_ready", "lastT_ready", "lastT_out", "row_ready"))
        lastT_stored = pg.sem("o_lastT_stored")
        exp_in, exp_out, table_ready = pg.sem("o_exp_in"), pg.sem("o_exp_out"), pg.sem("o_table_ready")
        picked_ready, ahead_ready = pg.sem("o_picked_ready"), pg.sem("o_ahead_ready")
        with nc.Block() as block:
            @block.gpsimd
            def _(pool):
                nc.gpsimd.iota(run_start[:, :], pattern=[[0, 1]], base=0, channel_multiplier=RUN,
                               allow_small_or_imprecise_dtypes=True).then_inc(run_ready, 1)
                for t in range(NT):
                    pool.indirect_dma_start(out=local[:, t, :], out_offset=None, in_=pg.sums_d,
                                            in_offset=bass.IndirectOffsetOnAxis(ap=pg.last[:, t:t + 1], axis=0)).then_inc(fetched, 16)

            @block.sync
            def _(sp):
                sp.wait_ge(lastT_out, 1)
                sp.dma_start(last_d, lastT[:, :]).then_inc(lastT_stored, 16)
                sp.wait_ge(lastT_stored, 16)
                sp.dma_start(last_row[:, :], row_of(last_d.rearrange("t p -> (t p)"), NPAD)).then_inc(row_ready, 16)

            @block.tensor
            def _(pe):
                pe.wait_ge(last_ready, 1)
                nc.tensor.transpose(picked[0][:, :, :].rearrange("p t k -> p (t k)")[0:NT, 0:P], last_f[:, :],
                                    pg.ident[:, :]).then_inc(lastT_ready, 1)
                hands.tensor(pe, 0, HEADS)
                hands.tensor(pe, 1, ROW)
                pe.wait_ge(table_ready, 1)
                for t in range(NT):
                    nc.tensor.matmul(picked[t // PICK][:, t % PICK, :], in_run[:, t * P:(t + 1) * P], handed[:, :],
                                     start=True, stop=True).then_inc(picked_ready, 1)

            @block.scalar
            def _(act):
                act.wait_ge(exp_in, 1)
                nc.scalar.activation(scale[:, :], scale[:, :], ACT.Exp).then_inc(exp_out, 1)
                for b in range(len(picked)):
                    n = min(PICK, NT - b * PICK)
                    act.wait_ge(picked_ready, b * PICK + n)
                    nc.scalar.activation(ahead[:, b * PICK:b * PICK + n, :], picked[b][:, 0:n, :], ACT.Copy).then_inc(ahead_ready, 1)
                act.wait_ge(exp_in, 2)
                nc.scalar.activation(powers[:, :, :], powers[:, :, :], ACT.Exp).then_inc(exp_out, 1)

            @block.vector
            def _(dve):
                ch = Chain(dve, steps)
                V = nc.vector
                ch.add(V.tensor_copy(first_f[:, :], pg.first[:, :]))
                ch(V.tensor_copy(last_f[:, :], pg.last[:, :]))
                dve.sem_inc(last_ready, 1)
                dve.wait_ge(lastT_ready, 1)
                ch(V.tensor_copy(lastT[:, :], picked[0][:, :, :].rearrange("p t k -> p (t k)")[0:NT, 0:P]))
                dve.sem_inc(lastT_out, 1)
                end_sums, end_tops = pg.run_end[:, 0:ROW], pg.run_end[:, ROW:STATE]
                ch.add(V.tensor_copy(give[:, 1, 0:HEADS], end_tops))
                ch(V.tensor_scalar(out=give[:, 0, 0:HEADS], in0=pg.whole[:, 0:1].to_broadcast([P, HEADS]), scalar1=-1.0,
                                   scalar2=BIG, op0=ALU.add, op1=ALU.mult))
                hands.vector(dve, ch, 0, HEADS, ALU.add, ALU.max, -BIG)
                ch.add(V.tensor_copy(handed[:, ROW:STATE], carry[:, 0:HEADS]))
                ch(V.tensor_tensor(out=top[:, :], in0=carry[:, 0:HEADS], in1=give[:, 0, 0:HEADS], op=ALU.add))
                ch(V.tensor_tensor(out=top[:, :], in0=top[:, :], in1=end_tops, op=ALU.max))
                ch.add(V.tensor_tensor(out=scale[:, 0:HEADS], in0=carry[:, 0:HEADS], in1=top[:, :], op=ALU.subtract))
                ch(V.tensor_tensor(out=scale[:, HEADS:], in0=end_tops, in1=top[:, :], op=ALU.subtract))
                ch(V.tensor_scalar_min(scale[:, :], scale[:, :], 0.0))
                dve.sem_inc(exp_in, 1)
                dve.wait_ge(exp_out, 1)
                ch.add(V.tensor_scalar(out=give[:, 0, GF:ROW], in0=scale[:, 0:HEADS], scalar1=pg.whole[:, 0:1], scalar2=None, op0=ALU.mult))
                ch.add(V.tensor_tensor(out=give[:, 1, GF:ROW], in0=end_sums[:, GF:ROW], in1=scale[:, HEADS:], op=ALU.mult))
                ch(V.tensor_tensor(out=give[:, 1, 0:GF].rearrange("p (h e) -> p h e", h=HEADS),
                                   in0=end_sums[:, 0:GF].rearrange("p (h e) -> p h e", h=HEADS),
                                   in1=scale[:, HEADS:].unsqueeze(2).to_broadcast([P, HEADS, EXPERTS]), op=ALU.mult))
                ch(V.tensor_copy(give[:, 0, 0:GF].rearrange("p (h e) -> p h e", h=HEADS),
                                 give[:, 0, GF:ROW].unsqueeze(2).to_broadcast([P, HEADS, EXPERTS])))
                hands.vector(dve, ch, 1, ROW, ALU.mult, ALU.add, 0.0)
                dve.wait_ge(run_ready, 1)
                ch.add(V.tensor_copy(handed[:, 0:ROW], carry[:, :]))
                ch.add(V.tensor_copy(handed[:, STATE:STATE + 1], run_start[:, :]))
                ch(V.tensor_scalar_add(run_stop[:, :], run_start[:, :], float(RUN)))
                dve.wait_ge(row_ready, 16)
                ch(V.tensor_scalar(out=not_before[:, :], in0=last_row[:, :], scalar1=run_start[:, 0:1], scalar2=None, op0=ALU.is_ge))
                ch(V.scalar_tensor_tensor(out=in_run[:, :], in0=last_row[:, :], scalar=run_stop[:, 0:1], in1=not_before[:, :],
                                          op0=ALU.is_lt, op1=ALU.mult))
                dve.sem_inc(table_ready, 1)
                dve.wait_ge(ahead_ready, len(picked))
                ch(V.tensor_tensor(out=starts_before[:, :], in0=first_f[:, :], in1=ahead[:, :, STATE], op=ALU.is_lt))
                ch(V.tensor_scalar(out=starts_before[:, :], in0=starts_before[:, :], scalar1=-1.0, scalar2=BIG, op0=ALU.add, op1=ALU.mult))
                before_tops = ahead[:, :, ROW:STATE]
                ch(V.tensor_tensor(out=before_tops, in0=before_tops, in1=starts_before[:, :].unsqueeze(2).to_broadcast([P, NT, HEADS]),
                                   op=ALU.add))
                dve.wait_ge(fetched, 16 * NT)
                ch(V.tensor_tensor(out=tops[:, :, :], in0=before_tops, in1=local[:, :, ROW:STATE], op=ALU.max))
                ch.add(V.tensor_tensor(out=powers[:, :, 0:HEADS], in0=before_tops, in1=tops[:, :, :], op=ALU.subtract))
                ch(V.tensor_tensor(out=powers[:, :, HEADS:], in0=local[:, :, ROW:STATE], in1=tops[:, :, :], op=ALU.subtract))
                dve.sem_inc(exp_in, 1)
                dve.wait_ge(exp_out, 2)
                for rows, h0 in ((ahead, 0), (local, HEADS)):
                    factor = powers[:, :, h0:h0 + HEADS]
                    feats = rows[:, :, 0:GF].rearrange("p t (h e) -> p t h e", h=HEADS)
                    ch.add(V.tensor_tensor(out=feats, in0=feats, in1=factor.unsqueeze(3).to_broadcast([P, NT, HEADS, EXPERTS]), op=ALU.mult))
                    ch.add(V.tensor_tensor(out=rows[:, :, GF:ROW], in0=rows[:, :, GF:ROW], in1=factor, op=ALU.mult))
                ch.wait()
                ch(V.tensor_tensor(out=pg.sums[:, :, :], in0=ahead[:, :, 0:ROW], in1=local[:, :, 0:ROW], op=ALU.add))


def stage_gate(pg):
    nc, a = pg.nc, pg.a
    with ExitStack() as st:
        sb = lambda n, s, d=F32: st.enter_context(nc.sbuf_tensor("t_" + n, s, d))
        bias, gain, shift = (sb(n, [P, GF]) for n in ("bias", "gain", "shift"))
        den, agg, sq = sb("den", [P, NT, HEADS]), sb("agg", [P, NT, GF]), sb("sq", [P, NT, GF])
        mean, var, std = sb("mean", [P, NT]), sb("var", [P, NT]), sb("std", [P, NT])
        score, ahead, cmp = sb("score", [P, NT, EXPERTS]), sb("ahead", [P, NT, EXPERTS]), sb("cmp", [P, NT])
        most, total = sb("most", [P, NT]), sb("total", [P, NT])
        loaded, steps = pg.sem("t_loaded"), pg.sem("t_steps")
        var_ready, std_ready, exp_in, exp_out = pg.sem("t_var_ready"), pg.sem("t_std_ready"), pg.sem("t_exp_in"), pg.sem("t_exp_out")
        with nc.Block() as block:
            @block.sync
            def _(sp):
                for d, v in ((bias, "b_gat"), (gain, "ln_gamma"), (shift, "ln_beta")):
                    sp.dma_start(d[:, :], row_of(a[v], GF)).then_inc(loaded, 16)
                sp.wait_ge(loaded, 48)

            @block.scalar
            def _(act):
                act.wait_ge(var_ready, 1)
                nc.scalar.activation(std[:, :], var[:, :], ACT.Sqrt).then_inc(std_ready, 1)
                act.wait_ge(exp_in, 1)
                nc.scalar.activation(score[:, :, :], score[:, :, :], ACT.Exp).then_inc(exp_out, 1)

            @block.vector
            def _(dve):
                ch = Chain(dve, steps)
                V = nc.vector
                nodes = lambda v: v[:, :].unsqueeze(1).to_broadcast([P, NT, GF])
                wide = lambda v, n: v[:, :].unsqueeze(2).to_broadcast([P, NT, n])
                dve.wait_ge(loaded, 48)
                ch(V.tensor_scalar_add(den[:, :, :], pg.sums[:, :, GF:ROW], 1e-16))
                ch(V.reciprocal(den[:, :, :], den[:, :, :]))
                ch(V.tensor_tensor(out=agg[:, :, :].rearrange("p t (h e) -> p t h e", h=HEADS),
                                   in0=pg.sums[:, :, 0:GF].rearrange("p t (h e) -> p t h e", h=HEADS),
                                   in1=den[:, :, :].unsqueeze(3).to_broadcast([P, NT, HEADS, EXPERTS]), op=ALU.mult))
                ch(V.tensor_tensor(out=agg[:, :, :], in0=agg[:, :, :], in1=nodes(bias), op=ALU.add))
                ch(V.tensor_reduce(out=mean[:, :], in_=agg[:, :, :], axis=AX, op=ALU.add))
                ch(V.tensor_scalar_mul(mean[:, :], mean[:, :], 1.0 / GF))
                ch(V.tensor_tensor(out=agg[:, :, :], in0=agg[:, :, :], in1=wide(mean, GF), op=ALU.subtract))
                ch(V.tensor_tensor(out=sq[:, :, :], in0=agg[:, :, :], in1=agg[:, :, :], op=ALU.mult))
                ch(V.tensor_reduce(out=var[:, :], in_=sq[:, :, :], axis=AX, op=ALU.add))
                ch(V.tensor_scalar(out=var[:, :], in0=var[:, :], scalar1=1.0 / GF, scalar2=LN_EPS, op0=ALU.mult, op1=ALU.add))
                dve.sem_inc(var_ready, 1)
                dve.wait_ge(std_ready, 1)
                ch(V.reciprocal(var[:, :], std[:, :]))
                ch(V.tensor_tensor(out=agg[:, :, :], in0=agg[:, :, :], in1=wide(var, GF), op=ALU.mult))
                ch(V.tensor_tensor(out=agg[:, :, :], in0=agg[:, :, :], in1=nodes(gain), op=ALU.mult))
                ch(V.tensor_tensor(out=agg[:, :, :], in0=agg[:, :, :], in1=nodes(shift), op=ALU.add))
                ch(V.tensor_reduce(out=score[:, :, :], in_=agg[:, :, :].rearrange("p t (h e) -> p t e h", h=HEADS), axis=AX, op=ALU.add))
                ch(V.tensor_scalar_mul(score[:, :, :], score[:, :, :], 1.0 / HEADS))
                ch(V.memset(ahead[:, :, :], 0.0))
                for e in range(EXPERTS):
                    for o in range(EXPERTS):
                        if o != e:
                            ch(V.tensor_tensor(out=cmp[:, :], in0=score[:, :, o], in1=score[:, :, e],
                                               op=ALU.is_ge if o < e else ALU.is_gt))
                            ch(V.tensor_tensor(out=ahead[:, :, e], in0=ahead[:, :, e], in1=cmp[:, :], op=ALU.add))
                ch(V.tensor_scalar(out=ahead[:, :, :], in0=ahead[:, :, :], scalar1=1.5, scalar2=None, op0=ALU.is_lt))
                ch(V.tensor_reduce(out=most[:, :], in_=score[:, :, :], axis=AX, op=ALU.max))
                ch(V.tensor_tensor(out=score[:, :, :], in0=score[:, :, :], in1=wide(most, EXPERTS), op=ALU.subtract))
                dve.sem_inc(exp_in, 1)
                dve.wait_ge(exp_out, 1)
                ch(V.tensor_tensor(out=score[:, :, :], in0=score[:, :, :], in1=ahead[:, :, :], op=ALU.mult))
                ch(V.tensor_reduce(out=total[:, :], in_=score[:, :, :], axis=AX, op=ALU.add))
                ch(V.reciprocal(total[:, :], total[:, :]))
                ch(V.tensor_tensor(out=pg.gate[:, :, :], in0=score[:, :, :], in1=wide(total, EXPERTS), op=ALU.mult))


def experts(pg, block, st, tensor_first, vector_first, vector_beside, vector_last, scalar_beside, scalar_last):
    nc, a = pg.nc, pg.a
    pg.y_d = pg.dram("y_d", [EXPERTS, NPAD, C]).ap()
    sb = lambda n, s, d=F32: st.enter_context(nc.sbuf_tensor("x_" + n, s, d))
    pb = lambda n, s, d=F32: st.enter_context(nc.psum_tensor("x_" + n, s, d))
    w1, w2 = sb("w1", [P, EXPERTS, KC, FF]), sb("w2", [P, EXPERTS, FC, C])
    b1, b2 = sb("b1", [P, EXPERTS, FC]), sb("b2", [P, EXPERTS, C])
    xT = sb("xT", [P, KC, SN])
    hT = [sb(f"hT{b}", [P, FC, SN]) for b in range(2)]
    y = [sb(f"y{b}", [P, ST, C]) for b in range(2)]
    hp = [pb(f"hp{i}", [P, HN]) for i in range(4)]
    yp = [pb(f"yp{i}", [P, C]) for i in range(2)]
    w_ready, xT_ready = pg.sem("x_w_ready"), pg.sem("x_xT_ready")
    hp_ready, hp_free, hT_ready, hT_used = pg.sem("x_hp_ready"), pg.sem("x_hp_free"), pg.sem("x_hT_ready"), pg.sem("x_hT_used")
    yp_ready, yp_free, y_ready = pg.sem("x_yp_ready"), pg.sem("x_yp_free"), pg.sem("x_y_ready")
    y_stored = [pg.sem(f"x_y_stored{b}") for b in range(2)]
    y_free, xT_used = pg.sem("x_y_free"), pg.sem("x_xT_used")
    UN = FC * 2

    @block.scalar
    def _(act):
        for e in range(EXPERTS):
            act.dma_start(w1[:, e, :, :], weights_of(a["ffn_w1"][e])).then_inc(w_ready, 16)
            act.dma_start(w2[:, e, :, :], a["ffn_w2"][e].rearrange("(f p) n -> p f n", p=P)).then_inc(w_ready, 16)
            with nc.allow_non_contiguous_dma(reason="vectors of 512"):
                act.dma_start(b1[:, e, :], a["ffn_b1"][e].rearrange("(f p) -> p f", p=P)).then_inc(w_ready, 16)
            act.dma_start(b2[:, e, :], row_of(a["ffn_b2"][e], C)).then_inc(w_ready, 16)
        act.dma_start(xT[:, :, :], feat_cols(pg.x3T_d, 0)).then_inc(xT_ready, 16)
        act.sem_inc(hp_free, 4)
        act.sem_inc(y_free, 2)
        act.wait_ge(w_ready, 4 * EXPERTS * 16)

        def store(i, e):
            k = i * EXPERTS + e
            act.wait_ge(y_ready, k + 1)
            act.dma_start(node_rows(pg.y_d[e], i), y[e % 2][:, :, :]).then_inc(y_stored[e % 2], 16)

        def hidden(i, e):
            act.wait_ge(hT_used, i * EXPERTS + e + 1)
            for n in range(UN):
                f, h = n // 2, n % 2
                k = (i * EXPERTS + e) * UN + n + 1
                act.wait_ge(hp_ready, k)
                nc.scalar.activation(hT[e % 2][:, f, h * HN:(h + 1) * HN], hp[n % 4][:, :], ACT.Gelu,
                                     bias=b1[:, e, f:f + 1]).then_inc(hT_ready, 1)
                act.wait_ge(hT_ready, k)
                act.sem_inc(hp_free, 1)

        def step(i, first, last):
            for e in range(EXPERTS):
                hidden(i, e)
                scalar_beside(act, i * EXPERTS + e)
                if e == EXPERTS - 1 and not last:
                    act.dma_start(xT[:, :, :], feat_cols(pg.x3T_d, i + 1)).then_inc(xT_ready, 16)
                if e > 0 or not first:
                    p = (e - 1) % EXPERTS
                    k = i * EXPERTS + e - 1
                    act.wait_ge(y_ready, k + 1)
                    act.dma_start(node_rows(pg.y_d[p], i if e else i - 1), y[p % 2][:, :, :]).then_inc(y_stored[p % 2], 16)
                    act.wait_ge(y_stored[p % 2], ((k // 2) if first else i * (EXPERTS // 2) + (e - 1) // 2) * 16 + 16)
                    act.sem_inc(y_free, 1)

        step(0, True, False)
        with act.Fori(1, STEPS - 1) as i:
            step(i, False, False)
        step(STEPS - 1, False, True)
        store(STEPS - 1, EXPERTS - 1)
        scalar_last(act)
        act.wait_ge(y_stored[1], STEPS * EXPERTS // 2 * 16)

    @block.tensor
    def _(pe):
        pe.sem_inc(hT_used, 2)
        tensor_first(pe)
        pe.wait_ge(w_ready, 4 * EXPERTS * 16)

        def up(i, e):
            for n in range(UN):
                f, h = n // 2, n % 2
                pe.wait_ge(hp_free, (i * EXPERTS + e) * UN + n + 1)
                for c in range(KC):
                    last = nc.tensor.matmul(hp[n % 4][:, :], w1[:, e, c, f * P:(f + 1) * P],
                                            xT[:, c, h * HN:(h + 1) * HN], start=(c == 0), stop=(c == KC - 1))
                last.then_inc(hp_ready, 1)

        def down(i, e):
            k = i * EXPERTS + e
            pe.wait_ge(hT_ready, k * UN + UN)
            for j in range(ST):
                pe.wait_ge(yp_free, k * ST + j + 1)
                for f in range(FC):
                    last = nc.tensor.matmul(yp[(e * ST + j) % 2][:, :], hT[e % 2][:, f, j * P:(j + 1) * P], w2[:, e, f, :],
                                            start=(f == 0), stop=(f == FC - 1))
                last.then_inc(yp_ready, 1)
            pe.wait_ge(yp_ready, k * ST + ST)
            pe.sem_inc(hT_used, 1)

        def step(i, first):
            pe.wait_ge(xT_ready, i * 16 + 16)
            for e in range(EXPERTS):
                up(i, e)
                if e > 0:
                    down(i, e - 1)
            down(i, EXPERTS - 1)

        with pe.Fori(0, STEPS) as i:
            step(i, False)

    @block.vector
    def _(dve):
        dve.sem_inc(yp_free, 2)
        vector_first(dve)
        dve.wait_ge(w_ready, 4 * EXPERTS * 16)

        def outputs(i, e):
            k = i * EXPERTS + e
            dve.wait_ge(y_free, k + 1)
            for j in range(ST):
                dve.wait_ge(yp_ready, k * ST + j + 1)
                nc.vector.tensor_tensor(out=y[e % 2][:, j, :], in0=yp[(e * ST + j) % 2][:, :], in1=b2[:, e, :],
                                        op=ALU.add).then_inc(yp_free, 1)
            dve.wait_ge(yp_free, k * ST + ST + 2)
            dve.sem_inc(y_ready, 1)

        for e in range(EXPERTS):
            vector_beside(dve, 0, e, True)
            outputs(0, e)
        with dve.Fori(1, STEPS) as i:
            for e in range(EXPERTS):
                vector_beside(dve, i, e)
                outputs(i, e)
        vector_last(dve)


def stage_combine(pg, out):
    nc, a = pg.nc, pg.a
    with ExitStack() as st:
        sb = lambda n, s, d=F32: st.enter_context(nc.sbuf_tensor("c_" + n, s, d))
        y = [sb(f"y{b}", [P, EXPERTS, ST, C]) for b in range(2)]
        acc = [sb(f"acc{b}", [P, ST, C]) for b in range(2)]
        y_ready = [pg.sem(f"c_y_ready{b}") for b in range(2)]
        y_free, done, added = pg.sem("c_y_free"), pg.sem("c_done"), pg.sem("c_added")
        saved = [pg.sem(f"c_saved{b}") for b in range(2)]
        final = pg.sem("c_final")
        with nc.Block() as block:
            @block.sync
            def _(sp):
                for i in range(STEPS):
                    if i >= 2:
                        sp.wait_ge(done, i - 1)
                        sp.wait_ge(saved[i % 2], (i // 2) * 16)
                    for e in range(EXPERTS):
                        sp.dma_start(y[i % 2][:, e, :, :], node_rows(pg.y_d[e], i)).then_inc(y_ready[i % 2], 16)
                    sp.dma_start(acc[i % 2][:, :, :], node_rows(pg.x2_d, i)).then_inc(y_ready[i % 2], 16)

            @block.vector
            def _(dve):
                n = 0
                for i in range(STEPS):
                    dve.wait_ge(y_ready[i % 2], (i // 2 + 1) * 16 * (EXPERTS + 1))
                    for e in range(EXPERTS):
                        for j in range(ST):
                            nc.vector.scalar_tensor_tensor(
                                out=acc[i % 2][:, j, :], in0=y[i % 2][:, e, j, :], scalar=pg.gate[:, i * ST + j, e:e + 1],
                                in1=acc[i % 2][:, j, :], op0=ALU.mult, op1=ALU.add).then_inc(added, 1)
                            n += 1
                        dve.wait_ge(added, n)
                    dve.sem_inc(done, 1)

            @block.scalar
            def _(act):
                for i in range(STEPS):
                    act.wait_ge(done, i + 1)
                    full = min(ST, (N_NODES - i * SN) // P)
                    act.dma_start(out[i * SN:i * SN + full * P, :].rearrange("(j p) c -> p j c", p=P),
                                  acc[i % 2][:, 0:full, :]).then_inc(saved[i % 2], 16)
                rest = N_NODES - (NT - 1) * P
                act.dma_start(out[N_NODES - rest:N_NODES, :], acc[(STEPS - 1) % 2][0:rest, ST - 1, :]).then_inc(final, 16)
                act.wait_ge(saved[0], (STEPS + 1) // 2 * 16)
                act.wait_ge(saved[1], STEPS // 2 * 16)
                act.wait_ge(final, 16)


def gps_layer_kernel(nc, out, **args):
    with ExitStack() as stack:
        pg = Program(nc, args, stack)
        setup(pg)
        stage_norm(pg)
        pg.end_stage()
        with ExitStack() as st:
            hold = lambda n, s, d: st.enter_context(nc.sbuf_tensor(n, s, d))
            pg.src_col, pg.place_col = hold("src_col", [P, GT], I32), hold("place_col", [P, GT], I32)
            pg.place = [hold(f"place{i}", [P, GB], I32) for i in range(SLOTS)]
            pg.source = [hold(f"source{i}", [P, GB], I32) for i in range(SLOTS)]
            pg.node_id = hold("node_id", [P, NT], I32)
            stage_sort(pg)
            pg.end_stage()
            pg.agg = hold("agg", [P, KC, NPAD + WIN], F32)
            stage_edges(pg)
            pg.end_stage()
            stage_mix(pg)
            pg.end_stage()
            stage_gnn(pg)
            pg.end_stage()
        stage_attend(pg)
        pg.end_stage()
        stage_join(pg)
        pg.end_stage()
        stage_gate(pg)
        stage_combine(pg, out)


def kernel(**inputs):
    import concourse.bacc as _bacc
    from concourse.bass_utils import run_bass_kernel_spmd as _run

    nc = _bacc.Bacc("TRN2", target_bir_lowering=False, num_devices=1)
    arrays, aps = {}, {}
    for name, value in layout(inputs).items():
        arrays[name] = value
        aps[name] = nc.dram_tensor(name, value.shape, mybir.dt.from_np(value.dtype), kind="ExternalInput").ap()
    out = nc.dram_tensor("out", (N_NODES, C), F32, kind="ExternalOutput").ap()
    gps_layer_kernel(nc, out, **aps)
    return _run(nc, [arrays], core_ids=[0]).results[0]["out"]


def layout(v):
    t = lambda m: np.ascontiguousarray(np.asarray(m).T)
    n = lambda m: np.ascontiguousarray(np.asarray(m))
    return {
        "x": n(v["x"]), "src": n(v["src"]), "dst": n(v["dst"]), "edge_attr": n(v["edge_attr_128"]),
        "w_edge": n(v["L0_gnn_W_edge"]), "b_edge": n(v["L0_gnn_b_edge"]),
        "gnn_w1": n(v["L0_gnn_W1"]), "gnn_b1": n(v["L0_gnn_b1"]), "gnn_w2": n(v["L0_gnn_W2"]),
        "gnn_b2": n(v["L0_gnn_b2"]), "gnn_eps": n(v["L0_gnn_eps"]).reshape(1, 1),
        "gnn_gamma": n(v["L0_gnn_gamma"]), "gnn_beta": n(v["L0_gnn_beta"]),
        "mix_wqkvT": t(v["L0_mix_Wqkv"]), "mix_g1": n(v["L0_mix_ln1_g"]), "mix_be1": n(v["L0_mix_ln1_b"]),
        "mix_w1T": t(v["L0_mix_W1"]), "mix_b1": n(v["L0_mix_b1"]), "mix_w2T": t(v["L0_mix_W2"]),
        "mix_b2": n(v["L0_mix_b2"]), "mix_g2": n(v["L0_mix_ln2_g"]), "mix_be2": n(v["L0_mix_ln2_b"]),
        "w_gat": n(v["L0_ffn_W_gat"]), "att_src": n(v["L0_ffn_att_src"]), "att_dst": n(v["L0_ffn_att_dst"]),
        "b_gat": n(v["L0_ffn_b_gat"]), "ln_gamma": n(v["L0_ffn_ln_gamma"]), "ln_beta": n(v["L0_ffn_ln_beta"]),
        "ffn_w1": n(v["L0_ffn_W1"]), "ffn_b1": n(v["L0_ffn_b1"]), "ffn_w2": n(v["L0_ffn_W2"]),
        "ffn_b2": n(v["L0_ffn_b2"]), "g_edges": n(v["L0_ffn_edge_index"]),
    }
```

```python
import numpy as np
import concourse.bass as bass
from concourse import mybir
from contextlib import ExitStack

F32 = mybir.dt.float32
BF16 = mybir.dt.bfloat16
I32 = mybir.dt.int32
ALU = mybir.AluOpType
ACT = mybir.ActivationFunctionType
AX = mybir.AxisListType.X

P = 128
N_NODES = 6250
C = 256
KC = C // P
N_EDGES = 100000
E_DIM = 128
G_EDGES = 131072
NT = -(-N_NODES // P)
NPAD = NT * P
ST = 7
STEPS = NT // ST
LAST = STEPS - 1
SN = ST * P
HN = SN // 2
LN_EPS = 1e-5
HD = 32
HH = P // HD
EXPERTS = 4
HEADS = 4
GF = HEADS * EXPERTS
FF = 512
FC = FF // P
ROW = GF + HEADS
STATE = ROW + HEADS
START = 1 + HEADS
BIG = 1.0e30


class Chain:

    def __init__(self, eng, sem, base=0):
        self.eng, self.sem, self.base, self.n = eng, sem, base, 0

    def add(self, ins):
        self.n += 1
        ins.then_inc(self.sem, 1)

    def wait(self):
        self.eng.wait_ge(self.sem, self.base + self.n)

    def __call__(self, ins):
        self.add(ins)
        self.wait()


class Program:

    def __init__(self, nc, args, stack):
        self.nc, self.a, self.stack = nc, args, stack
        self.turns = stack.enter_context(nc.semaphore("turns"))
        self.sems = []

    def sem(self, name):
        self.sems.append(self.nc.alloc_semaphore(name=name))
        return self.sems[-1]

    def end_stage(self):
        self.nc.clear_and_free_semaphores(self.sems)
        self.nc.all_engine_barrier()
        self.sems = []

    def dram(self, name, shape, dtype=F32):
        return self.nc.dram_tensor(name, shape, dtype)

    def keep(self, name, shape, dtype=F32):
        return self.stack.enter_context(self.nc.sbuf_tensor(name, shape, dtype))


def node_rows(ap, i):
    return ap[bass.ds(i * SN, SN), :].rearrange("(j p) c -> p j c", p=P)


def feat_cols(ap, i):
    return ap[:, :, bass.ds(i * SN, SN)].rearrange("h p n -> p h n")


def setup(pg):
    nc, a = pg.nc, pg.a
    pg.ident = pg.keep("ident", [P, P])
    pg.ones_row = pg.keep("ones_row", [1, P])
    pg.zeros = pg.keep("zeros", [P, 512])
    pg.headmask = pg.keep("headmask", [P, HH])
    pg.valid = pg.keep("valid", [P, NT])
    pg.kv_blocks = pg.keep("kv_blocks", [P, KC, P + HH])
    pg.first = pg.keep("first", [P, NT], I32)
    pg.last = pg.keep("last", [P, NT], I32)
    pg.starts = pg.keep("starts", [P, NT, START])
    pg.sums = pg.keep("sums", [P, NT, ROW])
    pg.run_end = pg.keep("run_end", [P, STATE])
    pg.whole = pg.keep("whole", [P, 1])
    pg.sums_d = pg.dram("sums_d", [P * RUN, STATE]).ap()
    pg.gate = pg.keep("gate", [P, NT, EXPERTS])
    pg.xpad = pg.dram("xpad", [NPAD, C]).ap()
    pg.xn_d = pg.dram("xn_d", [NPAD, C]).ap()
    pg.xb_d = pg.dram("xb_d", [NPAD, C]).ap()
    pg.xT_d = pg.dram("xT_d", [KC, P, NPAD]).ap()
    pg.mix_d = pg.dram("mix_d", [NPAD, C]).ap()
    pg.x2_d = pg.dram("x2_d", [NPAD, C]).ap()
    pg.x3T_d = pg.dram("x3T_d", [KC, P, NPAD]).ap()


MASKS = 8


def constants(pg, block):
    nc, a = pg.nc, pg.a
    s_zero = pg.zero_ready = pg.sem("zero_ready")
    s_mask = pg.mask_ready = pg.sem("mask_ready")
    s_pad = pg.pad_ready = pg.sem("pad_ready")

    @block.gpsimd
    def _(pool):
        nc.gpsimd.memset(pg.zeros[:, :], 0.0).then_inc(s_zero, 1)
        nc.gpsimd.memset(pg.ones_row[:, :], 1.0).then_inc(s_mask, 1)
        nc.gpsimd.memset(pg.ident[:, :], 0.0).then_inc(s_mask, 1)
        nc.gpsimd.memset(pg.headmask[:, :], 1.0).then_inc(s_mask, 1)
        nc.gpsimd.memset(pg.valid[:, :], 1.0).then_inc(s_mask, 1)
        pool.wait_ge(s_mask, 4)
        nc.gpsimd.affine_select(out=pg.ident[:, :], in_=pg.ident[:, :], compare_op=ALU.not_equal, fill=1.0,
                                base=0, pattern=[[-1, P]], channel_multiplier=1).then_inc(s_mask, 1)
        nc.gpsimd.affine_select(out=pg.headmask[:, :], in_=pg.headmask[:, :], compare_op=ALU.is_ge, fill=0.0,
                                base=0, pattern=[[-HD, HH]], channel_multiplier=1).then_inc(s_mask, 1)
        pool.wait_ge(s_mask, 6)
        nc.gpsimd.affine_select(out=pg.headmask[:, :], in_=pg.headmask[:, :], compare_op=ALU.is_ge, fill=0.0,
                                base=HD - 1, pattern=[[HD, HH]], channel_multiplier=-1).then_inc(s_mask, 1)
        nc.gpsimd.affine_select(out=pg.valid[:, :], in_=pg.valid[:, :], compare_op=ALU.is_ge, fill=0.0,
                                base=N_NODES - 1, pattern=[[-P, NT]], channel_multiplier=-1).then_inc(s_mask, 1)

    @block.sync
    def _(sp):
        sp.dma_start(pg.xpad[0:N_NODES, :], a["x"]).then_inc(s_pad, 16)
        sp.wait_ge(s_zero, 1)
        sp.dma_start(pg.xpad[N_NODES:NPAD, :], pg.zeros[0:NPAD - N_NODES, 0:C]).then_inc(s_pad, 16)


def norm_statistics(nc, dve, ch, turns, rows, stats, mv, var, var_ready, std, std_ready, count):
    for j in range(ST):
        ch.add(nc.vector.bn_stats(out=stats[:, j, :], in_=rows[:, j, :]))
    ch.wait()
    dve.sem_inc(turns, 1)
    for j in range(ST):
        ch.add(nc.vector.bn_aggr(out=mv[:, j, :], in_=stats[:, j, :]))
    ch.wait()
    nc.vector.tensor_scalar_add(var[:, :], mv[:, :, 1], LN_EPS).then_inc(var_ready, 1)
    dve.wait_ge(std_ready, count)
    ch(nc.vector.reciprocal(var[:, :], std[:, :]))


NORM_STEPS = 2 * ST + 1


def normalise(nc, ch, out, rows, mv, rstd):
    for j in range(ST):
        ch.add(nc.vector.tensor_scalar(out=out[:, j, :], in0=rows[:, j, :], scalar1=mv[:, j, 0:1],
                                       scalar2=rstd[:, j:j + 1], op0=ALU.subtract, op1=ALU.mult))
    ch.wait()


UNITS = [(q, min(4, KC * ST - q)) for q in range(0, KC * ST, 4)]
NU = len(UNITS)


def transpose_rows(nc, pe, rows, ident, tp, tp_ready, tp_free, count):
    for u, (q0, nq) in enumerate(UNITS):
        pe.wait_ge(tp_free, count + u + 1)
        for q in range(q0, q0 + nq):
            h, j = q // ST, q % ST
            last = nc.tensor.transpose(tp[u % 2][:, (q - q0) * P:(q - q0 + 1) * P],
                                       rows[:, j, h * P:(h + 1) * P], ident[:, :])
        last.then_inc(tp_ready, 1)


def copy_blocks(nc, act, out, tp, tp_ready, tp_free, out_ready, count):
    flat = out[:, :, :].rearrange("p h n -> p (h n)")
    for u, (q0, nq) in enumerate(UNITS):
        act.wait_ge(tp_ready, count + u + 1)
        nc.scalar.activation(flat[:, q0 * P:(q0 + nq) * P], tp[u % 2][:, 0:nq * P], ACT.Copy).then_inc(tp_free, 1)
    act.wait_ge(tp_free, count + NU + 2)
    act.sem_inc(out_ready, 1)


GT = G_EDGES // P
GB = 8
GR = GT // P
RUN = GT + NT
SLOTS = 2


NB = GT // GB
PAIRS = NB // SLOTS
PAIRS_IN_NORM = PAIRS // STEPS
assert PAIRS_IN_NORM == ST + 2


HOT_STEPS = 2
SET_STEPS = 2


def one_hots(nc, pg, b, tile, ready):
    nc.vector.tensor_tensor(out=pg.one_lo[b][:, :, :], in0=pg.iota_lo[:, :].unsqueeze(1).to_broadcast([P, GB, P]),
                            in1=pg.lo_col[:, bass.ds(tile, GB)].unsqueeze(2).to_broadcast([P, GB, P]),
                            op=ALU.is_equal).then_inc(ready, 1)
    nc.vector.tensor_tensor(out=pg.one_hi[b][:, :, :], in0=pg.iota_hi[:, :].unsqueeze(1).to_broadcast([P, GB, NT]),
                            in1=pg.hi_col[:, bass.ds(tile, GB)].unsqueeze(2).to_broadcast([P, GB, NT]),
                            op=ALU.is_equal).then_inc(ready, 1)


def hold_edges(pg, hold):
    pg.lo_col, pg.hi_col = hold("lo_col", [P, GT], BF16), hold("hi_col", [P, GT], BF16)
    pg.iota_lo = hold("iota_lo", [P, P], BF16)
    pg.iota_hi = hold("iota_hi", [P, NT], BF16)
    pg.one_lo = [hold(f"one_lo{i}", [P, GB, P], BF16) for i in range(SLOTS)]
    pg.one_hi = [hold(f"one_hi{i}", [P, GB, NT], BF16) for i in range(SLOTS)]
    pg.counts = hold("counts", [P, NT], F32)
    pg.lo_d = pg.dram("lo_d", [G_EDGES], BF16).ap()


def stage_norm(pg):
    nc, a = pg.nc, pg.a
    with ExitStack() as st:
        sb = lambda n, s, d=F32: st.enter_context(nc.sbuf_tensor("n_" + n, s, d))
        pb = lambda n, s, d=F32: st.enter_context(nc.psum_tensor("n_" + n, s, d))
        x_in, xn, xb = sb("x_in", [P, ST, C]), sb("xn", [P, ST, C]), sb("xb", [P, ST, C])
        xT = sb("xT", [P, KC, SN])
        b_edge = sb("b_edge", [P, C])
        wkv = sb("wkv", [P, KC, 2 * C])
        stats, mv = sb("stats", [P, ST, 6]), sb("mv", [P, ST, 2])
        std, rstd = sb("std", [P, ST]), sb("rstd", [P, ST])
        kpos, kexp, kf = (sb(n, [P, ST, C]) for n in ("kpos", "kexp", "kf"))
        vf = sb("vf", [P, ST, KC, P + 1])
        tp = [pb(f"tp{i}", [P, 512]) for i in range(2)]
        kp = [pb(f"kp{i}", [P, C]) for i in range(2)]
        vp = [pb(f"vp{i}", [P, C]) for i in range(2)]
        kv = pb("kv", [P, KC * (P + 1)])
        rows_ready, rows_free = pg.sem("n_rows_ready"), pg.sem("n_rows_free")
        w_ready, steps = pg.sem("n_w_ready"), pg.sem("n_steps")
        var_ready, std_ready = pg.sem("n_var_ready"), pg.sem("n_std_ready")
        xn_ready, xn_free, xb_ready = pg.sem("n_xn_ready"), pg.sem("n_xn_free"), pg.sem("n_xb_ready")
        stored = pg.sem("n_stored")
        tp_ready, tp_free = pg.sem("n_tp_ready"), pg.sem("n_tp_free")
        xT_ready, xT_free, xT_stored = pg.sem("n_xT_ready"), pg.sem("n_xT_free"), pg.sem("n_xT_stored")
        kvp_ready = pg.sem("n_kvp_ready")
        k_ready = pg.sem("n_k_ready")
        kf_ready, vf_ready, kv_used = pg.sem("n_kf_ready"), pg.sem("n_vf_ready"), pg.sem("n_kv_used")
        kv_done = pg.sem("n_kv_done")
        src_i, key_i, tmp_i = (sb(n, [P, GT], I32) for n in ("src_i", "key_i", "tmp_i"))
        src_f, lo_f, hi_f = (sb(n, [P, GT]) for n in ("src_f", "lo_f", "hi_f"))
        lo_b = sb("lo_b", [P, GT], BF16)
        total = pb("total", [P, NT])
        edges_loaded, esteps, const = pg.sem("n_edges_loaded"), pg.sem("n_esteps"), pg.sem("n_const")
        keys_ready, src_ready, lo_stored = pg.sem("n_keys_ready"), pg.sem("n_src_ready"), pg.sem("n_lo_stored")
        cp_ready, cp_free, cols_ready = pg.sem("n_cp_ready"), pg.sem("n_cp_free"), pg.sem("n_cols_ready")
        hot_ready, hot_used, counted = pg.sem("n_hot_ready"), pg.sem("n_hot_used"), pg.sem("n_counted")
        with nc.Block() as block:
            constants(pg, block)

            @block.sync
            def _(sp):
                sp.dma_start(wkv[:, :, :], a["mix_wqkvT"][:, C:3 * C].rearrange("(h p) n -> p h n", p=P)).then_inc(w_ready, 16)
                sp.dma_start(b_edge[:, :], a["b_edge"].rearrange("(o c) -> o c", o=1).to_broadcast([P, C])).then_inc(w_ready, 16)
                sp.wait_ge(keys_ready, 1)
                sp.dma_start(pg.lo_d.rearrange("(p c) -> p c", p=P), lo_b[:, :]).then_inc(lo_stored, 16)

                def load(i):
                    sp.wait_ge(rows_free, i + 1)
                    sp.sem_inc(pg.turns, 1)
                    sp.dma_start(x_in[:, :, :], node_rows(pg.xpad, i)).then_inc(rows_ready, 16)

                def store(i):
                    sp.wait_ge(xn_ready, i + 1)
                    sp.sem_inc(pg.turns, 1)
                    sp.dma_start(node_rows(pg.xn_d, i), xn[:, :, :]).then_inc(stored, 16)
                    sp.wait_ge(xb_ready, i + 1)
                    sp.sem_inc(pg.turns, 1)
                    sp.dma_start(node_rows(pg.xb_d, i), xb[:, :, :]).then_inc(stored, 16)
                    sp.wait_ge(xT_ready, i + 1)
                    sp.sem_inc(pg.turns, 1)
                    sp.dma_start(feat_cols(pg.xT_d, i), xT[:, :, :]).then_inc(stored, 16)
                    sp.wait_ge(stored, i * 48 + 48)
                    sp.sem_inc(xn_free, 1)
                    sp.sem_inc(xT_stored, 1)

                sp.sem_inc(xn_free, 1)
                sp.sem_inc(xT_stored, 1)
                sp.wait_ge(pg.pad_ready, 32)
                load(0)
                with sp.Fori(0, LAST) as i:
                    load(i + 1)
                    store(i)
                store(LAST)
                sp.wait_ge(lo_stored, 16)

            @block.gpsimd
            def _(pool):
                nc.gpsimd.iota(pg.iota_lo[:, :], pattern=[[1, P]], base=0, channel_multiplier=0,
                               allow_small_or_imprecise_dtypes=True).then_inc(const, 1)
                nc.gpsimd.iota(pg.iota_hi[:, :], pattern=[[1, NT]], base=0, channel_multiplier=0,
                               allow_small_or_imprecise_dtypes=True).then_inc(const, 1)
                pool.wait_ge(w_ready, 32)
                with pool.Fori(0, STEPS) as i:
                    pool.wait_ge(xn_ready, i + 1)
                    nc.gpsimd.tensor_tensor(out=xb[:, :, :], in0=xn[:, :, :],
                                            in1=b_edge[:, :].unsqueeze(1).to_broadcast([P, ST, C]),
                                            op=ALU.add).then_inc(xb_ready, 1)

            @block.vector
            def _(dve):
                dve.sem_inc(rows_free, 1)
                dve.wait_ge(pg.mask_ready, MASKS)
                ch = Chain(dve, esteps)
                dve.wait_ge(edges_loaded, 32)
                ch.add(nc.vector.tensor_scalar_min(src_f[:, :], src_i[:, :], float(N_NODES - 1)))
                ch(nc.vector.tensor_scalar_min(tmp_i[:, :], key_i[:, :], float(N_NODES)))
                ch(nc.vector.tensor_single_scalar(key_i[:, :], tmp_i[:, :], P - 1, op=ALU.bitwise_and))
                ch.add(nc.vector.tensor_copy(lo_f[:, :], key_i[:, :]))
                ch(nc.vector.tensor_copy(lo_b[:, :], key_i[:, :]))
                dve.sem_inc(keys_ready, 1)
                ch(nc.vector.tensor_single_scalar(key_i[:, :], tmp_i[:, :], 7, op=ALU.logical_shift_right))
                ch(nc.vector.tensor_copy(hi_f[:, :], key_i[:, :]))
                dve.sem_inc(src_ready, 1)
                dve.wait_ge(const, 2)
                dve.wait_ge(cols_ready, 1)

                def count_pair(n):
                    for b in range(SLOTS):
                        dve.wait_ge(hot_used, n * SLOTS + (b + 1))
                        one_hots(nc, pg, b, (n * SLOTS + b) * GB, hot_ready)

                dve.wait_ge(w_ready, 32)
                K = NORM_STEPS + ST
                with dve.Fori(0, STEPS) as i:
                    ch = Chain(dve, steps, i * K)
                    dve.wait_ge(rows_ready, i * 16 + 16)
                    norm_statistics(nc, dve, ch, pg.turns, x_in, stats, mv, rstd, var_ready, std, std_ready, i + 1)
                    dve.wait_ge(xn_free, i + 1)
                    normalise(nc, ch, xn, x_in, mv, rstd)
                    assert ch.n == K
                    dve.sem_inc(rows_free, 1)
                    dve.sem_inc(xn_ready, 1)
                    for n in range(2):
                        count_pair(i * PAIRS_IN_NORM + n)
                    for j in range(ST):
                        count_pair(i * PAIRS_IN_NORM + (j + 2))
                        if j == 0:
                            dve.wait_ge(kv_used, i + 1)
                        dve.wait_ge(k_ready, i * (2 * ST) + (j * 2 + 2))
                        nc.vector.scalar_tensor_tensor(out=kf[:, j, :], in0=kexp[:, j, :], scalar=1.0, in1=kpos[:, j, :],
                                                       op0=ALU.min, op1=ALU.add).then_inc(kf_ready, 1)
                count_pair(PAIRS - 1)
                dve.wait_ge(counted, 1)
                ch(nc.vector.tensor_scalar_add(pg.counts[:, :], total[:, :], 1.0))
                dve.wait_ge(kv_done, 1)
                kvs = kv[:, :].rearrange("p (h n) -> p h n", h=KC)
                hm = pg.headmask[:, :]
                for h in range(KC):
                    nc.vector.tensor_tensor(
                        out=pg.kv_blocks[:, h, 0:P].rearrange("p (g d) -> p g d", g=HH),
                        in0=kvs[:, h, 0:P].rearrange("p (g d) -> p g d", g=HH),
                        in1=hm.unsqueeze(2).to_broadcast([P, HH, HD]), op=ALU.mult)
                    nc.vector.tensor_scalar(out=pg.kv_blocks[:, h, P:P + HH], in0=hm, scalar1=kvs[:, h, P:P + 1],
                                            scalar2=None, op0=ALU.mult)

            @block.scalar
            def _(act):
                act.dma_start(key_i[:, :], a["g_edges"][1, :].rearrange("(p c) -> p c", p=P)).then_inc(edges_loaded, 16)
                act.dma_start(src_i[:, :], a["g_edges"][0, :].rearrange("(p c) -> p c", p=P)).then_inc(edges_loaded, 16)
                act.wait_ge(pg.mask_ready, MASKS)
                act.sem_inc(cp_free, 2)
                n = 0
                for dst in (pg.src_col, pg.lo_col, pg.hi_col):
                    for b in range(GR):
                        act.wait_ge(cp_ready, n + 1)
                        nc.scalar.activation(dst[:, :].rearrange("p (r b) -> p b r", b=GR)[:, b, :], tp[n % 2][:, 0:P],
                                             ACT.Copy).then_inc(cp_free, 1)
                        n += 1
                act.wait_ge(cp_free, n + 2)
                act.sem_inc(cols_ready, 1)
                act.sem_inc(tp_free, 2)
                with act.Fori(0, STEPS) as i:
                    act.wait_ge(var_ready, i + 1)
                    nc.scalar.activation(std[:, :], rstd[:, :], ACT.Sqrt).then_inc(std_ready, 1)
                    act.wait_ge(xT_stored, i + 1)
                    act.wait_ge(xT_free, i + 1)
                    copy_blocks(nc, act, xT, tp, tp_ready, tp_free, xT_ready, i * NU)
                    for j in range(ST):
                        act.wait_ge(kvp_ready, i * ST + j + 1)
                        if j == 0:
                            act.wait_ge(kv_used, i + 1)
                        nc.scalar.activation(vf[:, j, :, 0:P], vp[j % 2][:, :].rearrange("p (h n) -> p h n", h=KC),
                                             ACT.Copy).then_inc(vf_ready, 1)
                        for h in range(KC):
                            nc.scalar.activation(vf[:, j, h, P:P + 1], pg.valid[:, bass.ds(i * ST + j, 1)],
                                                 ACT.Copy).then_inc(vf_ready, 1)
                        nc.scalar.activation(kexp[:, j, :], kp[j % 2][:, :], ACT.Exp).then_inc(k_ready, 1)
                        nc.scalar.activation(kpos[:, j, :], kp[j % 2][:, :], ACT.Relu).then_inc(k_ready, 1)

            @block.tensor
            def _(pe):
                pe.wait_ge(pg.mask_ready, MASKS)
                pe.wait_ge(pg.zero_ready, 1)
                pe.wait_ge(src_ready, 1)
                n = 0
                for src in (src_f, lo_f, hi_f):
                    for b in range(GR):
                        pe.wait_ge(cp_free, n + 1)
                        nc.tensor.transpose(tp[n % 2][:, 0:P], src[:, b * P:(b + 1) * P], pg.ident[:, :]).then_inc(cp_ready, 1)
                        n += 1
                nc.tensor.matmul(total[:, :], pg.zeros[:, 0:P], pg.zeros[:, 0:NT], start=True, stop=True)
                pe.sem_inc(hot_used, SLOTS)

                def count_pair(n):
                    for b in range(SLOTS):
                        pe.wait_ge(hot_ready, n * (SLOTS * HOT_STEPS) + (b + 1) * HOT_STEPS)
                        for t in range(GB):
                            last = nc.tensor.matmul(total[:, :], pg.one_lo[b][:, t, :], pg.one_hi[b][:, t, :],
                                                    start=False, stop=True, skip_group_check=True)
                        last.then_inc(hot_used, 1)

                pe.wait_ge(w_ready, 32)
                pe.sem_inc(xT_free, 1)
                pe.sem_inc(kv_used, 1)
                nc.tensor.matmul(kv[:, :], pg.zeros[:, 0:P], pg.zeros[:, 0:KC * (P + 1)], start=True, stop=True)
                with pe.Fori(0, STEPS) as i:
                    pe.wait_ge(xn_ready, i + 1)
                    transpose_rows(nc, pe, xn, pg.ident, tp, tp_ready, tp_free, i * NU)
                    for n in range(2):
                        count_pair(i * PAIRS_IN_NORM + n)
                    pe.wait_ge(xT_ready, i + 1)
                    for j in range(ST):
                        if j >= 2:
                            pe.wait_ge(kf_ready, i * ST + j - 1)
                            pe.wait_ge(vf_ready, (i * ST + j - 1) * 3)
                        for o, out in enumerate((kp, vp)):
                            for c in range(KC):
                                last = nc.tensor.matmul(out[j % 2][:, :], xT[:, c, j * P:(j + 1) * P],
                                                        wkv[:, c, o * C:(o + 1) * C], start=(c == 0), stop=(c == KC - 1))
                        last.then_inc(kvp_ready, 1)
                        if j > 0:
                            count_pair(i * PAIRS_IN_NORM + (j + 1))
                    count_pair(i * PAIRS_IN_NORM + (ST + 1))
                    pe.wait_ge(kf_ready, i * ST + ST)
                    pe.wait_ge(vf_ready, (i * ST + ST) * 3)
                    pe.sem_inc(xT_free, 1)
                    for j in range(ST):
                        for h in range(KC):
                            last = nc.tensor.matmul(kv[:, h * (P + 1):(h + 1) * (P + 1)], kf[:, j, h * P:(h + 1) * P],
                                                    vf[:, j, h, :], start=False, stop=True, skip_group_check=True)
                    last.then_inc(kv_used, 1)
                pe.wait_ge(kv_used, STEPS + 1)
                pe.sem_inc(kv_done, 1)
                count_pair(PAIRS - 1)
                pe.wait_ge(hot_used, SLOTS + NB)
                pe.sem_inc(counted, 1)


SORT_BATCHES = 76
MIX_BATCHES = 32
GNN_BATCHES = 12
SUM_BATCHES = GT // GB - SORT_BATCHES - MIX_BATCHES - GNN_BATCHES


def scatter_batches(pg, pool, name, first, count, ready=None):
    nc = pg.nc
    copied = pg.sem(name + "_copied")
    sent = [pg.sem(f"{name}_sent{b}") for b in range(SLOTS)]

    def batch(i, b, fresh):
        k = i * SLOTS + b
        if ready is not None:
            pool.wait_ge(ready, first + k + 1)
        if not fresh:
            pool.wait_ge(sent[b], i * (16 * GB))
        nc.gpsimd.tensor_copy(pg.place[b][:, :], pg.place_col[:, bass.ds((first + k) * GB, GB)]).then_inc(copied, 1)
        nc.gpsimd.tensor_copy(pg.source[b][:, :], pg.src_col[:, bass.ds((first + k) * GB, GB)]).then_inc(copied, 1)
        pool.wait_ge(copied, k * 2 + 2)
        pool.sem_inc(pg.turns, 1)
        for t in range(GB):
            pool.indirect_dma_start(out=pg.sorted_d, out_offset=bass.IndirectOffsetOnAxis(ap=pg.place[b][:, t:t + 1], axis=0),
                                    in_=pg.source[b][:, t:t + 1], in_offset=None).then_inc(sent[b], 16)

    for b in range(SLOTS):
        batch(0, b, True)
    with pool.Fori(1, count // SLOTS) as i:
        for b in range(SLOTS):
            batch(i, b, False)
    for b in range(SLOTS):
        pool.wait_ge(sent[b], 16 * GB * (count // SLOTS))


def stage_sort(pg):
    nc, a = pg.nc, pg.a
    pg.sorted_d = pg.dram("sorted_d", [P * RUN, 1], I32).ap()
    with ExitStack() as st:
        sb = lambda n, s, d=F32: st.enter_context(nc.sbuf_tensor("s_" + n, s, d))
        pb = lambda n, s, d=F32: st.enter_context(nc.psum_tensor("s_" + n, s, d))
        place_col, lo_col, one_lo, one_hi, counts = pg.place_col, pg.lo_col, pg.one_lo, pg.one_hi, pg.counts
        iota_p = sb("iota_p", [P, 1])
        before = sb("before", [P, P])
        before_b = sb("before_b", [P, P], BF16)
        ones = sb("ones", [P, P])
        totals, starts, first_f, last_f, seed = (
            sb(n, [P, NT]) for n in ("totals", "starts", "first_f", "last_f", "seed"))
        lo_row = [sb(f"lo_row{i}", [P, GB, P], BF16) for i in range(SLOTS)]
        one_loT = [sb(f"one_loT{i}", [P, GB, P]) for i in range(SLOTS)]
        same = [sb(f"same{i}", [P, GB, P], BF16) for i in range(SLOTS)]
        seen = [sb(f"seen{i}", [P, NT]) for i in range(2)]
        ranked = sb("ranked", [P, GB, NT])
        place_f = sb("place_f", [P, GB])
        total = pb("total", [P, NT])
        live = pb("live", [P, NT])
        rank = [pb(f"rank{i}", [P, GB, NT]) for i in range(SLOTS)]
        steps, const = pg.sem("s_steps"), pg.sem("s_const")
        hot_ready = pg.sem("s_hot_ready")
        prefix_ready = pg.sem("s_prefix_ready")
        first_ready = pg.sem("s_first_ready")
        row_ready = [pg.sem(f"s_row_ready{i}") for i in range(SLOTS)]
        live_ready, seen_ready = pg.sem("s_live_ready"), pg.sem("s_seen_ready")
        sets_ready, sets_used = pg.sem("s_sets_ready"), pg.sem("s_sets_used")
        rank_ready, rank_free = pg.sem("s_rank_ready"), pg.sem("s_rank_free")
        place_ready = pg.sem("s_place_ready")
        with nc.Block() as block:
            @block.sync
            def _(sp):
                with sp.Fori(0, PAIRS) as i:
                    for b in range(SLOTS):
                        sp.wait_ge(sets_ready, (i * SLOTS + b) * SET_STEPS + SET_STEPS)
                        sp.sem_inc(pg.turns, 1)
                        rows = pg.lo_d[bass.ds((i * SLOTS + b) * GB * P, GB * P)]
                        sp.dma_start(lo_row[b][:, :, :].rearrange("p t e -> p (t e)"),
                                     rows.rearrange("(o n) -> o n", o=1).to_broadcast([P, GB * P])).then_inc(row_ready[b], 16)

            @block.gpsimd
            def _(pool):
                nc.gpsimd.iota(iota_p[:, :], pattern=[[0, 1]], base=0, channel_multiplier=1,
                               allow_small_or_imprecise_dtypes=True).then_inc(const, 1)
                nc.gpsimd.iota(pg.node_id[:, :], pattern=[[P, NT]], base=0, channel_multiplier=1).then_inc(const, 1)
                nc.gpsimd.memset(ones[:, :], 1.0).then_inc(const, 1)
                pool.wait_ge(const, 3)
                nc.gpsimd.affine_select(out=before[:, :], in_=ones[:, :], compare_op=ALU.is_ge, fill=0.0,
                                        base=-1, pattern=[[1, P]], channel_multiplier=-1).then_inc(const, 1)
                pool.wait_ge(const, 4)
                nc.gpsimd.tensor_copy(before_b[:, :], before[:, :]).then_inc(const, 1)
                scatter_batches(pg, pool, "s", 0, SORT_BATCHES, place_ready)

            @block.vector
            def _(dve):
                ch = Chain(dve, steps)
                dve.sem_inc(sets_ready, SLOTS * SET_STEPS)
                dve.sem_inc(rank_free, SLOTS)
                dve.wait_ge(const, 5)
                dve.wait_ge(prefix_ready, 1)
                ch(nc.vector.tensor_copy(totals[:, :], total[:, :]))
                ch(nc.vector.tensor_tensor_scan(out=starts[:, :], data0=ones[:, 0:NT], data1=totals[:, :], initial=0.0,
                                                op0=ALU.mult, op1=ALU.add))
                ch(nc.vector.tensor_tensor(out=starts[:, :], in0=starts[:, :], in1=totals[:, :], op=ALU.subtract))
                ch(nc.vector.tensor_tensor(out=first_f[:, :], in0=starts[:, :], in1=live[:, :], op=ALU.add))
                ch(nc.vector.tensor_copy(pg.first[:, :], first_f[:, :]))
                ch(nc.vector.tensor_scalar_add(seed[:, :], first_f[:, :], 1.0))
                dve.sem_inc(first_ready, 1)
                ch(nc.vector.tensor_tensor(out=last_f[:, :], in0=first_f[:, :], in1=counts[:, :], op=ALU.add))
                ch(nc.vector.tensor_scalar_add(pg.last[:, :], last_f[:, :], -1.0))
                base = ch.n

                def sets(ch, n, b, turn):
                    dve.wait_ge(sets_used, n + 1)
                    dve.wait_ge(row_ready[b], turn * 16 + 16)
                    ch.add(nc.vector.tensor_tensor(out=same[b][:, :, :], in0=lo_row[b][:, :, :],
                                                   in1=lo_col[:, bass.ds(n * GB, GB)].unsqueeze(2).to_broadcast([P, GB, P]),
                                                   op=ALU.is_equal))
                    nc.vector.tensor_scalar(out=one_loT[b][:, :, :], in0=lo_row[b][:, :, :], scalar1=iota_p[:, 0:1],
                                            scalar2=None, op0=ALU.is_equal).then_inc(sets_ready, 1)
                    ch.wait()
                    nc.vector.tensor_tensor(out=same[b][:, :, :], in0=same[b][:, :, :],
                                            in1=before_b[:, :].unsqueeze(1).to_broadcast([P, GB, P]),
                                            op=ALU.mult).then_inc(sets_ready, 1)

                def places(ch, n, b, ahead=True):
                    dve.wait_ge(rank_ready, n + 1)
                    ch(nc.vector.tensor_tensor(out=ranked[:, :, :], in0=rank[b][:, :, :], in1=one_hi[b][:, :, :], op=ALU.mult))
                    dve.sem_inc(rank_free, 1)
                    ch.add(nc.vector.tensor_reduce(out=place_f[:, :], in_=ranked[:, :, :], axis=AX, op=ALU.add))
                    if ahead:
                        one_hots(nc, pg, b, (n + 2) * GB, hot_ready)
                    ch.wait()
                    nc.vector.tensor_copy(place_col[:, bass.ds(n * GB, GB)], place_f[:, :]).then_inc(place_ready, 1)

                K = 3
                for b in range(SLOTS):
                    one_hots(nc, pg, b, b * GB, hot_ready)
                sets(Chain(dve, steps, base), 0, 0, 0)
                base += 1
                with dve.Fori(0, PAIRS - 1) as i:
                    ch = Chain(dve, steps, base + i * SLOTS * K)
                    sets(ch, i * 2 + 1, 1, i)
                    places(ch, i * 2, 0)
                    sets(ch, i * 2 + 2, 0, i + 1)
                    places(ch, i * 2 + 1, 1)
                    assert ch.n == SLOTS * K
                ch = Chain(dve, steps, base + (PAIRS - 1) * SLOTS * K)
                sets(ch, NB - 1, 1, PAIRS - 1)
                places(ch, NB - 2, 0, False)
                places(ch, NB - 1, 1, False)

            @block.scalar
            def _(act):
                with act.Fori(0, NB) as i:
                    for t in range(GB):
                        act.wait_ge(live_ready, i * GB + t + 1)
                        nc.scalar.activation(seen[t % 2][:, :], live[:, :], ACT.Copy).then_inc(seen_ready, 1)

            @block.tensor
            def _(pe):
                pe.sem_inc(sets_used, SLOTS)
                pe.wait_ge(const, 4)
                nc.tensor.matmul(total[:, :], ones[:, :], counts[:, :], start=True, stop=True)
                nc.tensor.matmul(live[:, :], before[:, :], counts[:, :], start=True, stop=True).then_inc(prefix_ready, 1)
                pe.wait_ge(first_ready, 1)
                nc.tensor.matmul(live[:, :], pg.ident[:, :], seed[:, :], start=True, stop=True).then_inc(live_ready, 1)
                with pe.Fori(0, PAIRS) as i:
                    for b in range(SLOTS):
                        n = i * SLOTS + b
                        pe.wait_ge(hot_ready, n * HOT_STEPS + HOT_STEPS)
                        pe.wait_ge(sets_ready, n * SET_STEPS + (SLOTS + 1) * SET_STEPS)
                        pe.wait_ge(rank_free, n + 1)
                        for t in range(GB):
                            pe.wait_ge(seen_ready, n * GB + t + 1)
                            nc.tensor.matmul(live[:, :], one_lo[b][:, t, :], one_hi[b][:, t, :],
                                             start=False, stop=True, skip_group_check=True).then_inc(live_ready, 1)
                            nc.tensor.matmul(rank[b][:, t, :], one_loT[b][:, t, :], seen[t % 2][:, :], start=True, stop=False)
                            last = nc.tensor.matmul(rank[b][:, t, :], same[b][:, t, :], one_hi[b][:, t, :], start=False, stop=True)
                        last.then_inc(rank_ready, 1)
                        pe.sem_inc(sets_used, 1)


EB = 8
EG = -(-N_EDGES // (P * EB))
E_FULL = N_EDGES // (P * EB)
E_TAIL = (N_EDGES - E_FULL * P * EB) // EB
WIN = 128
WINDOWS = -(-N_NODES // WIN)
EQ = EB // 2


def edge_groups(ap, tail=False):
    n = E_FULL * P * EB
    if tail:
        return ap[n:N_EDGES].rearrange("(p t) -> p t", t=EB)
    return ap[0:n].rearrange("(g p t) -> p g t", p=P, t=EB)


def stage_edges(pg):
    nc, a = pg.nc, pg.a
    with ExitStack() as st:
        sb = lambda n, s, d=F32: st.enter_context(nc.sbuf_tensor("e_" + n, s, d))
        pb = lambda n, s, d=F32: st.enter_context(nc.psum_tensor("e_" + n, s, d))
        src_raw, src_i = sb("src_raw", [P, EG, EB], I32), sb("src_i", [P, EG, EB], I32)
        dst_i, dst_f, node_f = sb("dst_i", [P, EG, EB], I32), sb("dst_f", [P, EG, EB]), sb("node_f", [P, EG, EB])
        ext, ext_n, ext_row = sb("ext", [P, 2, EG]), sb("ext_n", [EG, 2]), sb("ext_row", [1, 2, EG])
        more, more_sum, more_before = sb("more", [1, EG]), sb("more_sum", [1, EG]), sb("more_before", [1, EG])
        more_i = sb("more_i", [1, 2, EG], I32)
        table = sb("table", [1, 3, EG], I32)
        nodes = sb("nodes", [P, NPAD + WIN])
        w_edge = sb("w_edge", [P, C])
        index = [sb(f"index{b}", [P, EB], I32) for b in range(2)]
        xg = [sb(f"xg{b}", [P, EB, C]) for b in range(2)]
        ea = [sb(f"ea{b}", [P, EB, E_DIM]) for b in range(2)]
        eaT = [sb(f"eaT{b}", [P, EB, P]) for b in range(2)]
        msg = [sb(f"msg{b}", [P, EB, C]) for b in range(2)]
        hot = [sb(f"hot{b}", [P, EB, WIN]) for b in range(2)]
        hotx = sb("hotx", [P, EB, WIN])
        tp = [pb(f"tp{h}", [P, EB // 2, P]) for h in range(2)]
        pre = [pb(f"pre{q}", [P, 2, C]) for q in range(EQ)]
        part = [pb(f"part{b}", [P, 2, KC, WIN]) for b in range(2)]
        idx_init, idx_loaded, w_ready = pg.sem("e_idx_init"), pg.sem("e_idx_loaded"), pg.sem("e_w_ready")
        steps, src_ready, dst_fixed = pg.sem("e_steps"), pg.sem("e_src_ready"), pg.sem("e_dst_fixed")
        ext_ready, extT_ready, row_in, row_out = (pg.sem(n) for n in ("e_ext_ready", "e_extT_ready", "e_row_in", "e_row_out"))
        table_ready, nodes_ready = pg.sem("e_table_ready"), pg.sem("e_nodes_ready")
        dstf_ready = pg.sem("e_dstf_ready")
        index_ready, index_used = pg.sem("e_index_ready"), pg.sem("e_turns")
        gathered = [pg.sem(f"e_gathered{b}") for b in range(2)]
        ea_ready = [pg.sem(f"e_ea_ready{b}") for b in range(2)]
        tp_ready, eaT_ready, pre_ready = pg.sem("e_tp_ready"), pg.sem("e_eaT_ready"), pg.sem("e_pre_ready")
        msg_added, relu_done = pg.sem("e_msg_added"), pg.sem("e_relu_done")
        hot_ready, summed, added = pg.sem("e_hot_ready"), pg.sem("e_summed"), pg.sem("e_added")
        hotx_ready, summedx, addedx = pg.sem("e_hotx_ready"), pg.sem("e_summedx"), pg.sem("e_addedx")
        with nc.Block() as block:
            @block.sync
            def _(sp):
                sp.dma_start(w_edge[:, :], a["w_edge"]).then_inc(w_ready, 16)
                sp.wait_ge(idx_init, 2)
                sp.dma_start(dst_i[:, 0:E_FULL, :], edge_groups(a["dst"])).then_inc(idx_loaded, 16)
                sp.dma_start(src_raw[:, 0:E_FULL, :], edge_groups(a["src"])).then_inc(idx_loaded, 16)
                sp.dma_start(dst_i[0:E_TAIL, E_FULL, :], edge_groups(a["dst"], True)).then_inc(idx_loaded, 16)
                sp.dma_start(src_raw[0:E_TAIL, E_FULL, :], edge_groups(a["src"], True)).then_inc(idx_loaded, 16)

                def load(i, b, tail):
                    sp.wait_ge(tp_ready, (i * 2 + b) * 2 + 2)
                    if tail:
                        rows = a["edge_attr"][E_FULL * P * EB:N_EDGES, :].rearrange("(p t) d -> p t d", t=EB)
                        sp.dma_start(ea[b][0:E_TAIL, :, :], rows).then_inc(ea_ready[b], 16)
                    else:
                        rows = a["edge_attr"][bass.ds((i * 2 + b) * (P * EB), P * EB), :].rearrange("(p t) d -> p t d", t=EB)
                        sp.dma_start(ea[b][:, :, :], rows).then_inc(ea_ready[b], 16)

                with sp.Fori(0, EG // 2 - 1) as i:
                    load(i, 0, False)
                    load(i, 1, False)
                load(EG // 2 - 1, 0, False)
                load(EG // 2 - 1, 1, True)

            @block.gpsimd
            def _(pool):
                nc.gpsimd.memset(dst_i[:, :, :], N_NODES - 1).then_inc(idx_init, 1)
                nc.gpsimd.memset(src_raw[:, :, :], 0).then_inc(idx_init, 1)
                nc.gpsimd.iota(nodes[:, :], pattern=[[1, NPAD + WIN]], base=0, channel_multiplier=0,
                               allow_small_or_imprecise_dtypes=True).then_inc(nodes_ready, 1)
                nc.gpsimd.memset(pg.agg[:, :, :], 0.0).then_inc(nodes_ready, 1)
                pool.wait_ge(dstf_ready, 1)
                nc.gpsimd.affine_select(out=dst_f[:, EG - 1, :], in_=dst_f[:, EG - 1, :], compare_op=ALU.is_ge,
                                        fill=-1.0, base=E_TAIL - 1, pattern=[[0, EB]], channel_multiplier=-1).then_inc(dst_fixed, 1)
                pool.wait_ge(src_ready, 1)
                with pool.Fori(0, EG // 2) as i:
                    for b in range(2):
                        g = i * 2 + b
                        pool.wait_ge(msg_added, g * EQ + EQ)
                        nc.gpsimd.tensor_copy(index[b][:, :], src_i[:, bass.ds(g, 1), :].rearrange("p o t -> p (o t)")).then_inc(index_ready, 1)
                        pool.wait_ge(index_ready, g + 1)
                        pool.sem_inc(index_used, 1)
                        for t in range(EB):
                            pool.indirect_dma_start(out=xg[b][:, t, :], out_offset=None, in_=pg.xb_d,
                                                    in_offset=bass.IndirectOffsetOnAxis(ap=index[b][:, t:t + 1], axis=0)
                                                    ).then_inc(gathered[b], 16)

            @block.scalar
            def _(act):
                act.sem_inc(eaT_ready, 2)

                def copy_attributes(g, b):
                    for h in range(2):
                        act.wait_ge(tp_ready, g * 2 + h + 5)
                        nc.scalar.activation(eaT[b][:, h * EQ:(h + 1) * EQ, :], tp[h][:, :, :], ACT.Copy).then_inc(eaT_ready, 1)

                def rectify(g, b):
                    for h in range(2):
                        half = msg[b][:, h * EQ:(h + 1) * EQ, :]
                        act.wait_ge(msg_added, g * EQ + 2 * EQ + (h + 1) * EQ // 2)
                        nc.scalar.activation(half, half, ACT.Relu).then_inc(relu_done, 1)

                copy_attributes(0, 0)
                copy_attributes(1, 1)
                with act.Fori(0, EG // 2 - 1) as i:
                    for b in range(2):
                        rectify(i * 2 + b, b)
                        copy_attributes(i * 2 + (2 + b), b)
                rectify(EG - 2, 0)
                rectify(EG - 1, 1)

            @block.vector
            def _(dve):
                ch = Chain(dve, steps)
                dve.sem_inc(msg_added, 2 * EQ)
                dve.sem_inc(added, 2)
                dve.wait_ge(idx_loaded, 64)
                ch.add(nc.vector.tensor_copy(dst_f[:, :, :], dst_i[:, :, :]))
                ch(nc.vector.tensor_scalar_min(src_i[:, :, :], src_raw[:, :, :], float(N_NODES - 1)))
                dve.sem_inc(src_ready, 1)
                dve.sem_inc(dstf_ready, 1)
                ch(nc.vector.tensor_scalar(out=node_f[:, :, :], in0=dst_i[:, :, :], scalar1=0.0, scalar2=float(N_NODES - 1),
                                           op0=ALU.max, op1=ALU.min))
                ch.add(nc.vector.tensor_reduce(out=ext[:, 0, :], in_=node_f[:, :, :], axis=AX, op=ALU.min))
                ch(nc.vector.tensor_reduce(out=ext[:, 1, :], in_=node_f[:, :, :], axis=AX, op=ALU.max))
                dve.sem_inc(ext_ready, 1)
                dve.wait_ge(extT_ready, 1)
                ch(nc.vector.tensor_reduce(out=ext_n[:, 0:1], in_=pre[0][0:EG, 0, 0:P], axis=AX, op=ALU.min))
                ch(nc.vector.tensor_reduce(out=ext_n[:, 1:2], in_=pre[0][0:EG, 1, 0:P], axis=AX, op=ALU.max))
                dve.sem_inc(row_in, 1)
                dve.wait_ge(row_out, 1)
                ch(nc.vector.tensor_copy(ext_row[:, :, :], pre[1][0:1, :, 0:EG]))
                ch(nc.vector.tensor_tensor(out=more[:, :], in0=ext_row[:, 1, :], in1=ext_row[:, 0, :], op=ALU.subtract))
                ch(nc.vector.tensor_copy(more_i[:, 0, :], more[:, :]))
                ch(nc.vector.tensor_single_scalar(more_i[:, 1, :], more_i[:, 0, :], WIN.bit_length() - 1,
                                                  op=ALU.logical_shift_right))
                ch(nc.vector.tensor_copy(more[:, :], more_i[:, 1, :]))
                ch(nc.vector.tensor_tensor_scan(out=more_sum[:, :], data0=pg.ones_row[:, 0:EG], data1=more[:, :], initial=0.0,
                                                op0=ALU.mult, op1=ALU.add))
                ch(nc.vector.tensor_tensor(out=more_before[:, :], in0=more_sum[:, :], in1=more[:, :], op=ALU.subtract))
                ch.add(nc.vector.tensor_copy(table[:, 0, :], ext_row[:, 0, :]))
                ch.add(nc.vector.tensor_copy(table[:, 1, :], more[:, :]))
                ch(nc.vector.tensor_copy(table[:, 2, :], more_before[:, :]))
                dve.sem_inc(table_ready, 1)
                dve.wait_ge(dst_fixed, 1)
                dve.wait_ge(nodes_ready, 2)

                def one_hot(out, g, node):
                    return nc.vector.tensor_tensor(
                        out=out[:, :, :], in0=nodes[:, bass.ds(node, WIN)].unsqueeze(1).to_broadcast([P, EB, WIN]),
                        in1=dst_f[:, bass.ds(g, 1), :].rearrange("p o t -> p (o t)").unsqueeze(2).to_broadcast([P, EB, WIN]),
                        op=ALU.is_equal)

                def first_hot(g, b):
                    first = dve.value_load(table[0:1, 0, bass.ds(g, 1)], min_val=0, max_val=N_NODES - 1)
                    one_hot(hot[b], g, first).then_inc(hot_ready, 1)

                def messages(g, b, turn):
                    dve.wait_ge(gathered[b], turn * (16 * EB) + 16 * EB)
                    for q in range(EQ):
                        dve.wait_ge(pre_ready, g * EQ + q + 1)
                        nc.vector.tensor_tensor(out=msg[b][:, 2 * q:2 * q + 2, :], in0=pre[q][:, :, :],
                                                in1=xg[b][:, 2 * q:2 * q + 2, :], op=ALU.add).then_inc(msg_added, 1)

                def add_part(node, sums):
                    acc = pg.agg[:, :, bass.ds(node, WIN)]
                    return nc.vector.tensor_tensor(out=acc, in0=acc, in1=sums, op=ALU.add)

                window = lambda first, n: nc.s_assert_within(
                    first + n * WIN, 0, NPAD, skip_runtime_bounds_check_because=
                    "a group's last window starts at its largest destination or before")

                def finish_group(g, b, next_messages=None):
                    first = dve.value_load(table[0:1, 0, bass.ds(g, 1)], min_val=0, max_val=N_NODES - 1)
                    further = dve.value_load(table[0:1, 1, bass.ds(g, 1)], min_val=0, max_val=WINDOWS - 1)
                    before = dve.value_load(table[0:1, 2, bass.ds(g, 1)], min_val=0, max_val=EG * WINDOWS)
                    with dve.If(further > 0):
                        one_hot(hotx, g, window(first, 1)).then_inc(hotx_ready, 1)
                    if next_messages is not None:
                        messages(*next_messages)
                    dve.wait_ge(summed, g + 1)
                    add_part(first, part[b][:, 0, :, :]).then_inc(added, 1)
                    dve.wait_ge(added, g + 3)
                    dve.sem_inc(pg.turns, 1)
                    with dve.If(further > 0):
                        with dve.Fori(0, further) as j:
                            dve.wait_ge(summedx, before + j + 1)
                            dve.sem_inc(pg.turns, 1)
                            with dve.If(further > j + 1):
                                one_hot(hotx, g, window(first, j + 2)).then_inc(hotx_ready, 1)
                            add_part(window(first, j + 1), part[1 - b][:, 1, :, :]).then_inc(addedx, 1)
                            dve.wait_ge(addedx, before + j + 2)

                dve.sem_inc(addedx, 1)
                first_hot(0, 0)
                messages(0, 0, 0)
                with dve.Fori(0, EG // 2 - 1) as i:
                    for b in range(2):
                        g = i * 2 + b
                        first_hot(g + 1, 1 - b)
                        finish_group(g, b, (g + 1, 1 - b, i + b))
                first_hot(EG - 1, 1)
                finish_group(EG - 2, 0, (EG - 1, 1, EG // 2 - 1))
                finish_group(EG - 1, 1)

            @block.tensor
            def _(pe):
                pe.sem_inc(tp_ready, 4)
                pe.wait_ge(ext_ready, 1)
                for m in range(2):
                    last = nc.tensor.transpose(pre[0][0:EG, m, 0:P], ext[:, m, :], pg.ident[:, :])
                last.then_inc(extT_ready, 1)
                pe.wait_ge(row_in, 1)
                for m in range(2):
                    last = nc.tensor.transpose(pre[1][0:1, m, 0:EG], ext_n[:, m:m + 1], pg.ident[0:EG, 0:EG])
                last.then_inc(row_out, 1)
                pe.wait_ge(table_ready, 1)
                pe.wait_ge(w_ready, 16)

                def turn_attributes(i, b):
                    g = i * 2 + b
                    pe.wait_ge(ea_ready[b], i * 16 + 16)
                    for h in range(2):
                        pe.wait_ge(eaT_ready, g * 2 + h + 1)
                        for t in range(EQ):
                            last = nc.tensor.transpose(tp[h][:, t, :], ea[b][:, h * EQ + t, :], pg.ident[:, :])
                        last.then_inc(tp_ready, 1)

                def project(g, b):
                    for q in range(EQ):
                        if q % 2 == 0:
                            pe.wait_ge(eaT_ready, g * 2 + q // 2 + 3)
                        pe.wait_ge(msg_added, g * EQ + q + EQ + 1)
                        for t in range(2):
                            last = nc.tensor.matmul(pre[q][:, t, :], eaT[b][:, 2 * q + t, :], w_edge[:, :], start=True, stop=True)
                        last.then_inc(pre_ready, 1)

                def product(out, one_hots, b, h, t):
                    return nc.tensor.matmul(out[:, h, :], msg[b][:, t, h * P:(h + 1) * P], one_hots[:, t, :],
                                            start=(t == 0), stop=(t == EB - 1))

                def sum_group(g, b):
                    further = pe.value_load(table[0:1, 1, bass.ds(g, 1)], min_val=0, max_val=WINDOWS - 1)
                    before = pe.value_load(table[0:1, 2, bass.ds(g, 1)], min_val=0, max_val=EG * WINDOWS)
                    pe.wait_ge(hot_ready, g + 1)
                    pe.wait_ge(added, g + 1)
                    pe.wait_ge(addedx, before + 1)
                    for h in range(KC):
                        for t in range(EB):
                            if h == 0 and t % EQ == 0:
                                pe.wait_ge(relu_done, g * 2 + t // EQ + 1)
                            last = product(part[b][:, 0, :, :], hot[b], b, h, t)
                    last.then_inc(summed, 1)
                    with pe.If(further > 0):
                        with pe.Fori(0, further) as j:
                            pe.wait_ge(hotx_ready, before + j + 1)
                            pe.wait_ge(addedx, before + j + 1)
                            for h in range(KC):
                                for t in range(EB):
                                    last = product(part[1 - b][:, 1, :, :], hotx, b, h, t)
                            last.then_inc(summedx, 1)

                turn_attributes(0, 0)
                turn_attributes(0, 1)
                project(0, 0)
                with pe.Fori(0, EG // 2 - 1) as i:
                    for b in range(2):
                        project(i * 2 + (b + 1), 1 - b)
                        sum_group(i * 2 + b, b)
                        turn_attributes(i + 1, b)
                project(EG - 1, 1)
                sum_group(EG - 2, 0)
                sum_group(EG - 1, 1)


def row_of(ap, n):
    return ap.rearrange("(o c) -> o c", o=1).to_broadcast([P, n])


def col_of(ap):
    return ap.rearrange("(h p) -> p h", p=P)


def weights_of(ap):
    return ap.rearrange("(h p) n -> p h n", p=P)


def feature_block(nc, out, wT, xT, n):
    m, h = n // 2, n % 2
    for c in range(KC):
        last = nc.tensor.matmul(out[h][:, :], wT[:, c, m * P:(m + 1) * P], xT[:, c, h * HN:(h + 1) * HN],
                                start=(c == 0), stop=(c == KC - 1))
    return last


def apply_norm(nc, ch, out, rows, mv, rstd, gain, shift):
    for j in range(ST):
        ch.add(nc.vector.scalar_tensor_tensor(out=out[:, j, :], in0=rows[:, j, :], scalar=mv[:, j, 0:1], in1=gain[:, :],
                                              op0=ALU.subtract, op1=ALU.mult))
    ch.wait()
    for j in range(ST):
        ch.add(nc.vector.scalar_tensor_tensor(out=out[:, j, :], in0=out[:, j, :], scalar=rstd[:, j:j + 1], in1=shift[:, :],
                                              op0=ALU.mult, op1=ALU.add))
    ch.wait()


def stage_mix(pg):
    nc, a = pg.nc, pg.a
    with ExitStack() as st:
        sb = lambda n, s, d=F32: st.enter_context(nc.sbuf_tensor("m_" + n, s, d))
        pb = lambda n, s, d=F32: st.enter_context(nc.psum_tensor("m_" + n, s, d))
        wq, w1, w2 = (sb(n, [P, KC, C]) for n in ("wq", "w1", "w2"))
        b1 = sb("b1", [P, KC])
        b2, g1, be1, g2, be2 = (sb(n, [P, C]) for n in ("b2", "g1", "be1", "g2", "be2"))
        xT, xn = sb("xT", [P, KC, SN]), sb("xn", [P, ST, C])
        qpos, qexp, qT = (sb(n, [P, KC, SN]) for n in ("qpos", "qexp", "qT"))
        sums = sb("sums", [P, ST, KC, P + HH])
        z = sb("z", [P, ST, KC, HH])
        t, x1, rest, y, out = (sb(n, [P, ST, C]) for n in ("t", "x1", "rest", "y", "out"))
        x1T, hT = sb("x1T", [P, KC, SN]), sb("hT", [P, KC, SN])
        stats, mv, std, rstd = sb("stats", [P, ST, 6]), sb("mv", [P, ST, 2]), sb("std", [P, ST]), sb("rstd", [P, ST])
        fm = [pb(f"fm{i}", [P, HN]) for i in range(2)]
        att = [pb(f"att{i}", [P, KC, P + HH]) for i in range(2)]
        tp = [pb(f"tp{i}", [P, 512]) for i in range(2)]
        yp = [pb(f"yp{i}", [P, C]) for i in range(2)]
        w_ready, xT_loaded, xn_loaded = pg.sem("m_w_ready"), pg.sem("m_xT_loaded"), pg.sem("m_xn_loaded")
        steps, fm_ready, fm_free = pg.sem("m_steps"), pg.sem("m_fm_ready"), pg.sem("m_fm_free")
        q_ready, qT_ready = pg.sem("m_q_ready"), pg.sem("m_qT_ready")
        att_ready, att_free = pg.sem("m_att_ready"), pg.sem("m_att_free")
        sums_ready, sums_used = pg.sem("m_sums_ready"), pg.sem("m_sums_used")
        var_ready, std_ready, x1_ready = pg.sem("m_var_ready"), pg.sem("m_std_ready"), pg.sem("m_x1_ready")
        tp_ready, tp_free, x1T_ready = pg.sem("m_tp_ready"), pg.sem("m_tp_free"), pg.sem("m_x1T_ready")
        hT_ready, yp_ready, yp_free = pg.sem("m_hT_ready"), pg.sem("m_yp_ready"), pg.sem("m_yp_free")
        out_ready, out_stored, out_free = pg.sem("m_out_ready"), pg.sem("m_out_stored"), pg.sem("m_out_free")
        hidden_base = lambda i: i * 8 + 8 if i is not LAST else LAST * 8 + 4
        second_root = lambda i: i * 2 + 3 if i is not LAST else LAST * 2 + 2
        with nc.Block() as block:
            @block.sync
            def _(sp):
                sp.dma_start(wq[:, :, :], weights_of(a["mix_wqkvT"][:, 0:C])).then_inc(w_ready, 16)
                sp.dma_start(w1[:, :, :], weights_of(a["mix_w1T"])).then_inc(w_ready, 16)
                sp.dma_start(w2[:, :, :], weights_of(a["mix_w2T"])).then_inc(w_ready, 16)
                with nc.allow_non_contiguous_dma(reason="two vectors of 256"):
                    sp.dma_start(b1[:, :], col_of(a["mix_b1"])).then_inc(w_ready, 16)
                for d, v in ((b2, "mix_b2"), (g1, "mix_g1"), (be1, "mix_be1"), (g2, "mix_g2"), (be2, "mix_be2")):
                    sp.dma_start(d[:, :], row_of(a[v], C)).then_inc(w_ready, 16)
                sp.sem_inc(out_free, 1)
                with sp.Fori(0, STEPS) as i:
                    sp.wait_ge(out_ready, i + 1)
                    sp.dma_start(node_rows(pg.mix_d, i), out[:, :, :]).then_inc(out_stored, 16)
                    sp.wait_ge(out_stored, i * 16 + 16)
                    sp.sem_inc(out_free, 1)

            @block.gpsimd
            def _(pool):
                scatter_batches(pg, pool, "m", SORT_BATCHES, MIX_BATCHES)

            @block.tensor
            def _(pe):
                pe.wait_ge(w_ready, 9 * 16)

                def queries(i, base):
                    pe.wait_ge(xT_loaded, i * 16 + 16)
                    for n in range(4):
                        pe.wait_ge(fm_free, base + (n + 1))
                        feature_block(nc, fm, wq, xT, n).then_inc(fm_ready, 1)

                def attention(i):
                    pe.wait_ge(qT_ready, i * 4 + 4)
                    for j in range(ST):
                        pe.wait_ge(att_free, i * ST + j + 1)
                        for h in range(KC):
                            last = nc.tensor.matmul(att[j % 2][:, h, :], qT[:, h, j * P:(j + 1) * P], pg.kv_blocks[:, h, :],
                                                    start=True, stop=True)
                        last.then_inc(att_ready, 1)

                def turn(i, ahead=True):
                    pe.wait_ge(x1_ready, i + 1)
                    transpose_rows(nc, pe, x1, pg.ident, tp, tp_ready, tp_free, i * NU)
                    pe.wait_ge(x1T_ready, i + 1)
                    for n in range(4):
                        pe.wait_ge(fm_free, hidden_base(i) + (n + 1))
                        feature_block(nc, fm, w1, x1T, n).then_inc(fm_ready, 1)
                    if ahead:
                        queries(i + 2, hidden_base(i) + 4)
                    pe.wait_ge(hT_ready, i * 4 + 4)
                    for j in range(ST):
                        pe.wait_ge(yp_free, i * ST + j + 1)
                        for c in range(KC):
                            last = nc.tensor.matmul(yp[j % 2][:, :], hT[:, c, j * P:(j + 1) * P], w2[:, c, :],
                                                    start=(c == 0), stop=(c == KC - 1))
                        last.then_inc(yp_ready, 1)
                    if ahead:
                        attention(i + 2)

                queries(0, 0)
                attention(0)
                queries(1, 4)
                attention(1)
                with pe.Fori(0, STEPS - 2) as i:
                    turn(i)
                turn(LAST - 1, False)
                turn(LAST, False)

            @block.scalar
            def _(act):
                act.sem_inc(tp_free, 2)
                act.sem_inc(fm_free, 2)
                act.sem_inc(att_free, 2)

                def load_xT(i):
                    act.dma_start(xT[:, :, :], feat_cols(pg.xT_d, i)).then_inc(xT_loaded, 16)

                def load_xn(i):
                    act.dma_start(xn[:, :, :], node_rows(pg.xn_d, i)).then_inc(xn_loaded, 16)

                def queries(i, base, first=False):
                    if not first:
                        act.wait_ge(qT_ready, i * 4)
                    for n in range(4):
                        m, h = n // 2, n % 2
                        act.wait_ge(fm_ready, base + (n + 1))
                        nc.scalar.activation(qexp[:, m, h * HN:(h + 1) * HN], fm[h][:, :], ACT.Exp).then_inc(q_ready, 1)
                        nc.scalar.activation(qpos[:, m, h * HN:(h + 1) * HN], fm[h][:, :], ACT.Relu).then_inc(q_ready, 1)
                        act.wait_ge(q_ready, i * 8 + (n * 2 + 2))
                        act.sem_inc(fm_free, 1)

                def attention(i):
                    act.wait_ge(sums_used, i + 1)
                    for j in range(ST):
                        act.wait_ge(att_ready, i * ST + j + 1)
                        nc.scalar.activation(sums[:, j, :, :], att[j % 2][:, :, :], ACT.Copy).then_inc(att_free, 1)
                    act.wait_ge(att_free, i * ST + ST + 2)
                    act.sem_inc(sums_ready, 1)

                def root(count):
                    act.wait_ge(var_ready, count)
                    nc.scalar.activation(std[:, :], rstd[:, :], ACT.Sqrt).then_inc(std_ready, 1)

                def turn(i, ahead, load_ahead):
                    for n in range(4):
                        m, h = n // 2, n % 2
                        act.wait_ge(fm_ready, hidden_base(i) + (n + 1))
                        nc.scalar.activation(hT[:, m, h * HN:(h + 1) * HN], fm[h][:, :], ACT.Gelu,
                                             bias=b1[:, m:m + 1]).then_inc(hT_ready, 1)
                        act.wait_ge(hT_ready, i * 4 + n + 1)
                        act.sem_inc(fm_free, 1)
                    if i is not LAST:
                        root(i * 2 + 2)
                    if ahead:
                        load_xn(i + 2)
                        queries(i + 2, hidden_base(i) + 4)
                        if load_ahead:
                            load_xT(i + 3)
                        attention(i + 2)
                    if i is not LAST:
                        copy_blocks(nc, act, x1T, tp, tp_ready, tp_free, x1T_ready, i * NU + NU)
                    root(second_root(i))

                load_xT(0)
                load_xn(0)
                act.wait_ge(w_ready, 9 * 16)
                queries(0, 0, True)
                load_xT(1)
                attention(0)
                root(1)
                load_xn(1)
                queries(1, 4)
                load_xT(2)
                attention(1)
                copy_blocks(nc, act, x1T, tp, tp_ready, tp_free, x1T_ready, 0)
                with act.Fori(0, STEPS - 3) as i:
                    turn(i, True, True)
                turn(STEPS - 3, True, False)
                turn(LAST - 1, False, False)
                turn(LAST, False, False)

            @block.vector
            def _(dve):
                dve.sem_inc(yp_free, 2)
                dve.sem_inc(sums_used, 1)
                dve.wait_ge(w_ready, 9 * 16)

                def queries(i, first=False):
                    if not first:
                        dve.wait_ge(att_ready, i * ST)
                    for n in range(4):
                        m, h = n // 2, n % 2
                        dve.wait_ge(q_ready, i * 8 + (n * 2 + 2))
                        nc.vector.scalar_tensor_tensor(out=qT[:, m, h * HN:(h + 1) * HN], in0=qexp[:, m, h * HN:(h + 1) * HN],
                                                       scalar=1.0, in1=qpos[:, m, h * HN:(h + 1) * HN], op0=ALU.min, op1=ALU.add
                                                       ).then_inc(qT_ready, 1)

                def first_norm(ch, i, count, first=False):
                    dve.wait_ge(sums_ready, i + 1)
                    ch(nc.vector.tensor_scalar_add(z[:, :, :, :], sums[:, :, :, P:P + HH], 1e-6))
                    ch(nc.vector.reciprocal(z[:, :, :, :], z[:, :, :, :]))
                    for h in range(KC):
                        ch.add(nc.vector.tensor_tensor(out=t[:, :, h * P:(h + 1) * P].rearrange("p j (g d) -> p j g d", g=HH),
                                                       in0=sums[:, :, h, 0:P].rearrange("p j (g d) -> p j g d", g=HH),
                                                       in1=z[:, :, h, :].unsqueeze(3).to_broadcast([P, ST, HH, HD]), op=ALU.mult))
                    ch.wait()
                    dve.sem_inc(sums_used, 1)
                    dve.wait_ge(xn_loaded, i * 16 + 16)
                    ch(nc.vector.tensor_tensor(out=t[:, :, :], in0=t[:, :, :], in1=xn[:, :, :], op=ALU.add))
                    norm_statistics(nc, dve, ch, pg.turns, t, stats, mv, rstd, var_ready, std, std_ready, count)
                    if not first:
                        dve.wait_ge(x1T_ready, i)
                    apply_norm(nc, ch, x1, t, mv, rstd, g1, be1)
                    dve.sem_inc(x1_ready, 1)

                def turn(base, i, ahead=True):
                    ch = Chain(dve, steps, base)
                    ch(nc.vector.tensor_tensor(out=rest[:, :, :], in0=x1[:, :, :],
                                               in1=b2[:, :].unsqueeze(1).to_broadcast([P, ST, C]), op=ALU.add))
                    if i is not LAST:
                        first_norm(ch, i + 1, i * 2 + 2)
                    if ahead:
                        queries(i + 2)
                    for j in range(ST):
                        dve.wait_ge(yp_ready, i * ST + j + 1)
                        ch(nc.vector.tensor_tensor(out=y[:, j, :], in0=rest[:, j, :], in1=yp[j % 2][:, :], op=ALU.add))
                        dve.sem_inc(yp_free, 1)
                    norm_statistics(nc, dve, ch, pg.turns, y, stats, mv, rstd, var_ready, std, std_ready, second_root(i))
                    dve.wait_ge(out_free, i + 1)
                    apply_norm(nc, ch, out, y, mv, rstd, g2, be2)
                    dve.sem_inc(out_ready, 1)
                    return ch.n

                queries(0, True)
                ch = Chain(dve, steps)
                first_norm(ch, 0, 1, True)
                queries(1)
                K = 1 + ch.n + ST + NORM_STEPS + 2 * ST
                with dve.Fori(0, STEPS - 2) as i:
                    n = turn(i * K + ch.n, i)
                    assert n == K
                turn(ch.n + (STEPS - 2) * K, LAST - 1, False)
                turn(ch.n + (STEPS - 1) * K, LAST, False)


def stage_gnn(pg):
    nc, a = pg.nc, pg.a
    pg.table_d = pg.dram("table_d", [NPAD, ROW]).ap()
    with ExitStack() as st:
        sb = lambda n, s, d=F32: st.enter_context(nc.sbuf_tensor("g_" + n, s, d))
        pb = lambda n, s, d=F32: st.enter_context(nc.psum_tensor("g_" + n, s, d))
        h2T = sb("h2T", [P, KC, NPAD])
        w1, w2 = sb("w1", [P, KC, C]), sb("w2", [P, KC, C])
        b1, b2, gamma, beta = (sb(n, [P, KC]) for n in ("b1", "b2", "gamma", "beta"))
        gain = sb("gain", [P, 1])
        scale, shift = sb("scale", [P, KC]), sb("shift", [P, KC])
        bstats, bmv, bvar, bstd = sb("bstats", [P, KC, 2 * STEPS, 6]), sb("bmv", [P, KC, 2]), sb("bvar", [P, KC]), sb("bstd", [P, KC])
        h0T = sb("h0T", [P, KC, SN])
        xT, hT = sb("xT", [P, KC, SN]), sb("hT", [P, KC, SN])
        fm = [pb(f"fm{i}", [P, HN]) for i in range(2)]
        tp = [pb(f"tp{i}", [P, 512]) for i in range(2)]
        tb = [pb(f"tb{i}", [P, 512]) for i in range(2)]
        gp = pb("gp", [P, ST, GF])
        w_ready, loaded, xT_free = pg.sem("g_w_ready"), pg.sem("g_loaded"), pg.sem("g_xT_free")
        steps, h0_ready, h0_used = pg.sem("g_steps"), pg.sem("g_h0_ready"), pg.sem("g_h0_used")
        bvar_ready = pg.sem("g_bvar_ready")
        fm_ready, fm_free, hT_ready, h2_ready = pg.sem("g_fm_ready"), pg.sem("g_fm_free"), pg.sem("g_hT_ready"), pg.sem("g_h2_ready")
        with nc.Block() as block:
            @block.gpsimd
            def _(pool):
                scatter_batches(pg, pool, "g", SORT_BATCHES + MIX_BATCHES, GNN_BATCHES)

            @block.sync
            def _(sp):
                sp.dma_start(w1[:, :, :], weights_of(a["gnn_w1"])).then_inc(w_ready, 16)
                sp.dma_start(w2[:, :, :], weights_of(a["gnn_w2"])).then_inc(w_ready, 16)
                with nc.allow_non_contiguous_dma(reason="vectors of 256"):
                    for d, v in ((b1, "gnn_b1"), (b2, "gnn_b2"), (gamma, "gnn_gamma"), (beta, "gnn_beta")):
                        sp.dma_start(d[:, :], col_of(a[v])).then_inc(w_ready, 16)
                sp.dma_start(gain[:, :], a["gnn_eps"].to_broadcast([P, 1])).then_inc(w_ready, 16)
                with sp.Fori(0, STEPS) as i:
                    sp.wait_ge(xT_free, i + 1)
                    sp.dma_start(xT[:, :, :], feat_cols(pg.xT_d, i)).then_inc(loaded, 16)

            @block.vector
            def _(dve):
                dve.sem_inc(xT_free, 1)
                dve.wait_ge(w_ready, 7 * 16)
                ch = Chain(dve, steps)
                ch(nc.vector.tensor_scalar_add(gain[:, :], gain[:, :], 1.0))
                with dve.Fori(0, STEPS) as i:
                    dve.wait_ge(loaded, i * 16 + 16)
                    dve.wait_ge(h0_used, i + 1)
                    nc.vector.scalar_tensor_tensor(out=h0T[:, :, :], in0=xT[:, :, :], scalar=gain[:, 0:1],
                                                   in1=pg.agg[:, :, bass.ds(i * SN, SN)], op0=ALU.mult, op1=ALU.add
                                                   ).then_inc(h0_ready, 1)
                    dve.wait_ge(h0_ready, i + 1)
                    dve.sem_inc(xT_free, 1)
                dve.wait_ge(h2_ready, 4 * STEPS)
                for m in range(KC):
                    for k in range(2 * STEPS):
                        ch.add(nc.vector.bn_stats(out=bstats[:, m, k, :], in_=h2T[:, m, k * HN:min((k + 1) * HN, N_NODES)]))
                ch.wait()
                for m in range(KC):
                    ch.add(nc.vector.bn_aggr(out=bmv[:, m, :], in_=bstats[:, m, :, :].rearrange("p k s -> p (k s)")))
                ch.wait()
                ch(nc.vector.tensor_scalar_add(bvar[:, :], bmv[:, :, 1], 1e-5))
                dve.sem_inc(bvar_ready, 1)
                dve.wait_ge(h2_ready, 4 * STEPS + 1)
                ch(nc.vector.reciprocal(bvar[:, :], bstd[:, :]))
                ch(nc.vector.tensor_tensor(out=scale[:, :], in0=bvar[:, :], in1=gamma[:, :], op=ALU.mult))
                ch(nc.vector.tensor_tensor(out=shift[:, :], in0=bmv[:, :, 0], in1=scale[:, :], op=ALU.mult))
                ch(nc.vector.tensor_tensor(out=shift[:, :], in0=beta[:, :], in1=shift[:, :], op=ALU.subtract))

            @block.scalar
            def _(act):
                act.sem_inc(fm_free, 2)
                act.wait_ge(w_ready, 7 * 16)
                with act.Fori(0, STEPS) as i:
                    for n in range(4):
                        m, h = n // 2, n % 2
                        act.wait_ge(fm_ready, i * 8 + n + 1)
                        nc.scalar.activation(hT[:, m, h * HN:(h + 1) * HN], fm[n % 2][:, :], ACT.Relu,
                                             bias=b1[:, m:m + 1]).then_inc(fm_free, 1)
                    act.wait_ge(fm_free, i * 8 + 6)
                    act.sem_inc(hT_ready, 1)
                    for n in range(4):
                        m, h = n // 2, n % 2
                        act.wait_ge(fm_ready, i * 8 + n + 5)
                        nc.scalar.activation(h2T[:, m, bass.ds(i * SN + h * HN, HN)], fm[n % 2][:, :], ACT.Identity,
                                             bias=b2[:, m:m + 1]).then_inc(fm_free, 1)
                    act.wait_ge(fm_free, i * 8 + 10)
                    act.sem_inc(h2_ready, 4)
                act.wait_ge(bvar_ready, 1)
                nc.scalar.activation(bstd[:, :], bvar[:, :], ACT.Sqrt).then_inc(h2_ready, 1)

            @block.tensor
            def _(pe):
                pe.sem_inc(h0_used, 1)
                pe.wait_ge(w_ready, 7 * 16)
                with pe.Fori(0, STEPS) as i:
                    pe.wait_ge(h0_ready, i + 1)
                    for n in range(4):
                        pe.wait_ge(fm_free, i * 8 + n + 1)
                        feature_block(nc, fm, w1, h0T, n).then_inc(fm_ready, 1)
                    pe.wait_ge(hT_ready, i + 1)
                    pe.sem_inc(h0_used, 1)
                    for n in range(4):
                        pe.wait_ge(fm_free, i * 8 + n + 5)
                        feature_block(nc, fm, w2, hT, n).then_inc(fm_ready, 1)

        x_in, mix, x2 = sb("x_in", [P, ST, C]), sb("mix", [P, ST, C]), sb("x2", [P, ST, C])
        x3, x3T, rT = sb("x3", [P, ST, C]), xT, hT
        stats, mv, std, rstd = sb("stats", [P, ST, 6]), sb("mv", [P, ST, 2]), sb("std", [P, ST]), sb("rstd", [P, ST])
        wg = sb("wg", [P, KC, GF])
        att_s, att_d = sb("att_s", [P, GF]), sb("att_d", [P, GF])
        trow, prod = sb("trow", [P, ST, ROW]), sb("prod", [P, ST, GF])
        w3_ready, in_ready = pg.sem("j_w_ready"), pg.sem("j_in_ready")
        jsteps, rT_ready = pg.sem("j_steps"), pg.sem("j_rT_ready")
        bp_ready, bp_free = pg.sem("j_bp_ready"), pg.sem("j_bp_free")
        var_ready, std_ready, x2_ready, x3_ready = pg.sem("j_var_ready"), pg.sem("j_std_ready"), pg.sem("j_x2_ready"), pg.sem("j_x3_ready")
        x2_stored, x3T_stored, trow_stored = pg.sem("j_x2_stored"), pg.sem("j_x3T_stored"), pg.sem("j_trow_stored")
        loops_out = pg.sem("j_loops_out")
        x2_free, x3T_free, trow_free = pg.sem("j_x2_free"), pg.sem("j_x3T_free"), pg.sem("j_trow_free")
        tq_ready, tq_free, x3T_ready = pg.sem("j_tq_ready"), pg.sem("j_tq_free"), pg.sem("j_x3T_ready")
        gp_ready, trow_ready = pg.sem("j_gp_ready"), pg.sem("j_trow_ready")
        with nc.Block() as block:
            @block.sync
            def _(sp):
                sp.dma_start(wg[:, :, :], weights_of(a["w_gat"])).then_inc(w3_ready, 16)
                sp.dma_start(att_s[:, :], row_of(a["att_src"].rearrange("h e -> (h e)"), GF)).then_inc(w3_ready, 16)
                sp.dma_start(att_d[:, :], row_of(a["att_dst"].rearrange("h e -> (h e)"), GF)).then_inc(w3_ready, 16)

                def load(i):
                    sp.dma_start(x_in[:, :, :], node_rows(pg.xpad, i)).then_inc(in_ready, 16)
                    sp.dma_start(mix[:, :, :], node_rows(pg.mix_d, i)).then_inc(in_ready, 16)

                def store(i, more=True):
                    sp.wait_ge(x2_ready, i + 1)
                    sp.sem_inc(pg.turns, 1)
                    sp.dma_start(node_rows(pg.x2_d, i), x2[:, :, :]).then_inc(x2_stored, 16)
                    if more:
                        load(i + 1)
                    sp.wait_ge(x2_stored, i * 16 + 16)
                    sp.sem_inc(x2_free, 1)

                def store_table(i):
                    sp.wait_ge(trow_ready, i + 1)
                    sp.sem_inc(pg.turns, 1)
                    sp.dma_start(node_rows(pg.table_d, i), trow[:, :, :]).then_inc(trow_stored, 16)
                    sp.wait_ge(trow_stored, i * 16 + 16)
                    sp.sem_inc(trow_free, 1)

                sp.sem_inc(x2_free, 1)
                sp.sem_inc(trow_free, 1)
                load(0)
                store(0)
                with sp.Fori(0, LAST - 1) as i:
                    store(i + 1)
                    store_table(i)
                store(LAST, False)
                store_table(LAST - 1)
                store_table(LAST)

            @block.gpsimd
            def _(pool):
                scatter_batches(pg, pool, "j", SORT_BATCHES + MIX_BATCHES + GNN_BATCHES, SUM_BATCHES)
                for t in range(NT):
                    pool.indirect_dma_start(out=pg.sorted_d, out_offset=bass.IndirectOffsetOnAxis(ap=pg.first[:, t:t + 1], axis=0),
                                            in_=pg.node_id[:, t:t + 1], in_offset=None).then_inc(loops_out, 16)
                pool.wait_ge(loops_out, 16 * NT)

            @block.scalar
            def _(act):
                act.sem_inc(tq_free, 2)
                act.sem_inc(bp_free, 2)

                def rectify(i):
                    for m in range(KC):
                        nc.scalar.activation(rT[:, m, :], h2T[:, m, bass.ds(i * SN, SN)], ACT.Relu,
                                             bias=shift[:, m:m + 1], scale=scale[:, m:m + 1]).then_inc(rT_ready, 1)

                def root(i):
                    act.wait_ge(var_ready, i + 1)
                    nc.scalar.activation(std[:, :], rstd[:, :], ACT.Sqrt).then_inc(std_ready, 1)

                def copy(i):
                    act.wait_ge(x3T_free, i + 1)
                    copy_blocks(nc, act, x3T, tp, tq_ready, tq_free, x3T_ready, i * NU)
                    act.dma_start(feat_cols(pg.x3T_d, i), x3T[:, :, :]).then_inc(x3T_stored, 16)

                def free(i):
                    act.wait_ge(x3T_stored, i * 16 + 16)
                    act.sem_inc(x3T_free, 1)

                act.sem_inc(x3T_free, 1)
                rectify(0)
                root(0)
                with act.Fori(0, LAST) as i:
                    act.wait_ge(bp_ready, i * NU + NU)
                    rectify(i + 1)
                    copy(i)
                    root(i + 1)
                    free(i)
                copy(LAST)
                free(LAST)

            @block.tensor
            def _(pe):
                pe.wait_ge(w3_ready, 48)

                def turn_back(i):
                    pe.wait_ge(rT_ready, i * 2 + 2)
                    for u, (q0, nq) in enumerate(UNITS):
                        pe.wait_ge(bp_free, i * NU + (u + 1))
                        for q in range(q0, q0 + nq):
                            last = nc.tensor.transpose(tb[u % 2][:, (q - q0) * P:(q - q0 + 1) * P],
                                                       rT[:, q % KC, (q // KC) * P:(q // KC + 1) * P], pg.ident[:, :])
                        last.then_inc(bp_ready, 1)

                def turn(i):
                    pe.wait_ge(x3_ready, i + 1)
                    transpose_rows(nc, pe, x3, pg.ident, tp, tq_ready, tq_free, i * NU)

                def project(i):
                    pe.wait_ge(x3T_ready, i + 1)
                    pe.wait_ge(trow_free, i + 1)
                    for j in range(ST):
                        for c in range(KC):
                            last = nc.tensor.matmul(gp[:, j, :], x3T[:, c, j * P:(j + 1) * P], wg[:, c, :],
                                                    start=(c == 0), stop=(c == KC - 1))
                    last.then_inc(gp_ready, 1)

                turn_back(0)
                with pe.Fori(0, LAST) as i:
                    turn_back(i + 1)
                    turn(i)
                    project(i)
                turn(LAST)
                project(LAST)

            @block.vector
            def _(dve):
                dve.wait_ge(w3_ready, 48)
                ch = Chain(dve, jsteps)
                ch(nc.vector.memset(pg.starts[:, :, :], 0.0))
                ch(nc.vector.memset(pg.starts[:, :, 0:1], 1.0))

                def add_and_norm(ch, i, first=False):
                    dve.wait_ge(in_ready, i * 32 + 32)
                    dve.wait_ge(x2_free, i + 1)
                    x2f = x2[:, :, :].rearrange("p j c -> p (j c)")
                    xf = x_in[:, :, :].rearrange("p j c -> p (j c)")
                    for u, (q0, nq) in enumerate(UNITS):
                        dve.wait_ge(bp_ready, i * NU + (u + 1))
                        ch(nc.vector.tensor_tensor(out=x2f[:, q0 * P:(q0 + nq) * P], in0=xf[:, q0 * P:(q0 + nq) * P],
                                                   in1=tb[u % 2][:, 0:nq * P], op=ALU.add))
                        dve.sem_inc(bp_free, 1)
                    ch(nc.vector.tensor_tensor(out=x2[:, :, :], in0=x2[:, :, :], in1=mix[:, :, :], op=ALU.add))
                    dve.sem_inc(x2_ready, 1)
                    norm_statistics(nc, dve, ch, pg.turns, x2, stats, mv, rstd, var_ready, std, std_ready, i + 1)
                    if not first:
                        dve.wait_ge(x3T_ready, i)
                    normalise(nc, ch, x3, x2, mv, rstd)
                    dve.sem_inc(x3_ready, 1)

                def logits(ch, i):
                    dve.wait_ge(gp_ready, i + 1)
                    ch(nc.vector.tensor_copy(trow[:, :, 0:GF], gp[:, :, :]))
                    ch(nc.vector.tensor_tensor(out=prod[:, :, :], in0=trow[:, :, 0:GF],
                                               in1=att_s[:, :].unsqueeze(1).to_broadcast([P, ST, GF]), op=ALU.mult))
                    ch(nc.vector.tensor_reduce(out=trow[:, :, GF:ROW], in_=prod[:, :, :].rearrange("p j (h e) -> p j h e", h=HEADS),
                                               axis=AX, op=ALU.add))
                    dve.sem_inc(trow_ready, 1)
                    ch(nc.vector.tensor_tensor(out=prod[:, :, :], in0=trow[:, :, 0:GF],
                                               in1=att_d[:, :].unsqueeze(1).to_broadcast([P, ST, GF]), op=ALU.mult))
                    ch(nc.vector.tensor_reduce(out=pg.starts[:, bass.ds(i * ST, ST), 1:1 + HEADS],
                                               in_=prod[:, :, :].rearrange("p j (h e) -> p j h e", h=HEADS), axis=AX, op=ALU.add))

                add_and_norm(ch, 0, True)
                K = NU + 1 + NORM_STEPS + ST + 5
                with dve.Fori(0, LAST) as i:
                    turn_ch = Chain(dve, jsteps, i * K + ch.n)
                    add_and_norm(turn_ch, i + 1)
                    logits(turn_ch, i)
                    assert turn_ch.n == K
                logits(Chain(dve, jsteps, ch.n + LAST * K), LAST)


GC = 29
NG = RUN // GC
assert RUN % GC == 0 and NG % 2 == 1 and NG >= STEPS * EXPERTS
PICK = 512 // (STATE + 1)


class HandOn:

    def __init__(self, pg, name, hand, give, giveT, carryT, carry):
        self.pg, self.hand, self.give, self.giveT, self.carryT, self.carry = pg, hand, give, giveT, carryT, carry
        self.give_ready, self.giveT_ready, self.carryT_ready, self.carry_ready = (
            pg.sem(f"{name}_{n}") for n in ("give_ready", "giveT_ready", "carryT_ready", "carry_ready"))

    def tensor(self, pe, n, w):
        nc, hand = self.pg.nc, self.hand
        pe.wait_ge(self.give_ready, n + 1)
        for m in range(2):
            last = nc.tensor.transpose(hand[0:w, m, :], self.give[:, m, 0:w], self.pg.ident[:, :])
        last.then_inc(self.giveT_ready, 1)
        pe.wait_ge(self.carryT_ready, n + 1)
        nc.tensor.transpose(hand[:, 2, 0:w], self.carryT[0:w, 0:P], self.pg.ident[0:w, 0:w]).then_inc(self.carry_ready, 1)

    def vector(self, dve, ch, n, w, op0, op1, initial):
        V, giveT, carryT = self.pg.nc.vector, self.giveT, self.carryT
        dve.sem_inc(self.give_ready, 1)
        dve.wait_ge(self.giveT_ready, n + 1)
        ch(V.tensor_copy(giveT[0:w, :, :], self.hand[0:w, 0:2, :]))
        ch(V.memset(carryT[0:w, 0:1], initial))
        ch(V.tensor_tensor_scan(out=carryT[0:w, 1:P + 1], data0=giveT[0:w, 0, :], data1=giveT[0:w, 1, :],
                                initial=initial, op0=op0, op1=op1))
        dve.sem_inc(self.carryT_ready, 1)
        dve.wait_ge(self.carry_ready, n + 1)
        ch(V.tensor_copy(self.carry[:, 0:w], self.hand[:, 2, 0:w]))


DEST_STEPS = 3 + 2 * HEADS + 1 + 4 + HEADS


def stage_attend(pg):
    nc, a = pg.nc, pg.a
    starts_d = pg.dram("starts_d", [P * RUN, START]).ap()
    with ExitStack() as st:
        sb = lambda n, s, d=F32: st.enter_context(nc.sbuf_tensor("a_" + n, s, d))
        pb = lambda n, s, d=F32: st.enter_context(nc.psum_tensor("a_" + n, s, d))
        order = sb("order", [P, RUN], I32)
        heads = sb("heads", [P, RUN, START])
        keep, fresh, junk = sb("keep", [P, RUN]), sb("fresh", [P, RUN]), sb("junk", [P, RUN])
        index = [sb(f"index{b}", [P, GC], I32) for b in range(2)]
        got = [sb(f"got{b}", [P, GC, ROW]) for b in range(2)]
        scaled = [sb(f"scaled{b}", [P, GC, STATE]) for b in range(2)]
        powers = sb("powers", [P, GC, 2 * HEADS])
        give, giveT = sb("give", [P, 2, ROW]), sb("giveT", [ROW, 2, P])
        carryT, carry = sb("carryT", [ROW, P + 1]), sb("carry", [P, ROW])
        hand = pb("hand", [P, 3, P])
        zeroed, scattered, loaded = pg.sem("a_zeroed"), pg.sem("a_scattered"), pg.sem("a_loaded")
        heads_ready, index_ready = pg.sem("a_heads_ready"), pg.sem("a_index_ready")
        gathered = [pg.sem(f"a_gathered{b}") for b in range(2)]
        got_used, exp_in, exp_out = pg.sem("a_got_used"), pg.sem("a_exp_in"), pg.sem("a_exp_out")
        scaled_ready = pg.sem("a_scaled_ready")
        stored = [pg.sem(f"a_stored{b}") for b in range(2)]
        hands = HandOn(pg, "a", hand, give, giveT, carryT, carry)
        steps = pg.sem("a_steps")
        CHUNK_STEPS = 11 + ROW
        with nc.Block() as block:
            @block.sync
            def _(sp):
                sp.dma_start(order[:, :], pg.sorted_d.rearrange("(p c) o -> p (c o)", p=P)).then_inc(loaded, 16)
                z = pg.zeros[:, 0:START * GC].unsqueeze(1).to_broadcast([P, NG, START * GC])
                sp.dma_start(starts_d.rearrange("(p c) k -> p (c k)", p=P).rearrange("p (r z) -> p r z", z=START * GC), z).then_inc(zeroed, 16)
                sp.wait_ge(scattered, 16 * NT)
                sp.dma_start(heads[:, :, :], starts_d.rearrange("(p c) k -> p c k", p=P)).then_inc(heads_ready, 16)

                def store(k, b):
                    sp.wait_ge(scaled_ready, k + 1)
                    sp.dma_start(pg.sums_d.rearrange("(p c) k -> p c k", p=P)[:, bass.ds(k * GC, GC), :],
                                 scaled[b][:, :, :]).then_inc(stored[b], 16)

                with sp.Fori(0, NG // 2) as i:
                    store(i * 2, 0)
                    store(i * 2 + 1, 1)
                store(NG - 1, 0)
                for b in range(2):
                    sp.wait_ge(stored[b], 16 * (NG // 2 + 1 - b))

            @block.gpsimd
            def _(pool):
                pool.wait_ge(zeroed, 16)
                for t in range(NT):
                    pool.indirect_dma_start(out=starts_d, out_offset=bass.IndirectOffsetOnAxis(ap=pg.first[:, t:t + 1], axis=0),
                                            in_=pg.starts[:, t, :], in_offset=None).then_inc(scattered, 16)
                pool.wait_ge(loaded, 16)

                def gather(i, b, first=False):
                    k = i * 2 + b
                    if not first:
                        pool.wait_ge(got_used, k - 1)
                    nc.gpsimd.tensor_copy(index[b][:, :], order[:, bass.ds(k * GC, GC)]).then_inc(index_ready, 1)
                    pool.wait_ge(index_ready, k + 1)
                    pool.sem_inc(pg.turns, 1)
                    for t in range(GC):
                        pool.indirect_dma_start(out=got[b][:, t, :], out_offset=None, in_=pg.table_d,
                                                in_offset=bass.IndirectOffsetOnAxis(ap=index[b][:, t:t + 1], axis=0)
                                                ).then_inc(gathered[b], 16)

                gather(0, 0, True)
                gather(0, 1, True)
                with pool.Fori(1, NG // 2) as i:
                    gather(i, 0)
                    gather(i, 1)
                gather(NG // 2, 0)

            def exponents(act, k):
                act.wait_ge(exp_in, k + 1)
                nc.scalar.activation(powers[:, :, :], powers[:, :, :], ACT.Exp).then_inc(exp_out, 1)

            def destination_logits(dve, ch):
                V = nc.vector
                dve.wait_ge(heads_ready, 16)
                ch.add(V.tensor_scalar(out=keep[:, :], in0=heads[:, :, 0], scalar1=-1.0, scalar2=1.0, op0=ALU.mult, op1=ALU.add))
                ch(V.tensor_scalar(out=fresh[:, :], in0=heads[:, :, 0], scalar1=-BIG, scalar2=None, op0=ALU.mult))
                ch(V.tensor_reduce(out=pg.whole[:, :], in_=keep[:, :], axis=AX, op=ALU.min))
                for h in range(HEADS):
                    ch(V.tensor_tensor_scan(out=junk[:, :], data0=keep[:, :], data1=heads[:, :, 1 + h], initial=0.0,
                                            op0=ALU.mult, op1=ALU.add))
                    ch(V.tensor_copy(give[:, 1, h:h + 1], junk[:, RUN - 1:RUN]))
                ch(V.tensor_copy(give[:, 0, 0:HEADS], pg.whole[:, 0:1].to_broadcast([P, HEADS])))
                hands.vector(dve, ch, 0, HEADS, ALU.mult, ALU.add, 0.0)
                for h in range(HEADS):
                    ch.add(V.tensor_tensor_scan(out=heads[:, :, 1 + h], data0=keep[:, :], data1=heads[:, :, 1 + h],
                                                initial=carry[:, h:h + 1], op0=ALU.mult, op1=ALU.add))
                ch.wait()

            def chunk(dve, ch, k, b, turn, first=False, fresh_slot=False):
                V = nc.vector
                cols = bass.ds(k * GC, GC)
                before, now = scaled[1 - b], scaled[b]
                logits, tops = got[b][:, :, GF:ROW], now[:, :, ROW:STATE]
                dve.wait_ge(gathered[b], turn * (16 * GC) + 16 * GC)
                if not fresh_slot:
                    dve.wait_ge(stored[b], turn * 16)
                ch(V.tensor_tensor(out=logits, in0=logits, in1=heads[:, cols, 1:1 + HEADS], op=ALU.add))
                ch(V.scalar_tensor_tensor(out=logits, in0=logits, scalar=0.2, in1=logits, op0=ALU.mult, op1=ALU.max))
                for h in range(HEADS):
                    ch.add(V.tensor_tensor_scan(out=now[:, :, ROW + h], data0=fresh[:, cols], data1=got[b][:, :, GF + h],
                                                initial=-BIG if first else before[:, GC - 1, ROW + h:ROW + h + 1],
                                                op0=ALU.add, op1=ALU.max))
                ch.wait()
                ch.add(V.tensor_tensor(out=powers[:, 1:GC, 0:HEADS], in0=tops[:, 0:GC - 1, :], in1=tops[:, 1:GC, :], op=ALU.subtract))
                if first:
                    ch.add(V.tensor_scalar(out=powers[:, 0, 0:HEADS], in0=tops[:, 0, :], scalar1=-1.0, scalar2=-BIG,
                                           op0=ALU.mult, op1=ALU.add))
                else:
                    ch.add(V.tensor_tensor(out=powers[:, 0, 0:HEADS], in0=before[:, GC - 1, ROW:STATE], in1=tops[:, 0, :], op=ALU.subtract))
                ch(V.tensor_tensor(out=powers[:, :, HEADS:], in0=logits, in1=tops, op=ALU.subtract))
                nc.vector.tensor_scalar_min(powers[:, :, :], powers[:, :, :], 0.0).then_inc(exp_in, 1)
                dve.wait_ge(exp_out, k + 1)
                ch.add(V.tensor_tensor(out=powers[:, :, 0:HEADS], in0=powers[:, :, 0:HEADS],
                                       in1=keep[:, cols].unsqueeze(2).to_broadcast([P, GC, HEADS]), op=ALU.mult))
                feats = got[b][:, :, 0:GF].rearrange("p c (h e) -> p c h e", h=HEADS)
                ch(V.tensor_tensor(out=feats, in0=feats, in1=powers[:, :, HEADS:].unsqueeze(3).to_broadcast([P, GC, HEADS, EXPERTS]),
                                   op=ALU.mult))
                for c in range(ROW):
                    h = c // EXPERTS if c < GF else c - GF
                    ch.add(V.tensor_tensor_scan(out=now[:, :, c], data0=powers[:, :, h],
                                                data1=got[b][:, :, c] if c < GF else powers[:, :, HEADS + h],
                                                initial=0.0 if first else before[:, GC - 1, c:c + 1], op0=ALU.mult, op1=ALU.add))
                ch.wait()
                dve.sem_inc(got_used, 1)
                dve.sem_inc(scaled_ready, 1)


            def scan_first(pe):
                hands.tensor(pe, 0, HEADS)

            before = DEST_STEPS

            def chunks_first(dve):
                ch = Chain(dve, steps)
                destination_logits(dve, ch)
                assert ch.n == before, ch.n

            def chunk_beside(dve, i, e, first=False):
                if first:
                    ch = Chain(dve, steps, before + e * CHUNK_STEPS)
                    chunk(dve, ch, e, e % 2, e // 2, e == 0, e < 2)
                else:
                    ch = Chain(dve, steps, before + (i * EXPERTS + e) * CHUNK_STEPS)
                    chunk(dve, ch, i * EXPERTS + e, e % 2, i * (EXPERTS // 2) + e // 2)
                assert ch.n == CHUNK_STEPS, ch.n

            def chunks_last(dve):
                done = STEPS * EXPERTS
                with dve.Fori(done // 2, NG // 2) as j:
                    for b in range(2):
                        chunk(dve, Chain(dve, steps, before + (j * 2 + b) * CHUNK_STEPS), j * 2 + b, b, j)
                ch = Chain(dve, steps, before + (NG - 1) * CHUNK_STEPS)
                chunk(dve, ch, NG - 1, 0, NG // 2)
                ch(nc.vector.tensor_copy(pg.run_end[:, :], scaled[0][:, GC - 1, :]))

            def exponents_last(act):
                with act.Fori(STEPS * EXPERTS, NG) as k:
                    exponents(act, k)

            experts(pg, block, st, scan_first, chunks_first, chunk_beside, chunks_last, exponents, exponents_last)


def join(pg, block, st):
    nc = pg.nc
    last_d = pg.dram("last_d", [NT, P]).ap()
    sb = lambda n, s, d=F32: st.enter_context(nc.sbuf_tensor("o_" + n, s, d))
    pb = lambda n, s, d=F32: st.enter_context(nc.psum_tensor("o_" + n, s, d))
    local = sb("local", [P, NT, STATE])
    run_start, run_stop = sb("run_start", [P, 1]), sb("run_stop", [P, 1])
    last_f, first_f, lastT = sb("last_f", [P, NT]), sb("first_f", [P, NT]), sb("lastT", [NT, P])
    last_row, in_run = sb("last_row", [P, NPAD]), sb("in_run", [P, NPAD])
    give, giveT = sb("give", [P, 2, ROW]), sb("giveT", [ROW, 2, P])
    carryT, carry = sb("carryT", [ROW, P + 1]), sb("carry", [P, ROW])
    top = sb("top", [P, HEADS])
    scale = sb("scale", [P, 2 * HEADS])
    handed = sb("handed", [P, STATE + 1])
    ahead = sb("ahead", [P, NT, STATE + 1])
    starts_before = sb("starts_before", [P, NT])
    tops = sb("tops", [P, NT, HEADS])
    powers = sb("powers", [P, NT, 2 * HEADS])
    hand = pb("hand", [P, 3, P])
    picked = [pb(f"picked{b}", [P, PICK, STATE + 1]) for b in range(-(-NT // PICK))]
    hands = HandOn(pg, "o", hand, give, giveT, carryT, carry)
    run_ready, fetched, steps = pg.sem("o_run_ready"), pg.sem("o_fetched"), pg.sem("o_steps")
    last_ready, lastT_ready, lastT_out, row_ready = (
        pg.sem("o_" + n) for n in ("last_ready", "lastT_ready", "lastT_out", "row_ready"))
    lastT_stored = pg.sem("o_lastT_stored")
    exp_in, exp_out, table_ready = pg.sem("o_exp_in"), pg.sem("o_exp_out"), pg.sem("o_table_ready")
    picked_ready, ahead_ready = pg.sem("o_picked_ready"), pg.sem("o_ahead_ready")

    @block.gpsimd
    def _(pool):
        nc.gpsimd.iota(run_start[:, :], pattern=[[0, 1]], base=0, channel_multiplier=RUN,
                       allow_small_or_imprecise_dtypes=True).then_inc(run_ready, 1)
        for t in range(NT):
            pool.indirect_dma_start(out=local[:, t, :], out_offset=None, in_=pg.sums_d,
                                    in_offset=bass.IndirectOffsetOnAxis(ap=pg.last[:, t:t + 1], axis=0)).then_inc(fetched, 16)

    @block.sync
    def _(sp):
        sp.wait_ge(lastT_out, 1)
        sp.dma_start(last_d, lastT[:, :]).then_inc(lastT_stored, 16)
        sp.wait_ge(lastT_stored, 16)
        sp.dma_start(last_row[:, :], row_of(last_d.rearrange("t p -> (t p)"), NPAD)).then_inc(row_ready, 16)

    @block.tensor
    def _(pe):
        pe.wait_ge(last_ready, 1)
        nc.tensor.transpose(picked[0][:, :, :].rearrange("p t k -> p (t k)")[0:NT, 0:P], last_f[:, :],
                            pg.ident[:, :]).then_inc(lastT_ready, 1)
        hands.tensor(pe, 0, HEADS)
        hands.tensor(pe, 1, ROW)
        pe.wait_ge(table_ready, 1)
        for t in range(NT):
            nc.tensor.matmul(picked[t // PICK][:, t % PICK, :], in_run[:, t * P:(t + 1) * P], handed[:, :],
                             start=True, stop=True).then_inc(picked_ready, 1)

    @block.scalar
    def _(act):
        act.wait_ge(exp_in, 1)
        nc.scalar.activation(scale[:, :], scale[:, :], ACT.Exp).then_inc(exp_out, 1)
        for b in range(len(picked)):
            n = min(PICK, NT - b * PICK)
            act.wait_ge(picked_ready, b * PICK + n)
            nc.scalar.activation(ahead[:, b * PICK:b * PICK + n, :], picked[b][:, 0:n, :], ACT.Copy).then_inc(ahead_ready, 1)
        act.wait_ge(exp_in, 2)
        nc.scalar.activation(powers[:, :, :], powers[:, :, :], ACT.Exp).then_inc(exp_out, 1)

    @block.vector
    def _(dve):
        ch = Chain(dve, steps)
        V = nc.vector
        ch.add(V.tensor_copy(first_f[:, :], pg.first[:, :]))
        ch(V.tensor_copy(last_f[:, :], pg.last[:, :]))
        dve.sem_inc(last_ready, 1)
        dve.wait_ge(lastT_ready, 1)
        ch(V.tensor_copy(lastT[:, :], picked[0][:, :, :].rearrange("p t k -> p (t k)")[0:NT, 0:P]))
        dve.sem_inc(lastT_out, 1)
        end_sums, end_tops = pg.run_end[:, 0:ROW], pg.run_end[:, ROW:STATE]
        ch.add(V.tensor_copy(give[:, 1, 0:HEADS], end_tops))
        ch(V.tensor_scalar(out=give[:, 0, 0:HEADS], in0=pg.whole[:, 0:1].to_broadcast([P, HEADS]), scalar1=-1.0,
                           scalar2=BIG, op0=ALU.add, op1=ALU.mult))
        hands.vector(dve, ch, 0, HEADS, ALU.add, ALU.max, -BIG)
        ch.add(V.tensor_copy(handed[:, ROW:STATE], carry[:, 0:HEADS]))
        ch(V.tensor_tensor(out=top[:, :], in0=carry[:, 0:HEADS], in1=give[:, 0, 0:HEADS], op=ALU.add))
        ch(V.tensor_tensor(out=top[:, :], in0=top[:, :], in1=end_tops, op=ALU.max))
        ch.add(V.tensor_tensor(out=scale[:, 0:HEADS], in0=carry[:, 0:HEADS], in1=top[:, :], op=ALU.subtract))
        ch(V.tensor_tensor(out=scale[:, HEADS:], in0=end_tops, in1=top[:, :], op=ALU.subtract))
        ch(V.tensor_scalar_min(scale[:, :], scale[:, :], 0.0))
        dve.sem_inc(exp_in, 1)
        dve.wait_ge(exp_out, 1)
        ch.add(V.tensor_scalar(out=give[:, 0, GF:ROW], in0=scale[:, 0:HEADS], scalar1=pg.whole[:, 0:1], scalar2=None, op0=ALU.mult))
        ch.add(V.tensor_tensor(out=give[:, 1, GF:ROW], in0=end_sums[:, GF:ROW], in1=scale[:, HEADS:], op=ALU.mult))
        ch(V.tensor_tensor(out=give[:, 1, 0:GF].rearrange("p (h e) -> p h e", h=HEADS),
                           in0=end_sums[:, 0:GF].rearrange("p (h e) -> p h e", h=HEADS),
                           in1=scale[:, HEADS:].unsqueeze(2).to_broadcast([P, HEADS, EXPERTS]), op=ALU.mult))
        ch(V.tensor_copy(give[:, 0, 0:GF].rearrange("p (h e) -> p h e", h=HEADS),
                         give[:, 0, GF:ROW].unsqueeze(2).to_broadcast([P, HEADS, EXPERTS])))
        hands.vector(dve, ch, 1, ROW, ALU.mult, ALU.add, 0.0)
        dve.wait_ge(run_ready, 1)
        ch.add(V.tensor_copy(handed[:, 0:ROW], carry[:, :]))
        ch.add(V.tensor_copy(handed[:, STATE:STATE + 1], run_start[:, :]))
        ch(V.tensor_scalar_add(run_stop[:, :], run_start[:, :], float(RUN)))
        dve.wait_ge(row_ready, 16)
        ch(V.tensor_scalar(out=in_run[:, :], in0=last_row[:, :], scalar1=run_start[:, 0:1], scalar2=None, op0=ALU.is_ge))
        ch(V.scalar_tensor_tensor(out=in_run[:, :], in0=last_row[:, :], scalar=run_stop[:, 0:1], in1=in_run[:, :],
                                  op0=ALU.is_lt, op1=ALU.mult))
        dve.sem_inc(table_ready, 1)
        dve.wait_ge(ahead_ready, len(picked))
        ch(V.tensor_tensor(out=starts_before[:, :], in0=first_f[:, :], in1=ahead[:, :, STATE], op=ALU.is_lt))
        ch(V.tensor_scalar(out=starts_before[:, :], in0=starts_before[:, :], scalar1=-1.0, scalar2=BIG, op0=ALU.add, op1=ALU.mult))
        before_tops = ahead[:, :, ROW:STATE]
        ch(V.tensor_tensor(out=before_tops, in0=before_tops, in1=starts_before[:, :].unsqueeze(2).to_broadcast([P, NT, HEADS]),
                           op=ALU.add))
        dve.wait_ge(fetched, 16 * NT)
        ch(V.tensor_tensor(out=tops[:, :, :], in0=before_tops, in1=local[:, :, ROW:STATE], op=ALU.max))
        ch.add(V.tensor_tensor(out=powers[:, :, 0:HEADS], in0=before_tops, in1=tops[:, :, :], op=ALU.subtract))
        ch(V.tensor_tensor(out=powers[:, :, HEADS:], in0=local[:, :, ROW:STATE], in1=tops[:, :, :], op=ALU.subtract))
        dve.sem_inc(exp_in, 1)
        dve.wait_ge(exp_out, 2)
        for rows, h0 in ((ahead, 0), (local, HEADS)):
            factor = powers[:, :, h0:h0 + HEADS]
            feats = rows[:, :, 0:GF].rearrange("p t (h e) -> p t h e", h=HEADS)
            ch.add(V.tensor_tensor(out=feats, in0=feats, in1=factor.unsqueeze(3).to_broadcast([P, NT, HEADS, EXPERTS]), op=ALU.mult))
            ch.add(V.tensor_tensor(out=rows[:, :, GF:ROW], in0=rows[:, :, GF:ROW], in1=factor, op=ALU.mult))
        ch.wait()
        ch(V.tensor_tensor(out=pg.sums[:, :, :], in0=ahead[:, :, 0:ROW], in1=local[:, :, 0:ROW], op=ALU.add))


def gate(pg, block, st):
    nc, a = pg.nc, pg.a
    sb = lambda n, s, d=F32: st.enter_context(nc.sbuf_tensor("t_" + n, s, d))
    bias, gain, shift = (sb(n, [P, GF]) for n in ("bias", "gain", "shift"))
    den, agg, sq = sb("den", [P, NT, HEADS]), sb("agg", [P, NT, GF]), sb("sq", [P, NT, GF])
    mean, var, std = sb("mean", [P, NT]), sb("var", [P, NT]), sb("std", [P, NT])
    score, ahead, cmp = sb("score", [P, NT, EXPERTS]), sb("ahead", [P, NT, EXPERTS]), sb("cmp", [P, NT])
    most, total = sb("most", [P, NT]), sb("total", [P, NT])
    loaded, steps = pg.sem("t_loaded"), pg.sem("t_steps")
    var_ready, std_ready, exp_in, exp_out = pg.sem("t_var_ready"), pg.sem("t_std_ready"), pg.sem("t_exp_in"), pg.sem("t_exp_out")

    @block.sync
    def _(sp):
        for d, v in ((bias, "b_gat"), (gain, "ln_gamma"), (shift, "ln_beta")):
            sp.dma_start(d[:, :], row_of(a[v], GF)).then_inc(loaded, 16)
        sp.wait_ge(loaded, 48)

    @block.scalar
    def _(act):
        act.wait_ge(var_ready, 1)
        nc.scalar.activation(std[:, :], var[:, :], ACT.Sqrt).then_inc(std_ready, 1)
        act.wait_ge(exp_in, 1)
        nc.scalar.activation(score[:, :, :], score[:, :, :], ACT.Exp).then_inc(exp_out, 1)

    @block.vector
    def _(dve):
        ch = Chain(dve, steps)
        V = nc.vector
        nodes = lambda v: v[:, :].unsqueeze(1).to_broadcast([P, NT, GF])
        wide = lambda v, n: v[:, :].unsqueeze(2).to_broadcast([P, NT, n])
        dve.wait_ge(loaded, 48)
        ch(V.tensor_scalar_add(den[:, :, :], pg.sums[:, :, GF:ROW], 1e-16))
        ch(V.reciprocal(den[:, :, :], den[:, :, :]))
        ch(V.tensor_tensor(out=agg[:, :, :].rearrange("p t (h e) -> p t h e", h=HEADS),
                           in0=pg.sums[:, :, 0:GF].rearrange("p t (h e) -> p t h e", h=HEADS),
                           in1=den[:, :, :].unsqueeze(3).to_broadcast([P, NT, HEADS, EXPERTS]), op=ALU.mult))
        ch(V.tensor_tensor(out=agg[:, :, :], in0=agg[:, :, :], in1=nodes(bias), op=ALU.add))
        ch(V.tensor_reduce(out=mean[:, :], in_=agg[:, :, :], axis=AX, op=ALU.add))
        ch(V.tensor_scalar_mul(mean[:, :], mean[:, :], 1.0 / GF))
        ch(V.tensor_tensor(out=agg[:, :, :], in0=agg[:, :, :], in1=wide(mean, GF), op=ALU.subtract))
        ch(V.tensor_tensor(out=sq[:, :, :], in0=agg[:, :, :], in1=agg[:, :, :], op=ALU.mult))
        ch(V.tensor_reduce(out=var[:, :], in_=sq[:, :, :], axis=AX, op=ALU.add))
        ch(V.tensor_scalar(out=var[:, :], in0=var[:, :], scalar1=1.0 / GF, scalar2=LN_EPS, op0=ALU.mult, op1=ALU.add))
        dve.sem_inc(var_ready, 1)
        dve.wait_ge(std_ready, 1)
        ch(V.reciprocal(var[:, :], std[:, :]))
        ch(V.tensor_tensor(out=agg[:, :, :], in0=agg[:, :, :], in1=wide(var, GF), op=ALU.mult))
        ch(V.tensor_tensor(out=agg[:, :, :], in0=agg[:, :, :], in1=nodes(gain), op=ALU.mult))
        ch(V.tensor_tensor(out=agg[:, :, :], in0=agg[:, :, :], in1=nodes(shift), op=ALU.add))
        ch(V.tensor_reduce(out=score[:, :, :], in_=agg[:, :, :].rearrange("p t (h e) -> p t e h", h=HEADS), axis=AX, op=ALU.add))
        ch(V.tensor_scalar_mul(score[:, :, :], score[:, :, :], 1.0 / HEADS))
        ch(V.memset(ahead[:, :, :], 0.0))
        for e in range(EXPERTS):
            for o in range(EXPERTS):
                if o != e:
                    ch(V.tensor_tensor(out=cmp[:, :], in0=score[:, :, o], in1=score[:, :, e],
                                       op=ALU.is_ge if o < e else ALU.is_gt))
                    ch(V.tensor_tensor(out=ahead[:, :, e], in0=ahead[:, :, e], in1=cmp[:, :], op=ALU.add))
        ch(V.tensor_scalar(out=ahead[:, :, :], in0=ahead[:, :, :], scalar1=1.5, scalar2=None, op0=ALU.is_lt))
        ch(V.tensor_reduce(out=most[:, :], in_=score[:, :, :], axis=AX, op=ALU.max))
        ch(V.tensor_tensor(out=score[:, :, :], in0=score[:, :, :], in1=wide(most, EXPERTS), op=ALU.subtract))
        dve.sem_inc(exp_in, 1)
        dve.wait_ge(exp_out, 1)
        ch(V.tensor_tensor(out=score[:, :, :], in0=score[:, :, :], in1=ahead[:, :, :], op=ALU.mult))
        ch(V.tensor_reduce(out=total[:, :], in_=score[:, :, :], axis=AX, op=ALU.add))
        ch(V.reciprocal(total[:, :], total[:, :]))
        ch(V.tensor_tensor(out=pg.gate[:, :, :], in0=score[:, :, :], in1=wide(total, EXPERTS), op=ALU.mult))


def experts(pg, block, st, tensor_first, vector_first, vector_beside, vector_last, scalar_beside, scalar_last):
    nc, a = pg.nc, pg.a
    pg.y_d = pg.dram("y_d", [EXPERTS, NPAD, C]).ap()
    sb = lambda n, s, d=F32: st.enter_context(nc.sbuf_tensor("x_" + n, s, d))
    pb = lambda n, s, d=F32: st.enter_context(nc.psum_tensor("x_" + n, s, d))
    w1, w2 = sb("w1", [P, EXPERTS, KC, FF]), sb("w2", [P, EXPERTS, FC, C])
    b1, b2 = sb("b1", [P, EXPERTS, FC]), sb("b2", [P, EXPERTS, C])
    xT = sb("xT", [P, KC, SN])
    hT = [sb(f"hT{b}", [P, FC, SN]) for b in range(2)]
    y = [sb(f"y{b}", [P, ST, C]) for b in range(2)]
    hp = [pb(f"hp{i}", [P, HN]) for i in range(4)]
    yp = [pb(f"yp{i}", [P, C]) for i in range(2)]
    w_ready, xT_ready = pg.sem("x_w_ready"), pg.sem("x_xT_ready")
    hp_ready, hp_free, hT_ready, hT_used = pg.sem("x_hp_ready"), pg.sem("x_hp_free"), pg.sem("x_hT_ready"), pg.sem("x_hT_used")
    yp_ready, yp_free, y_ready = pg.sem("x_yp_ready"), pg.sem("x_yp_free"), pg.sem("x_y_ready")
    y_stored = [pg.sem(f"x_y_stored{b}") for b in range(2)]
    y_free = pg.sem("x_y_free")
    UN = FC * 2

    @block.scalar
    def _(act):
        for e in range(EXPERTS):
            act.dma_start(w1[:, e, :, :], weights_of(a["ffn_w1"][e])).then_inc(w_ready, 16)
            act.dma_start(w2[:, e, :, :], a["ffn_w2"][e].rearrange("(f p) n -> p f n", p=P)).then_inc(w_ready, 16)
            with nc.allow_non_contiguous_dma(reason="vectors of 512"):
                act.dma_start(b1[:, e, :], a["ffn_b1"][e].rearrange("(f p) -> p f", p=P)).then_inc(w_ready, 16)
            act.dma_start(b2[:, e, :], row_of(a["ffn_b2"][e], C)).then_inc(w_ready, 16)
        act.dma_start(xT[:, :, :], feat_cols(pg.x3T_d, 0)).then_inc(xT_ready, 16)
        act.sem_inc(hp_free, 4)
        act.sem_inc(y_free, 2)
        act.wait_ge(w_ready, 4 * EXPERTS * 16)

        def store(i, e):
            k = i * EXPERTS + e
            act.wait_ge(y_ready, k + 1)
            act.dma_start(node_rows(pg.y_d[e], i), y[e % 2][:, :, :]).then_inc(y_stored[e % 2], 16)

        def hidden(i, e):
            act.wait_ge(hT_used, i * EXPERTS + e + 1)
            for n in range(UN):
                f, h = n // 2, n % 2
                k = (i * EXPERTS + e) * UN + n + 1
                act.wait_ge(hp_ready, k)
                nc.scalar.activation(hT[e % 2][:, f, h * HN:(h + 1) * HN], hp[n % 4][:, :], ACT.Gelu,
                                     bias=b1[:, e, f:f + 1]).then_inc(hT_ready, 1)
                act.wait_ge(hT_ready, k)
                act.sem_inc(hp_free, 1)

        def step(i, first, last):
            for e in range(EXPERTS):
                hidden(i, e)
                scalar_beside(act, i * EXPERTS + e)
                if e == EXPERTS - 1 and not last:
                    act.dma_start(xT[:, :, :], feat_cols(pg.x3T_d, i + 1)).then_inc(xT_ready, 16)
                if e > 0 or not first:
                    p = (e - 1) % EXPERTS
                    k = i * EXPERTS + e - 1
                    act.wait_ge(y_ready, k + 1)
                    act.dma_start(node_rows(pg.y_d[p], i if e else i - 1), y[p % 2][:, :, :]).then_inc(y_stored[p % 2], 16)
                    act.wait_ge(y_stored[p % 2], ((k // 2) if first else i * (EXPERTS // 2) + (e - 1) // 2) * 16 + 16)
                    act.sem_inc(y_free, 1)

        step(0, True, False)
        with act.Fori(1, STEPS - 1) as i:
            step(i, False, False)
        step(STEPS - 1, False, True)
        store(STEPS - 1, EXPERTS - 1)
        scalar_last(act)
        act.wait_ge(y_stored[1], STEPS * EXPERTS // 2 * 16)

    @block.tensor
    def _(pe):
        pe.sem_inc(hT_used, 2)
        tensor_first(pe)
        pe.wait_ge(w_ready, 4 * EXPERTS * 16)

        def up(i, e):
            for n in range(UN):
                f, h = n // 2, n % 2
                pe.wait_ge(hp_free, (i * EXPERTS + e) * UN + n + 1)
                for c in range(KC):
                    last = nc.tensor.matmul(hp[n % 4][:, :], w1[:, e, c, f * P:(f + 1) * P],
                                            xT[:, c, h * HN:(h + 1) * HN], start=(c == 0), stop=(c == KC - 1))
                last.then_inc(hp_ready, 1)

        def down(i, e):
            k = i * EXPERTS + e
            pe.wait_ge(hT_ready, k * UN + UN)
            for j in range(ST):
                pe.wait_ge(yp_free, k * ST + j + 1)
                for f in range(FC):
                    last = nc.tensor.matmul(yp[(e * ST + j) % 2][:, :], hT[e % 2][:, f, j * P:(j + 1) * P], w2[:, e, f, :],
                                            start=(f == 0), stop=(f == FC - 1))
                last.then_inc(yp_ready, 1)
            pe.wait_ge(yp_ready, k * ST + ST)
            pe.sem_inc(hT_used, 1)

        with pe.Fori(0, STEPS) as i:
            pe.wait_ge(xT_ready, i * 16 + 16)
            for e in range(EXPERTS):
                up(i, e)
                if e > 0:
                    down(i, e - 1)
            down(i, EXPERTS - 1)

    @block.vector
    def _(dve):
        dve.sem_inc(yp_free, 2)
        vector_first(dve)
        dve.wait_ge(w_ready, 4 * EXPERTS * 16)

        def outputs(i, e):
            k = i * EXPERTS + e
            dve.wait_ge(y_free, k + 1)
            for j in range(ST):
                dve.wait_ge(yp_ready, k * ST + j + 1)
                nc.vector.tensor_tensor(out=y[e % 2][:, j, :], in0=yp[(e * ST + j) % 2][:, :], in1=b2[:, e, :],
                                        op=ALU.add).then_inc(yp_free, 1)
            dve.wait_ge(yp_free, k * ST + ST + 2)
            dve.sem_inc(y_ready, 1)

        for e in range(EXPERTS):
            vector_beside(dve, 0, e, True)
            outputs(0, e)
        with dve.Fori(1, STEPS) as i:
            for e in range(EXPERTS):
                vector_beside(dve, i, e)
                outputs(i, e)
        vector_last(dve)


SLOTS_OUT = 3


def combine(pg, block, st, out):
    nc, a = pg.nc, pg.a
    sb = lambda n, s, d=F32: st.enter_context(nc.sbuf_tensor("c_" + n, s, d))
    y = [sb(f"y{b}", [P, EXPERTS, ST, C]) for b in range(SLOTS_OUT)]
    acc = [sb(f"acc{b}", [P, ST, C]) for b in range(SLOTS_OUT)]
    y_ready = [pg.sem(f"c_y_ready{b}") for b in range(SLOTS_OUT)]
    done, added = pg.sem("c_done"), pg.sem("c_added")
    saved = [pg.sem(f"c_saved{b}") for b in range(SLOTS_OUT)]
    final = pg.sem("c_final")

    @block.sync
    def _(sp):
        for i in range(STEPS):
            if i >= SLOTS_OUT:
                sp.wait_ge(done, i - SLOTS_OUT + 1)
                sp.wait_ge(saved[i % SLOTS_OUT], (i // SLOTS_OUT) * 16)
            for e in range(EXPERTS):
                sp.dma_start(y[i % SLOTS_OUT][:, e, :, :], node_rows(pg.y_d[e], i)).then_inc(y_ready[i % SLOTS_OUT], 16)
            sp.dma_start(acc[i % SLOTS_OUT][:, :, :], node_rows(pg.x2_d, i)).then_inc(y_ready[i % SLOTS_OUT], 16)

    @block.vector
    def _(dve):
        n = 0
        for i in range(STEPS):
            dve.wait_ge(y_ready[i % SLOTS_OUT], (i // SLOTS_OUT + 1) * 16 * (EXPERTS + 1))
            for e in range(EXPERTS):
                for j in range(ST):
                    nc.vector.scalar_tensor_tensor(
                        out=acc[i % SLOTS_OUT][:, j, :], in0=y[i % SLOTS_OUT][:, e, j, :], scalar=pg.gate[:, i * ST + j, e:e + 1],
                        in1=acc[i % SLOTS_OUT][:, j, :], op0=ALU.mult, op1=ALU.add).then_inc(added, 1)
                    n += 1
                dve.wait_ge(added, n)
            dve.sem_inc(done, 1)

    @block.scalar
    def _(act):
        for i in range(STEPS):
            act.wait_ge(done, i + 1)
            full = min(ST, (N_NODES - i * SN) // P)
            act.dma_start(out[i * SN:i * SN + full * P, :].rearrange("(j p) c -> p j c", p=P),
                          acc[i % SLOTS_OUT][:, 0:full, :]).then_inc(saved[i % SLOTS_OUT], 16)
        rest = N_NODES - (NT - 1) * P
        act.dma_start(out[N_NODES - rest:N_NODES, :], acc[(STEPS - 1) % SLOTS_OUT][0:rest, ST - 1, :]).then_inc(final, 16)
        for b in range(SLOTS_OUT):
            act.wait_ge(saved[b], len(range(b, STEPS, SLOTS_OUT)) * 16)
        act.wait_ge(final, 16)


def stage_output(pg, out):
    nc = pg.nc
    with ExitStack() as st:
        with nc.Block() as block:
            join(pg, block, st)
            gate(pg, block, st)
            combine(pg, block, st, out)


def gps_layer_kernel(nc, out, **args):
    with ExitStack() as stack:
        pg = Program(nc, args, stack)
        setup(pg)
        with ExitStack() as st:
            hold = lambda n, s, d: st.enter_context(nc.sbuf_tensor(n, s, d))
            pg.src_col, pg.place_col = hold("src_col", [P, GT], I32), hold("place_col", [P, GT], I32)
            pg.place = [hold(f"place{i}", [P, GB], I32) for i in range(SLOTS)]
            pg.source = [hold(f"source{i}", [P, GB], I32) for i in range(SLOTS)]
            pg.node_id = hold("node_id", [P, NT], I32)
            with ExitStack() as sorting:
                hold_edges(pg, lambda n, s, d: sorting.enter_context(nc.sbuf_tensor(n, s, d)))
                stage_norm(pg)
                pg.end_stage()
                stage_sort(pg)
                pg.end_stage()
            pg.agg = hold("agg", [P, KC, NPAD + WIN], F32)
            stage_edges(pg)
            pg.end_stage()
            stage_mix(pg)
            pg.end_stage()
            stage_gnn(pg)
            pg.end_stage()
        stage_attend(pg)
        pg.end_stage()
        stage_output(pg, out)


def kernel(**inputs):
    import concourse.bacc as _bacc
    from concourse.bass_utils import run_bass_kernel_spmd as _run

    nc = _bacc.Bacc("TRN2", target_bir_lowering=False, num_devices=1)
    arrays, aps = {}, {}
    for name, value in layout(inputs).items():
        arrays[name] = value
        aps[name] = nc.dram_tensor(name, value.shape, mybir.dt.from_np(value.dtype), kind="ExternalInput").ap()
    out = nc.dram_tensor("out", (N_NODES, C), F32, kind="ExternalOutput").ap()
    gps_layer_kernel(nc, out, **aps)
    return _run(nc, [arrays], core_ids=[0]).results[0]["out"]


def layout(v):
    t = lambda m: np.ascontiguousarray(np.asarray(m).T)
    n = lambda m: np.ascontiguousarray(np.asarray(m))
    return {
        "x": n(v["x"]), "src": n(v["src"]), "dst": n(v["dst"]), "edge_attr": n(v["edge_attr_128"]),
        "w_edge": n(v["L0_gnn_W_edge"]), "b_edge": n(v["L0_gnn_b_edge"]),
        "gnn_w1": n(v["L0_gnn_W1"]), "gnn_b1": n(v["L0_gnn_b1"]), "gnn_w2": n(v["L0_gnn_W2"]),
        "gnn_b2": n(v["L0_gnn_b2"]), "gnn_eps": n(v["L0_gnn_eps"]).reshape(1, 1),
        "gnn_gamma": n(v["L0_gnn_gamma"]), "gnn_beta": n(v["L0_gnn_beta"]),
        "mix_wqkvT": t(v["L0_mix_Wqkv"]), "mix_g1": n(v["L0_mix_ln1_g"]), "mix_be1": n(v["L0_mix_ln1_b"]),
        "mix_w1T": t(v["L0_mix_W1"]), "mix_b1": n(v["L0_mix_b1"]), "mix_w2T": t(v["L0_mix_W2"]),
        "mix_b2": n(v["L0_mix_b2"]), "mix_g2": n(v["L0_mix_ln2_g"]), "mix_be2": n(v["L0_mix_ln2_b"]),
        "w_gat": n(v["L0_ffn_W_gat"]), "att_src": n(v["L0_ffn_att_src"]), "att_dst": n(v["L0_ffn_att_dst"]),
        "b_gat": n(v["L0_ffn_b_gat"]), "ln_gamma": n(v["L0_ffn_ln_gamma"]), "ln_beta": n(v["L0_ffn_ln_beta"]),
        "ffn_w1": n(v["L0_ffn_W1"]), "ffn_b1": n(v["L0_ffn_b1"]), "ffn_w2": n(v["L0_ffn_W2"]),
        "ffn_b2": n(v["L0_ffn_b2"]), "g_edges": n(v["L0_ffn_edge_index"]),
    }
```
